# Optimizing a Trainium2 kernel written in Bass

```python
import numpy as np
import jax
import jax.numpy as jnp

def _softmax(x, axis=-1):
    return jax.nn.softmax(x, axis=axis)

def _gelu(x):
    return jax.nn.gelu(x, approximate=True)

def _silu(x):
    return jax.nn.silu(x)

def _sigmoid(x):
    return jax.nn.sigmoid(x)

def _layernorm(x, axis=-1, eps=1e-05):
    m = jnp.mean(x, axis=axis, keepdims=True)
    v = jnp.var(x, axis=axis, keepdims=True)
    return (x - m) / jnp.sqrt(v + eps)

def _scatter_add(tgt, idx, src, axis=0):
    return tgt.at[idx].add(src)

def _segment_sum(src, seg, n):
    return jax.ops.segment_sum(src, seg, n)
kernel_name = 'mk_adaln_d2_jaxref_r8_e67abc'

def setup_inputs(seed: int=0):
    np.random.seed(seed)
    _w = jnp.asarray

    def _L0_attn_setup():
        import jax, jax.numpy as jnp
        import numpy as np
        B, L, D_MODEL, D_STATE, D_HIDDEN = (4, 512, 128, 32, 512)
        RMIN, RMAX, MAX_PHASE = (0.8, 0.95, 2.0 * np.pi)

        def _lru_scan(lam, Bu):
            lam_b = jnp.broadcast_to(lam, Bu.shape)

            def comb(a, b):
                return (a[0] * b[0], b[0] * a[1] + b[1])
            _, states = jax.lax.associative_scan(comb, (lam_b, Bu), axis=1)
            return states

        def _reference_tuple_inner(x3d, nu_log, theta_log, B_re, B_im, C_re, C_im, D_mat, W1, W2, res_logit):
            lam = jnp.exp(-jnp.exp(nu_log) + 1j * jnp.exp(theta_log))
            gamma = jnp.sqrt(1.0 - jnp.abs(lam) ** 2)
            Bn = gamma[:, None] * (B_re + 1j * B_im)
            Bu = jnp.einsum('bld,nd->bln', x3d.astype(jnp.complex64), Bn)
            states = _lru_scan(lam.astype(jnp.complex64), Bu)
            y = jnp.einsum('bln,mn->blm', states, C_re + 1j * C_im).real + jnp.einsum('bld,md->blm', x3d, D_mat)
            z = jax.nn.gelu(y @ W1) @ W2
            out = x3d + jax.nn.sigmoid(res_logit) * z
            st = states[:, -1]
            return (out, st)
        key = jax.random.key(seed)
        ks = jax.random.split(key, 10)
        u1 = jax.random.uniform(ks[0], (D_STATE,))
        u2 = jax.random.uniform(ks[1], (D_STATE,))
        nu_log = jnp.log(-0.5 * jnp.log(u1 * (RMAX ** 2 - RMIN ** 2) + RMIN ** 2))
        theta_log = jnp.log(MAX_PHASE * u2)
        B_re = jax.random.normal(ks[2], (D_STATE, D_MODEL)) / np.sqrt(2.0 * D_MODEL)
        B_im = jax.random.normal(ks[3], (D_STATE, D_MODEL)) / np.sqrt(2.0 * D_MODEL)
        C_re = jax.random.normal(ks[4], (D_MODEL, D_STATE)) / np.sqrt(D_STATE)
        C_im = jax.random.normal(ks[5], (D_MODEL, D_STATE)) / np.sqrt(D_STATE)
        D_mat = jax.random.normal(ks[6], (D_MODEL, D_MODEL)) / np.sqrt(D_MODEL)
        W1 = jax.random.normal(ks[7], (D_MODEL, D_HIDDEN)) * np.sqrt(2.0 / D_MODEL)
        W2 = jax.random.normal(ks[8], (D_HIDDEN, D_MODEL)) * np.sqrt(2.0 / D_HIDDEN)
        res_logit = jnp.asarray(-1.0, dtype=jnp.float32)
        x3d = jax.random.normal(ks[9], (B, L, D_MODEL), dtype=jnp.float32)
        return {'x3d': x3d, 'nu_log': nu_log, 'theta_log': theta_log, 'B_re': B_re, 'B_im': B_im, 'C_re': C_re, 'C_im': C_im, 'D_mat': D_mat, 'W1': W1, 'W2': W2, 'res_logit': res_logit}
    _L0_attn_in = _L0_attn_setup()

    def _L0_ffn_setup():
        import jax, jax.numpy as jnp
        import numpy as np
        B, T, C = (2, 64, 128)
        I = 512
        E = 8
        K = 2
        key = jax.random.key(seed)
        ks = jax.random.split(key, 8)
        s = 0.02
        return {'x': jax.random.normal(ks[0], (B, T, C), jnp.float32), 'Wr1': jax.random.normal(ks[1], (C, C // 4), jnp.float32) * s, 'br1': jnp.zeros((C // 4,), jnp.float32), 'Wr2': jax.random.normal(ks[2], (C // 4, E), jnp.float32) * s, 'br2': jnp.zeros((E,), jnp.float32), 'Ws1': jax.random.normal(ks[3], (C, I), jnp.float32) * s, 'bs1': jnp.zeros((I,), jnp.float32), 'Ws2': jax.random.normal(ks[4], (I, C), jnp.float32) * s, 'bs2': jnp.zeros((C,), jnp.float32), 'We1': jax.random.normal(ks[5], (E, C, I), jnp.float32) * s, 'be1': jnp.zeros((E, I), jnp.float32), 'We2': jax.random.normal(ks[6], (E, I, C), jnp.float32) * s, 'be2': jnp.zeros((E, C), jnp.float32)}
    _L0_ffn_in = _L0_ffn_setup()
    _L0_c = _w((lambda *s: np.random.randn(*s).astype(np.float32) * 0.05)(2, 128))
    _L0_wmod = _w((lambda *s: np.random.randn(*s).astype(np.float32) * 0.05)(128, 6 * 128) * 128 ** (-0.5))

    def _L1_attn_setup():
        import jax, jax.numpy as jnp
        import numpy as np
        EPS = 1e-06

        def _rmsnorm(z, w):
            zf = z.astype(jnp.float32)
            zn = zf * jax.lax.rsqrt(jnp.mean(zf * zf, axis=-1, keepdims=True) + EPS)
            return zn.astype(z.dtype) * w
        key = jax.random.key(seed)
        ks = jax.random.split(key, 6)
        B, T, D, H = (4, 512, 128, 256)
        x = jax.random.normal(ks[0], (B, T, D), dtype=jnp.float32)
        input_norm_w = jnp.ones((D,), dtype=jnp.float32)
        a_log = jax.random.normal(ks[1], (D,), dtype=jnp.float32) * 0.5
        c_out = jax.random.normal(ks[2], (D,), dtype=jnp.float32)
        d_skip = jax.random.normal(ks[3], (D,), dtype=jnp.float32)
        ff_norm_w = jnp.ones((D,), dtype=jnp.float32)
        ff_fc_w = jax.random.normal(ks[4], (H, D), dtype=jnp.float32) * 0.02
        ff_proj_w = jax.random.normal(ks[5], (D, H), dtype=jnp.float32) * 0.02
        return {'x': x, 'input_norm_w': input_norm_w, 'a_log': a_log, 'c_out': c_out, 'd_skip': d_skip, 'ff_norm_w': ff_norm_w, 'ff_fc_w': ff_fc_w, 'ff_proj_w': ff_proj_w}
    _L1_attn_in = _L1_attn_setup()

    def _L1_ffn_setup():
        import jax, jax.numpy as jnp
        import numpy as np
        NH, NKV, E, K = (16, 4, 8, 2)
        CAP_FACTOR = 1.25
        LN_EPS = 1e-05

        def _layer_norm(x, w, b):
            mu = jnp.mean(x, axis=-1, keepdims=True)
            var = jnp.mean(jnp.square(x - mu), axis=-1, keepdims=True)
            return (x - mu) * jax.lax.rsqrt(var + LN_EPS) * w + b
        key = jax.random.key(seed)
        ks = jax.random.split(key, 6)
        S, B, H, F = (256, 1, 128, 256)
        HD = H // NH
        qkv_out = NKV * (NH // NKV + 2) * HD
        f32 = jnp.float32
        return {'hidden_states': jax.random.normal(ks[0], (S, B, H), f32), 'ln1_weight': jnp.ones((H,), f32), 'ln1_bias': jnp.zeros((H,), f32), 'ln2_weight': jnp.ones((H,), f32), 'ln2_bias': jnp.zeros((H,), f32), 'qkv_weight': jax.random.normal(ks[1], (qkv_out, H), f32) * 0.02, 'proj_weight': jax.random.normal(ks[2], (H, H), f32) * 0.02, 'router_weight': jax.random.normal(ks[3], (H, E), f32) * 0.02, 'moe_w1': jax.random.normal(ks[4], (E, H, F), f32) * 0.02, 'moe_w2': jax.random.normal(ks[5], (F and E, F, H), f32)[:E] * 0.02 if False else jax.random.normal(ks[5], (E, F, H), f32) * 0.02}
    _L1_ffn_in = _L1_ffn_setup()
    _L1_c = _w((lambda *s: np.random.randn(*s).astype(np.float32) * 0.05)(2, 128))
    _L1_wmod = _w((lambda *s: np.random.randn(*s).astype(np.float32) * 0.05)(128, 6 * 128) * 128 ** (-0.5))
    _d = {'L0_attn_x3d': _L0_attn_in['x3d'], 'L0_attn_nu_log': _L0_attn_in['nu_log'], 'L0_attn_theta_log': _L0_attn_in['theta_log'], 'L0_attn_B_re': _L0_attn_in['B_re'], 'L0_attn_B_im': _L0_attn_in['B_im'], 'L0_attn_C_re': _L0_attn_in['C_re'], 'L0_attn_C_im': _L0_attn_in['C_im'], 'L0_attn_D_mat': _L0_attn_in['D_mat'], 'L0_attn_W1': _L0_attn_in['W1'], 'L0_attn_W2': _L0_attn_in['W2'], 'L0_attn_res_logit': _L0_attn_in['res_logit'], 'L0_ffn_Wr1': _L0_ffn_in['Wr1'], 'L0_ffn_br1': _L0_ffn_in['br1'], 'L0_ffn_Wr2': _L0_ffn_in['Wr2'], 'L0_ffn_br2': _L0_ffn_in['br2'], 'L0_ffn_Ws1': _L0_ffn_in['Ws1'], 'L0_ffn_bs1': _L0_ffn_in['bs1'], 'L0_ffn_Ws2': _L0_ffn_in['Ws2'], 'L0_ffn_bs2': _L0_ffn_in['bs2'], 'L0_ffn_We1': _L0_ffn_in['We1'], 'L0_ffn_be1': _L0_ffn_in['be1'], 'L0_ffn_We2': _L0_ffn_in['We2'], 'L0_ffn_be2': _L0_ffn_in['be2'], 'L0_c': _L0_c, 'L0_wmod': _L0_wmod, 'L1_attn_input_norm_w': _L1_attn_in['input_norm_w'], 'L1_attn_a_log': _L1_attn_in['a_log'], 'L1_attn_c_out': _L1_attn_in['c_out'], 'L1_attn_d_skip': _L1_attn_in['d_skip'], 'L1_attn_ff_norm_w': _L1_attn_in['ff_norm_w'], 'L1_attn_ff_fc_w': _L1_attn_in['ff_fc_w'], 'L1_attn_ff_proj_w': _L1_attn_in['ff_proj_w'], 'L1_ffn_ln1_weight': _L1_ffn_in['ln1_weight'], 'L1_ffn_ln1_bias': _L1_ffn_in['ln1_bias'], 'L1_ffn_ln2_weight': _L1_ffn_in['ln2_weight'], 'L1_ffn_ln2_bias': _L1_ffn_in['ln2_bias'], 'L1_ffn_qkv_weight': _L1_ffn_in['qkv_weight'], 'L1_ffn_proj_weight': _L1_ffn_in['proj_weight'], 'L1_ffn_router_weight': _L1_ffn_in['router_weight'], 'L1_ffn_moe_w1': _L1_ffn_in['moe_w1'], 'L1_ffn_moe_w2': _L1_ffn_in['moe_w2'], 'L1_c': _L1_c, 'L1_wmod': _L1_wmod}
    _x0 = _d['L0_attn_x3d']
    _d['L0_attn_x3d'] = jax.random.normal(jax.random.fold_in(jax.random.key(seed), 1), (2, 1024, 128), dtype=_x0.dtype)
    del _x0
    return _d

def reference(L0_attn_x3d, L0_attn_nu_log, L0_attn_theta_log, L0_attn_B_re, L0_attn_B_im, L0_attn_C_re, L0_attn_C_im, L0_attn_D_mat, L0_attn_W1, L0_attn_W2, L0_attn_res_logit, L0_ffn_Wr1, L0_ffn_br1, L0_ffn_Wr2, L0_ffn_br2, L0_ffn_Ws1, L0_ffn_bs1, L0_ffn_Ws2, L0_ffn_bs2, L0_ffn_We1, L0_ffn_be1, L0_ffn_We2, L0_ffn_be2, L0_c, L0_wmod, L1_attn_input_norm_w, L1_attn_a_log, L1_attn_c_out, L1_attn_d_skip, L1_attn_ff_norm_w, L1_attn_ff_fc_w, L1_attn_ff_proj_w, L1_ffn_ln1_weight, L1_ffn_ln1_bias, L1_ffn_ln2_weight, L1_ffn_ln2_bias, L1_ffn_qkv_weight, L1_ffn_proj_weight, L1_ffn_router_weight, L1_ffn_moe_w1, L1_ffn_moe_w2, L1_c, L1_wmod):

    def _L0_attn_ref(x3d, nu_log, theta_log, B_re, B_im, C_re, C_im, D_mat, W1, W2, res_logit):
        import jax, jax.numpy as jnp
        import numpy as np
        B, L, D_MODEL, D_STATE, D_HIDDEN = (4, 512, 128, 32, 512)
        RMIN, RMAX, MAX_PHASE = (0.8, 0.95, 2.0 * np.pi)

        def _lru_scan(lam, Bu):
            lam_b = jnp.broadcast_to(lam, Bu.shape)

            def comb(a, b):
                return (a[0] * b[0], b[0] * a[1] + b[1])
            _, states = jax.lax.associative_scan(comb, (lam_b, Bu), axis=1)
            return states

        def _reference_tuple_inner(x3d, nu_log, theta_log, B_re, B_im, C_re, C_im, D_mat, W1, W2, res_logit):
            lam = jnp.exp(-jnp.exp(nu_log) + 1j * jnp.exp(theta_log))
            gamma = jnp.sqrt(1.0 - jnp.abs(lam) ** 2)
            Bn = gamma[:, None] * (B_re + 1j * B_im)
            Bu = jnp.einsum('bld,nd->bln', x3d.astype(jnp.complex64), Bn)
            states = _lru_scan(lam.astype(jnp.complex64), Bu)
            y = jnp.einsum('bln,mn->blm', states, C_re + 1j * C_im).real + jnp.einsum('bld,md->blm', x3d, D_mat)
            z = jax.nn.gelu(y @ W1) @ W2
            out = x3d + jax.nn.sigmoid(res_logit) * z
            st = states[:, -1]
            return (out, st)
        return _reference_tuple_inner(x3d, nu_log, theta_log, B_re, B_im, C_re, C_im, D_mat, W1, W2, res_logit)[0]

    def _L0_ffn_ref(x, Wr1, br1, Wr2, br2, Ws1, bs1, Ws2, bs2, We1, be1, We2, be2):
        import jax, jax.numpy as jnp
        import numpy as np
        B, T, C = (2, 64, 128)
        I = 512
        E = 8
        K = 2
        Bb, Tt, Cc = x.shape
        xf = x.reshape(-1, Cc)
        logits = jax.nn.relu(xf @ Wr1 + br1) @ Wr2 + br2
        gates = jax.nn.softmax(logits, axis=-1)
        tg, ti = jax.lax.top_k(gates, K)
        tg = jax.nn.softmax(tg / K, axis=-1)
        out = jax.nn.silu(xf @ Ws1 + bs1) @ Ws2 + bs2
        for e in range(E):
            h = jax.nn.silu(xf @ We1[e] + be1[e]) @ We2[e] + be2[e]
            w = jnp.sum(tg * (ti == e), axis=-1)
            out = out + w[:, None] * h
        return out.reshape(Bb, Tt, Cc)

    def _L1_attn_ref(x, input_norm_w, a_log, c_out, d_skip, ff_norm_w, ff_fc_w, ff_proj_w):
        import jax, jax.numpy as jnp
        import numpy as np
        EPS = 1e-06

        def _rmsnorm(z, w):
            zf = z.astype(jnp.float32)
            zn = zf * jax.lax.rsqrt(jnp.mean(zf * zf, axis=-1, keepdims=True) + EPS)
            return zn.astype(z.dtype) * w
        normed = _rmsnorm(x, input_norm_w)
        a = jnp.exp(-jnp.exp(a_log))
        A = jnp.broadcast_to(a, normed.shape)

        def combine(e1, e2):
            a1, b1 = e1
            a2, b2 = e2
            return (a1 * a2, a2 * b1 + b2)
        _, h = jax.lax.associative_scan(combine, (A, normed), axis=1)
        scan_out = h * c_out + normed * d_skip
        x1 = x + scan_out
        n2 = _rmsnorm(x1, ff_norm_w)
        hidden = jax.nn.silu(jnp.einsum('btd,hd->bth', n2, ff_fc_w))
        ff_out = jnp.einsum('bth,dh->btd', hidden, ff_proj_w)
        return x1 + ff_out

    def _L1_ffn_ref(hidden_states, ln1_weight, ln1_bias, ln2_weight, ln2_bias, qkv_weight, proj_weight, router_weight, moe_w1, moe_w2):
        import jax, jax.numpy as jnp
        import numpy as np
        NH, NKV, E, K = (16, 4, 8, 2)
        CAP_FACTOR = 1.25
        LN_EPS = 1e-05

        def _layer_norm(x, w, b):
            mu = jnp.mean(x, axis=-1, keepdims=True)
            var = jnp.mean(jnp.square(x - mu), axis=-1, keepdims=True)
            return (x - mu) * jax.lax.rsqrt(var + LN_EPS) * w + b
        S, B, H = hidden_states.shape
        HD = H // NH
        q_per_kv = NH // NKV
        ln1 = _layer_norm(hidden_states, ln1_weight, ln1_bias)
        qkv = jnp.einsum('sbh,oh->sbo', ln1, qkv_weight)
        qkv = qkv.reshape(S, B, NKV, (q_per_kv + 2) * HD)
        q = qkv[..., :q_per_kv * HD].reshape(S, B, NH, HD)
        k = qkv[..., q_per_kv * HD:(q_per_kv + 1) * HD]
        v = qkv[..., (q_per_kv + 1) * HD:]
        qb = jnp.transpose(q, (1, 2, 0, 3)).reshape(B, NKV, q_per_kv, S, HD)
        kb = jnp.transpose(k, (1, 2, 0, 3))
        vb = jnp.transpose(v, (1, 2, 0, 3))
        scale = 1.0 / np.sqrt(HD).astype(np.float32)
        scores = jnp.einsum('bgqsd,bgtd->bgqst', qb, kb) * scale
        causal = jnp.tril(jnp.ones((S, S), bool))
        scores = jnp.where(causal, scores, jnp.finfo(scores.dtype).min)
        attn = jax.nn.softmax(scores, axis=-1)
        ao = jnp.einsum('bgqst,bgtd->bgqsd', attn, vb)
        ao = ao.reshape(B, NH, S, HD)
        ao = jnp.transpose(ao, (2, 0, 1, 3)).reshape(S, B, H)
        proj = jnp.einsum('sbh,oh->sbo', ao, proj_weight)
        h1 = hidden_states + proj
        ln2 = _layer_norm(h1, ln2_weight, ln2_bias)
        x = ln2.reshape(-1, H)
        N = x.shape[0]
        logits = x @ router_weight
        probs = jax.nn.softmax(logits, axis=-1)
        top_p, top_i = jax.lax.top_k(probs, K)
        top_p = top_p / jnp.sum(top_p, axis=-1, keepdims=True)
        exp_idx = top_i.reshape(-1)
        exp_p = top_p.reshape(-1)
        order = jnp.argsort(exp_idx, stable=True)
        sorted_exp = exp_idx[order]
        counts = jnp.bincount(exp_idx, length=E)
        offsets = jnp.concatenate([jnp.zeros((1,), counts.dtype), jnp.cumsum(counts)[:-1]])
        within = jnp.arange(N * K) - offsets[sorted_exp]
        cap = int(np.ceil(N * K / E * CAP_FACTOR))
        T = E * cap
        valid = within < cap
        dst = jnp.where(valid, sorted_exp * cap + within, T)
        padded_tokens = jnp.zeros((T, H), x.dtype).at[dst].set(x[order // K], mode='drop')
        padded_probs = jnp.zeros((T,), exp_p.dtype).at[dst].set(exp_p[order], mode='drop')
        padded_tid = jnp.zeros((T,), jnp.int32).at[dst].set((order // K).astype(jnp.int32), mode='drop')
        xt = padded_tokens.reshape(E, cap, H)
        fc1 = jax.nn.gelu(jnp.einsum('ech,ehf->ecf', xt, moe_w1))
        fc2 = jnp.einsum('ecf,efh->ech', fc1, moe_w2).reshape(T, H)
        weighted = fc2 * padded_probs[:, None]
        moe_out = jnp.zeros((N, H), hidden_states.dtype).at[padded_tid].add(weighted)
        return h1 + moe_out.reshape(S, B, H)
    x = L0_attn_x3d
    mod = (_silu(L0_c) @ L0_wmod).reshape(L0_c.shape[0], 6, 1, -1)
    sa, ca, ga, sb, cb, gb = (mod[:, 0], mod[:, 1], mod[:, 2], mod[:, 3], mod[:, 4], mod[:, 5])
    ga = (2 * (ga >= 0) - 1) * jnp.maximum(jnp.abs(ga), 0.25)
    gb = (2 * (gb >= 0) - 1) * jnp.maximum(jnp.abs(gb), 0.25)
    h = _layernorm(x, axis=-1) * (1 + ca) + sa
    x = x + ga * _L0_attn_ref(h, L0_attn_nu_log, L0_attn_theta_log, L0_attn_B_re, L0_attn_B_im, L0_attn_C_re, L0_attn_C_im, L0_attn_D_mat, L0_attn_W1, L0_attn_W2, L0_attn_res_logit)
    h = _layernorm(x, axis=-1) * (1 + cb) + sb
    x = x + gb * _L0_ffn_ref(h, L0_ffn_Wr1, L0_ffn_br1, L0_ffn_Wr2, L0_ffn_br2, L0_ffn_Ws1, L0_ffn_bs1, L0_ffn_Ws2, L0_ffn_bs2, L0_ffn_We1, L0_ffn_be1, L0_ffn_We2, L0_ffn_be2)
    mod = (_silu(L1_c) @ L1_wmod).reshape(L1_c.shape[0], 6, 1, -1)
    sa, ca, ga, sb, cb, gb = (mod[:, 0], mod[:, 1], mod[:, 2], mod[:, 3], mod[:, 4], mod[:, 5])
    ga = (2 * (ga >= 0) - 1) * jnp.maximum(jnp.abs(ga), 0.25)
    gb = (2 * (gb >= 0) - 1) * jnp.maximum(jnp.abs(gb), 0.25)
    h = _layernorm(x, axis=-1) * (1 + ca) + sa
    x = x + ga * _L1_attn_ref(h, L1_attn_input_norm_w, L1_attn_a_log, L1_attn_c_out, L1_attn_d_skip, L1_attn_ff_norm_w, L1_attn_ff_fc_w, L1_attn_ff_proj_w)
    h = _layernorm(x, axis=-1) * (1 + cb) + sb
    x = x + gb * _L1_ffn_ref(h, L1_ffn_ln1_weight, L1_ffn_ln1_bias, L1_ffn_ln2_weight, L1_ffn_ln2_bias, L1_ffn_qkv_weight, L1_ffn_proj_weight, L1_ffn_router_weight, L1_ffn_moe_w1, L1_ffn_moe_w2)
    return x

_drawn_inputs = setup_inputs


def setup_inputs(seed=0):
    import zlib

    import numpy as np

    out = dict(_drawn_inputs(seed))
    spreads = {'L0_ffn_br1': (0.0, 0.8),
     'L0_ffn_br2': (0.0, 0.319),
     'L0_ffn_bs1': (0.0, 0.8),
     'L0_ffn_bs2': (0.0, 0.32),
     'L0_ffn_be1': (0.0, 0.8),
     'L0_ffn_be2': (0.0, 0.428),
     'L1_attn_input_norm_w': (1.0, 0.2),
     'L1_attn_ff_norm_w': (1.0, 0.6),
     'L1_ffn_ln1_weight': (1.0, 0.6),
     'L1_ffn_ln1_bias': (0.0, 0.8),
     'L1_ffn_ln2_weight': (1.0, 0.6),
     'L1_ffn_ln2_bias': (0.0, 0.8)}
    factors = {'L0_attn_nu_log': 2.959,
     'L0_ffn_Wr1': 7.116,
     'L0_ffn_Wr2': 4.191,
     'L0_ffn_Ws1': 4.491,
     'L0_ffn_Ws2': 4.045,
     'L0_ffn_We1': 6.366,
     'L0_ffn_We2': 5.787,
     'L1_attn_ff_fc_w': 6.547,
     'L1_attn_ff_proj_w': 6.377,
     'L1_ffn_qkv_weight': 5.45,
     'L1_ffn_proj_weight': 5.475,
     'L1_ffn_router_weight': 8.0,
     'L1_ffn_moe_w1': 8.0,
     'L1_ffn_moe_w2': 8.0}
    for name, (base, spread) in spreads.items():
        noise = np.random.default_rng([zlib.crc32(name.encode()), seed]).standard_normal(out[name].shape)
        drawn = base * np.exp(spread * noise) if base else spread * noise
        out[name] = jnp.asarray(drawn.astype(out[name].dtype))
    for name, factor in factors.items():
        out[name] = (out[name] * factor).astype(out[name].dtype)
    return out
```

```python
from contextlib import ExitStack

import numpy as np

import concourse.bass as bass
from concourse import mybir

F32 = mybir.dt.float32
F32R = mybir.dt.float32r
I32 = mybir.dt.int32
U32 = mybir.dt.uint32
ALU = mybir.AluOpType
ACT = mybir.ActivationFunctionType
AX = mybir.AxisListType

P = 128
CH = 512
TPC = CH // P


def two_part(value, bits=12):
    high = np.float32(value)
    high = (high.view(np.uint32) & np.uint32(0xFFFFFFFF << (24 - bits) & 0xFFFFFFFF)).view(np.float32)
    return float(high), float(value - float(high))


def adaln_two_layers(nc, A, out):
    B, L, D = A["L0_attn_x3d"].shape
    NS = A["L0_attn_B_re"].shape[0]
    HID = A["L0_attn_W1"].shape[1]
    NJ0 = HID // P
    NE = A["L0_ffn_We1"].shape[0]
    NR = A["L0_ffn_Wr1"].shape[1]
    NJ1 = A["L1_ffn_moe_w1"].shape[2] // P
    NF = A["L1_attn_ff_fc_w"].shape[0] // P
    QKV = A["L1_ffn_qkv_weight"].shape[0]
    T = B * L
    NT = T // P
    NC = T // CH
    CPB = NC // B
    NKV, NH = 4, 16
    HD = D // NH
    QPK = NH // NKV
    GW = (QPK + 2) * HD
    CAP = float(-(-T * 2 * 5 // (NE * 4)))
    assert D == P and 4 * NS == P and NE == 8 and CPB == 2 and B == 2 and NJ0 == 4 and NJ1 == 2 and NF == 2

    x_rows = A["L0_attn_x3d"].rearrange("b (t p) d -> p (b t) d", p=P)
    out_rows = out.rearrange("b (t p) d -> p (b t) d", p=P)

    def column(name):
        return A[name].rearrange("(p a) -> p a", a=1)

    with ExitStack() as ctx:
        def sb(name, shape, dt=F32):
            return ctx.enter_context(nc.sbuf_tensor(name, shape, dt))

        def sems(names):
            return [ctx.enter_context(nc.semaphore(n)) for n in names.split()]

        X = sb("X", [P, NT, D])
        XN = sb("XN", [P, NT, D])
        H = sb("H", [P, T])
        Hh = sb("Hh", [P, T], F32R)
        Hl = sb("Hl", [P, T], F32R)
        HT = sb("HT", [P, NT, D])
        ACC = sb("ACC", [P, T])
        WRAW = [[sb(f"wraw{n}_{s}", [P, HID]) for s in range(2)] for n in (1, 2)]
        W1h = [sb(f"w1h_{s}", [P, NJ0, P], F32R) for s in range(2)]
        W1l = [sb(f"w1l_{s}", [P, NJ0, P], F32R) for s in range(2)]
        W2h = [sb(f"w2h_{s}", [P, NJ0, P], F32R) for s in range(2)]
        W2l = [sb(f"w2l_{s}", [P, NJ0, P], F32R) for s in range(2)]
        AH = [sb(f"ah_{s}", [P, NJ0, CH], F32R) for s in range(2)]
        AL = [sb(f"al_{s}", [P, NJ0, CH], F32R) for s in range(2)]
        R = sb("R", [P, 10752])
        GT = sb("GT", [P, T])
        MODR = sb("MODR", [P, B, 6, D])

        def cut(at, n):
            return R[:, at:at + n]

        TIN, TC, TS = cut(0, L), cut(1024, L + 1), cut(2304, L + 1)
        Q, WC, WS = cut(3584, CH), cut(4096, CH), cut(4608, CH)
        Y = [cut(5120, CH), cut(9728, CH)]
        U = [cut(5632, CH), cut(6144, CH)]
        G0 = cut(6656, NJ0 * CH).rearrange("p (j n) -> p j n", j=NJ0)
        T1 = cut(8704, CH)
        T2 = [cut(9216, CH), cut(10240, CH)]
        DTMP = cut(9728, CH)
        A32 = cut(0, NJ0 * CH).rearrange("p (j n) -> p j n", j=NJ0)
        WB = [cut(2048, CH), cut(2560, CH)]
        MG = [cut(3072, CH), cut(3584, CH)]
        GR = cut(4096, 2 * T).rearrange("p (g n) -> p g n", g=2)
        TE = [cut(8192, CH), cut(8704, CH)]
        NTK = cut(0, NC * CH).rearrange("p (t n) -> p t n", n=D)
        NFM = cut(2048, CH)
        HS = [cut(2560, CH), cut(3072, CH)]
        SK = cut(3584, CH)
        X1 = cut(4096, T)
        N2 = cut(6144, CH)
        G1 = cut(6656, NF * CH).rearrange("p (j n) -> p j n", j=NF)
        U1, U2 = cut(7680, CH), cut(8192, CH)
        QV = cut(0, NT * QKV).rearrange("p (t n) -> p t n", n=QKV)
        AO = cut(3072, T).rearrange("p (t n) -> p t n", n=D)
        PR = cut(5120, L)
        PR2 = cut(6144, L)
        AOT = [cut(7168, CH), cut(7680, CH)]

        LW1 = sb("LW1", [P, HID])
        LW2 = sb("LW2", [P, NJ0, D])
        TR = sb("TR", [P, 11, P])
        TW = sb("TW", [P, 11, P])
        WMOD = [sb(f"wmod{n}", [P, 6 * D]) for n in range(2)]
        CT = sb("CT", [P, 2, B])
        SC = sb("SC", [P, 2, B])
        SCB = sb("SCB", [P, B, P])
        MF = sb("MF", [P, 2, 6, B])
        ID = sb("ID", [P, P])
        UT = sb("UT", [P, P])
        ON = sb("ON", [P, P])
        WR1 = sb("WR1", [P, NR])
        WR2 = sb("WR2", [NR + 1, NE])
        RT = sb("RT", [P, NE])
        BR1 = sb("BR1", [NR, 1])
        B1 = sb("B1", [P, 1 + NE, NJ0])
        B1S = [sb(f"b1s_{n}", [P, NJ0]) for n in range(2)]
        BE2 = sb("BE2", [NE, D])
        COL = sb("COL", [P, 12])
        EX = sb("EX", [P, 3])
        SM = sb("SM", [P, 24])
        SI = sb("SI", [P, 4], I32)
        ST = sb("ST", [P, NT, 6])
        MV = sb("MV", [P, NT, 2])
        VE = sb("VE", [P, NT])
        RS = sb("RS", [P, NT])
        MH = sb("MH", [P, NT])
        EQ1 = sb("EQ1", [P, NT, NE])
        EQ2 = sb("EQ2", [P, NT, NE])
        GA = sb("GA", [P, NT, NE])
        PG = sb("PG", [P, NT, NE])
        M8 = sb("M8", [P, NT, NE])
        I8 = sb("I8", [P, NT, NE], U32)
        IF = sb("IF", [P, NT, 2])
        IO = sb("IO", [P, NT, NE])
        RV = sb("RV", [P, 6, NT])
        SP2 = sb("SP2", [P, 2 * 6, TPC * NH])
        CS = sb("CS", [P, NE, NT])
        D0 = sb("D0", [P, NE, NT])
        CSO = sb("CSO", [P, NE, NT])
        DEC = sb("DEC", [P, 3])
        EK = sb("EK", [P, 3])
        EF = sb("EF", [P, 3])
        EQ = sb("EQ", [P, 3])
        EI = sb("EI", [P, 3], I32)
        SG = sb("SG", [P, 3])
        GTMP = sb("GTMP", [P, 2, 2, B])

        PS = ctx.enter_context(nc.psum_tensor("PS", [P, 8, CH], F32))

        PAR, SIG, R1, RTH, RA = SM, 21, 0, 1, 2
        NU, TH, AL_, CO, DS, FNW, INW, L1W, L1B, L2W, L2B, BS2 = range(12)
        T_BW, T_M1, T_M2, T_D, T_F0, T_F1, T_P0, T_P1, T_Q0, T_Q1, T_PJ = range(11)

        (x_in, col_in, tr_in, mod_in, lru_in, small_in, raw_in0, raw_in1, gr_in, gr1_in, out_in) = sems(
            "x_in col_in tr_in mod_in lru_in small_in raw_in0 raw_in1 gr_in gr1_in out_in")
        raw_in = [raw_in0, raw_in1]
        (const, dch, pch, ach, sc_done, modps, mod_done, modr_done, scb_done, gam_in, gam, trig_in, trig, turned, tw_done) = sems(
            "const dch pch ach sc_done modps mod_done modr_done scb_done gam_in gam trig_in trig turned tw_done")
        (a_ve, a_rs, a_xn, a_tp, a_h, a_bu, a_u, a_wc, a_ws, a_y, a_yc, a_hid, a_gel, a_z, a_t, a_bk, a_x) = sems(
            "a_ve a_rs a_xn a_tp a_h a_bu a_u a_wc a_ws a_y a_yc a_hid a_gel a_z a_t a_bk a_x")
        (b_ve, b_rs, b_xn, b_tp, b_h, b_hh, b_hl, b_r1, b_rl, b_lg, b_d, b_e, b_g, b_gt, b_gtc) = sems(
            "b_ve b_rs b_xn b_tp b_h b_hh b_hl b_r1 b_rl b_lg b_d b_e b_g b_gt b_gtc")
        (w_split, m_hid, m_act, m_hi, m_hi_act, m_lo, m_out, m_gated, m_wb, m_acc) = sems(
            "w_split m_hid m_act m_hi m_hi_act m_lo m_out m_gated m_wb m_acc")
        (c_be, c_t, c_bk, c_x) = sems("c_be c_t c_bk c_x")
        (d_ve, d_rs, d_xn, d_ht, d_ve2, d_rs2, d_nt, d_tp, d_nf, d_hs, d_x1, d_tp2, d_x1t, d_ve3, d_rs3, d_n2t, d_tp3, d_n2, d_fc,
         d_g, d_pj, d_u, d_bk, d_x) = sems(
            "d_ve d_rs d_xn d_ht d_ve2 d_rs2 d_nt d_tp d_nf d_hs d_x1 d_tp2 d_x1t d_ve3 d_rs3 d_n2t d_tp3 d_n2 d_fc d_g d_pj "
            "d_u d_bk d_x")
        (e_ve, e_rs, e_xn, e_mod, e_ve2, e_rs2, e_n1, e_tp, e_l1, e_qk, e_qv, e_dd, e_e, e_ao, e_at, e_aot, e_pj, e_h1, e_ve3,
         e_rs3, e_n2, e_tp2, e_l2, e_hh, e_hl, e_lg, e_d, e_ee, e_cs, e_cn, e_g, e_gt, e_gtc, e_bk, e_o) = sems(
            "e_ve e_rs e_xn e_mod e_ve2 e_rs2 e_n1 e_tp e_l1 e_qk e_qv e_dd e_e e_ao e_at e_aot e_pj e_h1 e_ve3 "
            "e_rs3 e_n2 e_tp2 e_l2 e_hh e_hl e_lg e_d e_ee e_cs e_cn e_g e_gt e_gtc e_bk e_o")

        BK = dict(a_tp=0, a_bu=1, a_y=2, a_hid=3, a_z=5, a_bk=6, b_tp=0, b_r1=1, b_lg=7, gt=6, c_be=6, c_bk=7,
                  d_tp=0, d_tpn=1, d_tp2=2, d_tp3=3, d_fc=4, d_pj=6, d_bk=7, e_tp=0, e_qk=1, e_at=3, e_pj=4, e_tp2=5, e_lg=6)

        SA, CA, GAT, SBT, CB, GB = range(6)

        def tiles(c):
            return range(TPC * c, TPC * (c + 1))

        def tk(c):
            return slice(CH * c, CH * (c + 1))

        A_ORDER = ("a_ve a_rs a_xn a_tp a_h a_bu a_u a_ws a_y a_yc a_hid a_gel a_t a_bk a_x "
                   "b_ve b_rs b_xn b_tp b_h b_hl b_r1 b_rl b_lg").split()
        B_ORDER = ("c_be c_t c_bk c_x "
                   "d_ve d_rs d_xn d_ht d_ve2 d_rs2 d_nt d_tp d_nf d_x1 d_tp2 d_x1t d_ve3 d_rs3 d_n2t d_tp3 d_n2 d_fc d_g d_pj d_u d_bk d_x "
                   "e_ve e_rs e_xn e_mod e_ve2 e_rs2 e_n1 e_tp e_l1 e_qk e_qv e_dd e_e e_ao e_at e_aot e_pj e_h1 e_rs3 e_n2 e_tp2 "
                   "e_l2 e_hl e_lg").split()

        def wave(order, **mine):
            assert set(mine) <= set(order)
            for w in range(len(order) + NC - 1):
                for c in range(NC):
                    if 0 <= w - c < len(order) and order[w - c] in mine:
                        mine[order[w - c]](c)

        block = ctx.enter_context(nc.Block())

        @block.sync
        def _(sp):
            def load(dst, src, sem):
                sp.dma_start(dst, src).then_inc(sem, 16)

            with nc.allow_non_contiguous_dma(reason="small parameters"):
                for c in range(NC):
                    load(X[:, TPC * c:TPC * (c + 1), :], x_rows[:, TPC * c:TPC * (c + 1), :], x_in)
                    if c == 0:
                        for g in range(4):
                            load(COL[NS * g:NS * (g + 1), NU:NU + 1], column("L0_attn_nu_log"), col_in)
                            load(COL[NS * g:NS * (g + 1), TH:TH + 1], column("L0_attn_theta_log"), col_in)
                        load(COL[:, AL_:AL_ + 1], column("L1_attn_a_log"), col_in)
                        for n in range(2):
                            load(CT[:, n, :], A[f"L{n}_c"].rearrange("b d -> d b"), mod_in)
                            load(WMOD[n][:, :], A[f"L{n}_wmod"], mod_in)
                for g, n in enumerate(["L0_attn_B_re", "L0_attn_B_im", "L0_attn_B_im", "L0_attn_B_re"]):
                    load(TR[NS * g:NS * (g + 1), 0, :], A[n], tr_in)
                for g, (n, m) in enumerate([("L0_attn_C_re", "L0_attn_C_im"), ("L0_attn_C_im", "L0_attn_C_re")] * 2):
                    load(TR[:, 1, NS * g:NS * (g + 1)], A[n], tr_in)
                    load(TR[:, 2, NS * g:NS * (g + 1)], A[m], tr_in)
                load(TR[:, 3, :], A["L0_attn_D_mat"], tr_in)
                load(LW1[:, :], A["L0_attn_W1"], lru_in)
                load(LW2[:, :, :], A["L0_attn_W2"].rearrange("(j p) n -> p j n", p=P), lru_in)
                load(TR[:, 4:6, :], A["L1_attn_ff_fc_w"].rearrange("(j p) n -> p j n", p=P), tr_in)
                load(TR[:, 6:8, :], A["L1_attn_ff_proj_w"].rearrange("o (j n) -> o j n", j=NF), tr_in)
                load(TR[:, 8, :], A["L1_ffn_qkv_weight"][0:P, :], tr_in)
                load(TR[0:QKV - P, 9, :], A["L1_ffn_qkv_weight"][P:QKV, :], tr_in)
                load(TR[:, 10, :], A["L1_ffn_proj_weight"], tr_in)
                load(SM[:, 20:21], A["L0_attn_res_logit"].to_broadcast([P, 1]), small_in)
                for k, n in ((CO, "L1_attn_c_out"), (DS, "L1_attn_d_skip"), (FNW, "L1_attn_ff_norm_w"),
                             (INW, "L1_attn_input_norm_w"), (L1W, "L1_ffn_ln1_weight"), (L1B, "L1_ffn_ln1_bias"),
                             (L2W, "L1_ffn_ln2_weight"), (L2B, "L1_ffn_ln2_bias"), (BS2, "L0_ffn_bs2")):
                    load(COL[:, k:k + 1], column(n), small_in)
                load(WR1[:, :], A["L0_ffn_Wr1"], small_in)
                load(WR2[0:NR, :], A["L0_ffn_Wr2"], small_in)
                load(WR2[NR:NR + 1, :], A["L0_ffn_br2"].rearrange("(a n) -> a n", a=1), small_in)
                load(BR1[:, :], column("L0_ffn_br1"), small_in)
                load(B1[:, 0, :], A["L0_ffn_bs1"].rearrange("(p j) -> p j", j=NJ0), small_in)
                load(B1[:, 1:1 + NE, :], A["L0_ffn_be1"].rearrange("e (p j) -> p e j", j=NJ0), small_in)
                load(BE2[:, :], A["L0_ffn_be2"], small_in)
                load(RT[:, :], A["L1_ffn_router_weight"], small_in)

            def raw(q):
                s = q % 2
                if q >= 2:
                    sp.wait_ge(w_split, q - 1)
                w1 = A["L0_ffn_Ws1"] if q == 0 else A["L0_ffn_We1"][q - 1] if q <= NE else A["L1_ffn_moe_w1"][q - 1 - NE]
                w2 = A["L0_ffn_Ws2"] if q == 0 else A["L0_ffn_We2"][q - 1] if q <= NE else A["L1_ffn_moe_w2"][q - 1 - NE]
                nj = NJ0 if q <= NE else NJ1
                load(WRAW[0][s][:, 0:nj * P], w1, raw_in[s])
                load(WRAW[1][s][:, 0:nj * P], w2.rearrange("(p j) n -> p (j n)", j=nj), raw_in[s])

            for q in range(1 + NE):
                raw(q)
                if q == 2:
                    sp.wait_ge(b_gtc, NC)
                    for e in range(NE):
                        load(GR[32 * (e % 4):32 * (e % 4) + 1, e // 4, :], GT[e:e + 1, :], gr_in)
            for q in range(1 + NE, 1 + 2 * NE):
                raw(q)
                if q == 2 + NE:
                    sp.wait_ge(e_gtc, NC)
                    for e in range(NE):
                        load(GR[32 * (e % 4):32 * (e % 4) + 1, e // 4, :], GT[e:e + 1, :], gr1_in)
            for c in range(NC):
                sp.wait_ge(e_o, c + 1)
                sp.dma_start(out_rows[:, TPC * c:TPC * (c + 1), :], X[:, TPC * c:TPC * (c + 1), :]).then_inc(out_in, 16)
            sp.wait_ge(out_in, 16 * NC)

        @block.gpsimd
        def _(pool):
            linked = [0]

            def link(ins):
                linked[0] += 1
                ins.then_inc(pch, 1)
                pool.wait_ge(pch, linked[0])

            nc.gpsimd.memset(MH[:, :], -0.5)
            nc.gpsimd.memset(ID[:, :], 0.0)
            nc.gpsimd.memset(D0[:, :, :], 1.0)
            link(nc.gpsimd.memset(ON[:, :], 1.0))
            nc.gpsimd.affine_select(out=ID[:, :], in_=ID[:, :], compare_op=ALU.not_equal, fill=1.0, base=0,
                                    pattern=[[-1, P]], channel_multiplier=1).then_inc(const, 1)
            nc.gpsimd.affine_select(out=UT[:, :], in_=ON[:, :], compare_op=ALU.is_gt, fill=0.0, base=0,
                                    pattern=[[1, P]], channel_multiplier=-1).then_inc(const, 1)
            nc.gpsimd.memset(D0[:, :, 0:1], 0.0).then_inc(const, 1)
            nc.gpsimd.iota(IO[:, :, :], [[0, NT], [1, NE]], base=0, channel_multiplier=0,
                           allow_small_or_imprecise_dtypes=True).then_inc(const, 1)

            pool.wait_ge(gam_in, 1)
            nc.gpsimd.tensor_tensor(SM[:, 19:20], SM[:, 18:19], SM[:, 22:23], ALU.pow).then_inc(gam, 1)

            def root(ve, rs, c):
                pool.wait_ge(ve, c + 1)
                nc.gpsimd.tensor_tensor(RS[:, tiles(c)[0]:tiles(c)[-1] + 1], VE[:, tiles(c)[0]:tiles(c)[-1] + 1],
                                        MH[:, tiles(c)[0]:tiles(c)[-1] + 1], ALU.pow).then_inc(rs, 1)

            def a_out_sin(c):
                pool.wait_ge(a_u, c + 1)
                if c >= 1:
                    pool.wait_ge(a_y, c)
                nc.gpsimd.tensor_tensor(WS, TS[:, (c % CPB) * CH:(c % CPB + 1) * CH], U[c % 2], ALU.mult).then_inc(a_ws, 1)

            wave(A_ORDER, a_rs=lambda c: root(a_ve, a_rs, c), a_ws=a_out_sin, b_rs=lambda c: root(b_ve, b_rs, c))

            splits = [0]

            def split(q, nj):
                splits[0] += 1
                s = q % 2
                pool.wait_ge(raw_in[s], 32 * (q // 2 + 1))
                if q >= 2:
                    pool.wait_ge(m_out, 4 * (q - 1))
                r1 = WRAW[0][s][:, 0:nj * P].rearrange("p (m j) -> p j m", j=nj)
                r2 = WRAW[1][s][:, 0:nj * P].rearrange("p (j m) -> p j m", j=nj)
                if q <= NE:
                    nc.gpsimd.tensor_copy(B1S[s][:, :], B1[:, q, :])
                nc.gpsimd.tensor_copy(W1h[s][:, 0:nj, :], r1)
                link(nc.gpsimd.tensor_copy(W2h[s][:, 0:nj, :], r2))
                nc.gpsimd.tensor_tensor(W1l[s][:, 0:nj, :], r1, W1h[s][:, 0:nj, :].bitcast(F32), ALU.subtract)
                nc.gpsimd.tensor_tensor(W2l[s][:, 0:nj, :], r2, W2h[s][:, 0:nj, :].bitcast(F32),
                                        ALU.subtract).then_inc(w_split, 1)

            def spread(k, e, c, rows_in):
                if k >= 2:
                    pool.wait_ge(m_gated, k - 1)
                if e < 0:
                    nc.gpsimd.memset(WB[k % 2], 1.0).then_inc(m_wb, 1)
                else:
                    pool.wait_ge(rows_in, 16 * NE)
                    pool.wait_ge(m_acc, k - 1)
                    pool.wait_ge(w_split, splits[0])
                    nc.gpsimd.partition_broadcast(WB[k % 2], GR[32 * (e % 4):32 * (e % 4) + 1, e // 4, tk(c)]).then_inc(m_wb, 1)
                    pool.wait_ge(m_wb, k + 1)

            def accumulate(k, c):
                pool.wait_ge(m_gated, k + 1)
                pool.wait_ge(m_acc, k)
                nc.gpsimd.tensor_tensor(ACC[:, tk(c)], ACC[:, tk(c)], MG[k % 2], ALU.add).then_inc(m_acc, 1)

            pool.wait_ge(a_x, NC)
            pool.wait_ge(small_in, 16 * 18)
            link(nc.gpsimd.memset(ACC[:, :], 0.0))
            split(0, NJ0)
            split(1, NJ0)
            for k in range(NC * (1 + NE)):
                e, c = k // NC - 1, k % NC
                spread(k, e, c, gr_in)
                if k >= 1:
                    accumulate(k - 1, (k - 1) % NC)
                if c == 1 and 2 <= e + 2 <= NE:
                    split(e + 2, NJ0)
            accumulate(NC * (1 + NE) - 1, NC - 1)
            split(1 + NE, NJ1)
            split(2 + NE, NJ1)

            def modulate(xn, mod, c, shift, scale):
                pool.wait_ge(xn, c + 1)
                b = c // CPB
                t = slice(TPC * c, TPC * (c + 1))
                if c == 0:
                    pool.wait_ge(modr_done, 1)
                nc.gpsimd.tensor_tensor(HT[:, t, :], XN[:, t, :], MODR[:, b, scale:scale + 1, :].to_broadcast([P, TPC, D]), ALU.mult)\
                    .then_inc(pch, 1)
                linked[0] += 1
                pool.wait_ge(pch, linked[0])
                nc.gpsimd.tensor_tensor(HT[:, t, :], HT[:, t, :], MODR[:, b, shift:shift + 1, :].to_broadcast([P, TPC, D]), ALU.add)\
                    .then_inc(mod, 1)

            wave(B_ORDER, d_rs=lambda c: root(d_ve, d_rs, c), d_ht=lambda c: modulate(d_xn, d_ht, c, SA, CA),
                 d_rs2=lambda c: root(d_ve2, d_rs2, c), d_rs3=lambda c: root(d_ve3, d_rs3, c),
                 e_rs=lambda c: root(e_ve, e_rs, c), e_mod=lambda c: modulate(e_xn, e_mod, c, SBT, CB),
                 e_rs2=lambda c: root(e_ve2, e_rs2, c), e_rs3=lambda c: root(e_ve3, e_rs3, c))

            base = NC * (1 + NE)
            pool.wait_ge(e_h1, NC)
            link(nc.gpsimd.memset(ACC[:, :], 0.0))
            for k in range(NC * NE):
                e, c = k // NC, k % NC
                spread(base + k, e, c, gr1_in)
                if k >= 1:
                    accumulate(base + k - 1, (k - 1) % NC)
                if c == 1 and 1 <= e < NE - 1:
                    split(1 + NE + e + 1, NJ1)
            accumulate(base + NC * NE - 1, NC - 1)

        @block.scalar
        def _(act):
            act.wait_ge(mod_in, 64)
            nc.scalar.activation(SC[:, :, :], CT[:, :, :], ACT.Silu).then_inc(sc_done, 1)
            act.wait_ge(trig_in, 1)
            nc.scalar.activation(SM[:, 10:12], SM[:, 8:10], ACT.Sin).then_inc(trig, 1)
            act.wait_ge(small_in, 16 * 18)
            nc.scalar.activation(SM[:, SIG:SIG + 1], SM[:, 20:21], ACT.Sigmoid).then_inc(trig, 1)

            def evacuate(tp, out_sem, c, dst, bank, scale, bias=0.0):
                act.wait_ge(tp, c + 1)
                nc.scalar.activation(dst, PS[:, bank, :], ACT.Identity, scale=scale, bias=bias).then_inc(out_sem, 1)

            def st_a_h(c):
                if c == 0:
                    act.wait_ge(mod_done, 1)
                b = c // CPB
                evacuate(a_tp, a_h, c, H[:, tk(c)], BK["a_tp"], MF[:, 0, CA, b:b + 1], MF[:, 0, SA, b:b + 1])

            def st_a_yc(c):
                act.wait_ge(a_y, c + 1)
                if c >= 2:
                    act.wait_ge(a_hid, NJ0 * (c - 1))
                nc.scalar.activation(Y[c % 2], PS[:, BK["a_y"], :], ACT.Copy).then_inc(a_yc, 1)

            def st_a_gel(c):
                if c >= 1:
                    act.wait_ge(a_z, c)
                for j in range(NJ0):
                    n = NJ0 * c + j
                    act.wait_ge(a_hid, n + 1)
                    nc.scalar.activation(G0[:, j, :], PS[:, BK["a_hid"] + n % 2, :], ACT.Gelu_apprx_tanh).then_inc(a_gel, 1)

            def st_b_h(c):
                b = c // CPB
                evacuate(b_tp, b_h, c, H[:, tk(c)], BK["b_tp"], MF[:, 0, CB, b:b + 1], MF[:, 0, SBT, b:b + 1])
                nc.scalar.activation(Hh[:, tk(c)], PS[:, BK["b_tp"], :], ACT.Identity, scale=MF[:, 0, CB, b:b + 1],
                                     bias=MF[:, 0, SBT, b:b + 1]).then_inc(b_hh, 1)

            def st_b_rl(c):
                act.wait_ge(b_r1, c + 1)
                nc.scalar.activation(GT[0:NR, tk(c)], PS[0:NR, BK["b_r1"], :], ACT.Relu, bias=BR1[:, :]).then_inc(b_rl, 1)

            wave(A_ORDER, a_h=st_a_h, a_yc=st_a_yc, a_gel=st_a_gel, b_h=st_b_h, b_rl=st_b_rl)

            def routing_exps(d, e):
                act.wait_ge(d, 1)
                nc.scalar.activation(PG[:, :, :], GA[:, :, :], ACT.Exp).then_inc(e, 1)

            def rows_out(gt, gtc):
                for c in range(NC):
                    act.wait_ge(gt, c + 1)
                    nc.scalar.activation(GT[0:NE, tk(c)], PS[0:NE, BK["gt"] + c % 2, 0:CH], ACT.Copy).then_inc(gtc, 1)

            def step(hb, ob, slot, nj, bank0, func, par, first=False):
                def high(j):
                    act.wait_ge(m_act, hb + j + 1)
                    if not first:
                        act.wait_ge(m_out, ob - 1)
                    nc.scalar.activation(AH[par][:, j, :], A32[:, j, :], ACT.Copy).then_inc(m_hi_act, 1)

                for j in range(nj):
                    act.wait_ge(m_hid, hb + j + 1)
                    if not (first and par == 0):
                        act.wait_ge(m_lo, hb - nj + j + 1)
                    bias = 0.0 if slot is None else B1S[slot][:, j:j + 1]
                    nc.scalar.activation(A32[:, j, :], PS[:, bank0 + j, :], func, bias=bias).then_inc(m_act, 1)
                    if j % 2 == 0 and j >= 2:
                        high(j - 1)
                high(nj - 1)

            act.wait_ge(a_x, NC)
            routing_exps(b_d, b_e)
            act.wait_ge(b_d, 2)
            nc.scalar.activation(RV[:, 4, :], RV[:, 3, :], ACT.Exp, scale=0.5).then_inc(b_e, 1)
            for k in range(NC):
                step(NJ0 * k, k, 0, NJ0, 0, ACT.Silu, k % 2, first=k < 2)
                if k == 1:
                    rows_out(b_gt, b_gtc)
            with act.Fori(0, NE // 2) as i:
                for n in range(2 * NC):
                    step(NJ0 * NC + 2 * NC * NJ0 * i + NJ0 * n, NC + 2 * NC * i + n, (1 + n // NC) % 2, NJ0, 0, ACT.Silu, n % 2)

            def st_d_nf(c):
                if c >= 1:
                    act.wait_ge(d_x1, c)
                evacuate(d_tp, d_nf, c, NFM, BK["d_tpn"], COL[:, INW:INW + 1])

            def st_d_x1t(c):
                evacuate(d_tp2, d_x1t, c, XN[:, TPC * c:TPC * (c + 1), :].rearrange("p t d -> p (t d)"), BK["d_tp2"], 1.0)

            def st_d_n2(c):
                if c >= 1:
                    act.wait_ge(d_fc, NF * c)
                evacuate(d_tp3, d_n2, c, N2, BK["d_tp3"], COL[:, FNW:FNW + 1])

            def st_d_g(c):
                if c >= 1:
                    act.wait_ge(d_pj, c)
                for j in range(NF):
                    act.wait_ge(d_fc, NF * c + j + 1)
                    nc.scalar.activation(G1[:, j, :], PS[:, BK["d_fc"] + j, :], ACT.Silu).then_inc(d_g, 1)

            def st_e_l1(c):
                evacuate(e_tp, e_l1, c, H[:, tk(c)], BK["e_tp"], COL[:, L1W:L1W + 1], COL[:, L1B:L1B + 1])

            def st_e_qv(c):
                act.wait_ge(d_x, NC)
                for n in range(TPC // 2):
                    act.wait_ge(e_qk, (TPC // 2) * c + n + 1)
                    t = TPC * c + 2 * n
                    nc.scalar.activation(QV[:, t:t + 2, :], PS[:, BK["e_qk"] + n, 0:2 * QKV].rearrange("p (t n) -> p t n", t=2),
                                         ACT.Copy).then_inc(e_qv, 1)

            def st_e_e(c):
                if c >= CPB:
                    n = 6 * (c % 2)
                    act.wait_ge(e_dd, c - CPB + 1)
                    nc.scalar.activation(SP2[:, n + 2:n + 4, :], SP2[:, n:n + 2, :], ACT.Exp,
                                         scale=float(1.0 / np.sqrt(np.float32(HD)))).then_inc(e_e, 1)

            def st_e_aot(c):
                if c >= 2:
                    act.wait_ge(e_pj, c - 1)
                evacuate(e_at, e_aot, c, AOT[c % 2], BK["e_at"], 1.0)

            def st_e_l2(c):
                evacuate(e_tp2, e_l2, c, H[:, tk(c)], BK["e_tp2"], COL[:, L2W:L2W + 1], COL[:, L2B:L2B + 1])
                nc.scalar.activation(Hh[:, tk(c)], PS[:, BK["e_tp2"], :], ACT.Identity, scale=COL[:, L2W:L2W + 1],
                                     bias=COL[:, L2B:L2B + 1]).then_inc(e_hh, 1)

            wave(B_ORDER, d_nf=st_d_nf, d_x1t=st_d_x1t, d_n2=st_d_n2, d_g=st_d_g, e_l1=st_e_l1, e_qv=st_e_qv, e_e=st_e_e, e_aot=st_e_aot,
                 e_l2=st_e_l2)

            hb, ob = NJ0 * NC * (1 + NE), NC * (1 + NE)
            act.wait_ge(e_h1, NC)
            routing_exps(e_d, e_ee)
            for k in range(2):
                step(hb + NJ1 * k, ob + k, None, NJ1, NJ1 * (k % 2), ACT.Gelu_apprx_tanh, k % 2)
            rows_out(e_gt, e_gtc)
            for k in range(2, 2 * NC):
                step(hb + NJ1 * k, ob + k, None, NJ1, NJ1 * (k % 2), ACT.Gelu_apprx_tanh, k % 2)
            with act.Fori(1, NE // 2) as i:
                for n in range(2 * NC):
                    step(hb + 2 * NC * NJ1 * i + NJ1 * n, ob + 2 * NC * i + n, None, NJ1, NJ1 * (n % 2), ACT.Gelu_apprx_tanh, n % 2)

        @block.tensor
        def _(pe):
            def mm(bank, lhsT, rhs, start=True, stop=True, rows=P, cols=slice(0, CH)):
                return nc.tensor.matmul(PS[0:rows, bank, cols], lhsT, rhs, start=start, stop=stop)

            def turn_tiles(bank, src, rows=P):
                for n in range(TPC):
                    last = nc.tensor.transpose(PS[0:rows, bank, n * P:(n + 1) * P], src(n), ID[:, :])
                return last

            pe.wait_ge(const, 1)
            pe.wait_ge(sc_done, 1)
            for n in range(2):
                for j in range(6):
                    at = (6 * n + j) * B
                    last = mm(7, WMOD[n][:, j * D:(j + 1) * D], SC[:, n, :], cols=slice(at, at + B))
            last.then_inc(modps, 1)
            pe.wait_ge(tr_in, 16 * 18)
            for bank, (lo, hi) in ((4, (0, 4)), (5, (4, 8))):
                for n in range(lo, hi):
                    last = nc.tensor.transpose(PS[:, bank, (n - lo) * P:(n - lo + 1) * P], TR[:, n, :], ID[:, :])
                last.then_inc(turned, 1)
            nc.tensor.transpose(PS[:, 6, 0:P], TR[:, 8, :], ID[:, :])
            nc.tensor.transpose(PS[:, 6, P:QKV], TR[0:QKV - P, 9, :], ID[0:QKV - P, 0:QKV - P])
            nc.tensor.transpose(PS[:, 6, QKV:QKV + P], TR[:, 10, :], ID[:, :]).then_inc(turned, 1)
            pe.wait_ge(scb_done, 1)
            for b in range(B):
                for n in range(2):
                    last = mm(2 * b + n, SCB[:, b, :], WMOD[1][:, n * 3 * D:(n + 1) * 3 * D], cols=slice(0, 3 * D))
            last.then_inc(modps, 1)

            def st_a_tp(c):
                pe.wait_ge(a_xn, c + 1)
                if c == 0:
                    pe.wait_ge(modr_done, 1)
                if c >= 1:
                    pe.wait_ge(a_h, c)
                turn_tiles(BK["a_tp"], lambda n: XN[:, TPC * c + n, :]).then_inc(a_tp, 1)

            def st_a_bu(c):
                if c == 0:
                    pe.wait_ge(tw_done, 3)
                pe.wait_ge(a_h, c + 1)
                if c >= 1:
                    pe.wait_ge(a_u, c)
                mm(BK["a_bu"], TW[:, T_BW, :], H[:, tk(c)]).then_inc(a_bu, 1)

            def st_a_y(c):
                pe.wait_ge(a_wc, c + 1)
                if c >= 1:
                    pe.wait_ge(a_yc, c)
                mm(BK["a_y"], TW[:, T_D, :], H[:, tk(c)], stop=False)
                mm(BK["a_y"], TW[:, T_M1, :], WC, start=False, stop=False)
                pe.wait_ge(a_ws, c + 1)
                mm(BK["a_y"], TW[:, T_M2, :], WS, start=False).then_inc(a_y, 1)

            def st_a_hid(c):
                if c == 0:
                    pe.wait_ge(lru_in, 32)
                pe.wait_ge(a_yc, c + 1)
                for j in range(NJ0 + 1):
                    n = NJ0 * c + j
                    if j < NJ0:
                        if n >= 2:
                            pe.wait_ge(a_gel, n - 1)
                        mm(BK["a_hid"] + n % 2, LW1[:, j * P:(j + 1) * P], Y[c % 2]).then_inc(a_hid, 1)
                    if j == 0:
                        if c >= 1:
                            pe.wait_ge(a_t, c)
                        continue
                    pe.wait_ge(a_gel, n)
                    last = mm(BK["a_z"], LW2[:, j - 1, :], G0[:, j - 1, :], start=(j == 1), stop=(j == NJ0))
                last.then_inc(a_z, 1)

            def st_a_bk(c):
                pe.wait_ge(a_t, c + 1)
                if c >= 1:
                    pe.wait_ge(a_x, c)
                turn_tiles(BK["a_bk"], lambda n: T2[c % 2][:, n * P:(n + 1) * P]).then_inc(a_bk, 1)

            def st_b_tp(c):
                if c == 0:
                    pe.wait_ge(a_h, NC)
                else:
                    pe.wait_ge(b_hh, c)
                pe.wait_ge(b_xn, c + 1)
                turn_tiles(BK["b_tp"], lambda n: XN[:, TPC * c + n, :]).then_inc(b_tp, 1)

            def st_b_r1(c):
                if c == 0:
                    pe.wait_ge(a_u, NC)
                    pe.wait_ge(small_in, 16 * 18)
                else:
                    pe.wait_ge(b_rl, c)
                pe.wait_ge(b_h, c + 1)
                mm(BK["b_r1"], WR1[:, :], H[:, tk(c)], rows=NR).then_inc(b_r1, 1)

            def st_b_lg(c):
                if c == 0:
                    pe.wait_ge(mod_done, 1)
                pe.wait_ge(b_rl, c + 1)
                for t in tiles(c):
                    last = mm(BK["b_lg"], GT[0:NR + 1, t * P:(t + 1) * P], WR2[:, :], cols=slice(t * NE, (t + 1) * NE))
                last.then_inc(b_lg, 1)

            wave(A_ORDER, a_tp=st_a_tp, a_bu=st_a_bu, a_y=st_a_y, a_hid=st_a_hid, a_bk=st_a_bk,
                 b_tp=st_b_tp, b_r1=st_b_r1, b_lg=st_b_lg)

            def hidden(hb, wq, slot, c, nj, bank0, back, first=False):
                if wq is not None:
                    pe.wait_ge(w_split, wq)
                for j in range(nj):
                    if not first:
                        pe.wait_ge(m_act, hb + j + 1 - back)
                    mm(bank0 + j, W1h[slot][:, j, :], Hh[:, tk(c)], stop=False)
                    mm(bank0 + j, W1h[slot][:, j, :], Hl[:, tk(c)], start=False, stop=False)
                    mm(bank0 + j, W1l[slot][:, j, :], Hh[:, tk(c)], start=False).then_inc(m_hid, 1)

            def output(hb, ob, slot, par, nj, first=False):
                if not first:
                    pe.wait_ge(m_gated, ob - 1)
                for j in range(nj):
                    pe.wait_ge(m_lo, hb + j + 1)
                    mm(4 + par, W2h[slot][:, j, :], AH[par][:, j, :], start=(j == 0), stop=False)
                    mm(4 + par, W2l[slot][:, j, :], AH[par][:, j, :], start=False, stop=False)
                    last = mm(4 + par, W2h[slot][:, j, :], AL[par][:, j, :], start=False, stop=(j == nj - 1))
                last.then_inc(m_out, 1)

            def weights_rows(g, lg_read, gt):
                pe.wait_ge(g, 1)
                for c in range(NC):
                    if c >= 2:
                        pe.wait_ge(b_gtc if gt is b_gt else e_gtc, c - 1)
                    turn_tiles(BK["gt"] + c % 2, lambda n: GA[:, TPC * c + n, :], rows=NE).then_inc(gt, 1)

            pe.wait_ge(b_hl, NC)
            pe.wait_ge(b_hh, NC)
            pe.wait_ge(b_rl, NC)
            pe.wait_ge(a_x, NC)
            hidden(0, 1, 0, 0, NJ0, 0, NJ0, first=True)
            hidden(NJ0, None, 0, 1, NJ0, 0, NJ0)
            weights_rows(b_g, None, b_gt)
            output(0, 0, 0, 0, NJ0, first=True)
            for k in range(2, NC):
                hidden(NJ0 * k, None, 0, k, NJ0, 0, NJ0)
                output(NJ0 * (k - 1), k - 1, 0, (k - 1) % 2, NJ0, first=k == 2)
            with pe.Fori(0, NE // 2) as i:
                for n in range(2 * NC):
                    hb, ob = NJ0 * NC + 2 * NC * NJ0 * i + NJ0 * n, NC + 2 * NC * i + n
                    slot = (1 + n // NC) % 2
                    hidden(hb, 2 * i + 2 + n // NC if n % NC == 0 else None, slot, n % NC, NJ0, 0, NJ0)
                    output(hb - NJ0, ob - 1, slot if n % NC else 1 - slot, (n + 1) % 2, NJ0)
            output(NJ0 * (NC * (1 + NE) - 1), NC * (1 + NE) - 1, NE % 2, 1, NJ0)

            def st_c_be(c):
                if c == 0:
                    pe.wait_ge(b_gtc, NC)
                else:
                    pe.wait_ge(c_t, c)
                mm(BK["c_be"], BE2[:, :], GT[0:NE, tk(c)]).then_inc(c_be, 1)

            def st_c_bk(c):
                pe.wait_ge(c_t, c + 1)
                if c >= 1:
                    pe.wait_ge(c_x, c)
                turn_tiles(BK["c_bk"], lambda n: TE[c % 2][:, n * P:(n + 1) * P]).then_inc(c_bk, 1)

            def st_d_tp(c):
                pe.wait_ge(d_nt, c + 1)
                if c >= 1:
                    pe.wait_ge(d_x1, c)
                else:
                    pe.wait_ge(m_act, NJ0 * NC * (1 + NE))
                turn_tiles(BK["d_tp"], lambda n: HT[:, TPC * c + n, :])
                turn_tiles(BK["d_tpn"], lambda n: NTK[:, TPC * c + n, :]).then_inc(d_tp, 1)

            def st_d_tp2(c):
                pe.wait_ge(d_x1, c + 1)
                if c >= 1:
                    pe.wait_ge(d_x1t, c)
                turn_tiles(BK["d_tp2"], lambda n: X1[:, c * CH + n * P:c * CH + (n + 1) * P]).then_inc(d_tp2, 1)

            def st_d_tp3(c):
                pe.wait_ge(d_n2t, c + 1)
                if c >= 1:
                    pe.wait_ge(d_n2, c)
                turn_tiles(BK["d_tp3"], lambda n: XN[:, TPC * c + n, :]).then_inc(d_tp3, 1)

            def st_d_fc(c):
                pe.wait_ge(d_n2, c + 1)
                if c == 0:
                    pe.wait_ge(m_gated, NC * (1 + NE))
                for j in range(NF):
                    if c >= 1:
                        pe.wait_ge(d_g, NF * (c - 1) + j + 1)
                    mm(BK["d_fc"] + j, TW[:, T_F0 + j, :], N2).then_inc(d_fc, 1)

            def st_d_pj(c):
                if c >= 1:
                    pe.wait_ge(d_u, c)
                else:
                    pe.wait_ge(c_t, NC)
                for j in range(NF):
                    pe.wait_ge(d_g, NF * c + j + 1)
                    last = mm(BK["d_pj"], TW[:, T_P0 + j, :], G1[:, j, :], start=(j == 0), stop=(j == NF - 1))
                last.then_inc(d_pj, 1)

            def st_d_bk(c):
                pe.wait_ge(d_u, c + 1)
                if c >= 1:
                    pe.wait_ge(d_x, c)
                else:
                    pe.wait_ge(c_x, NC)
                turn_tiles(BK["d_bk"], lambda n: U2[:, n * P:(n + 1) * P]).then_inc(d_bk, 1)

            def st_e_tp(c):
                pe.wait_ge(e_n1, c + 1)
                if c >= 1:
                    pe.wait_ge(e_l1, c)
                else:
                    pe.wait_ge(d_x1, NC)
                turn_tiles(BK["e_tp"], lambda n: XN[:, TPC * c + n, :]).then_inc(e_tp, 1)

            def st_e_qk(c):
                pe.wait_ge(e_l1, c + 1)
                if c == 0:
                    pe.wait_ge(d_n2t, NC)
                for n in range(TPC // 2):
                    if c >= 1:
                        pe.wait_ge(e_qv, (TPC // 2) * (c - 1) + n + 1)
                    for m in range(2):
                        t = TPC * c + 2 * n + m
                        last = mm(BK["e_qk"] + n, H[:, t * P:(t + 1) * P], TW[:, T_Q0:T_Q0 + 2, :].rearrange("p a b -> p (a b)")[:, 0:QKV],
                                  cols=slice(m * QKV, (m + 1) * QKV))
                    last.then_inc(e_qk, 1)

            def st_e_at(c):
                pe.wait_ge(e_ao, c + 1)
                if c >= 1:
                    pe.wait_ge(e_aot, c)
                turn_tiles(BK["e_at"], lambda n: AO[:, TPC * c + n, :]).then_inc(e_at, 1)

            def st_e_pj(c):
                pe.wait_ge(e_aot, c + 1)
                if c >= 1:
                    pe.wait_ge(e_h1, c)
                for n in range(TPC):
                    last = mm(BK["e_pj"], AOT[c % 2][:, n * P:(n + 1) * P], TW[:, T_PJ, :], cols=slice(n * P, (n + 1) * P))
                last.then_inc(e_pj, 1)

            def st_e_tp2(c):
                pe.wait_ge(e_n2, c + 1)
                if c >= 1:
                    pe.wait_ge(e_hh, c)
                turn_tiles(BK["e_tp2"], lambda n: XN[:, TPC * c + n, :]).then_inc(e_tp2, 1)

            def st_e_lg(c):
                pe.wait_ge(e_l2, c + 1)
                for t in tiles(c):
                    last = mm(BK["e_lg"], H[:, t * P:(t + 1) * P], RT[:, :], cols=slice(t * NE, (t + 1) * NE))
                last.then_inc(e_lg, 1)

            wave(B_ORDER, c_be=st_c_be, c_bk=st_c_bk, d_tp=st_d_tp, d_tp2=st_d_tp2, d_tp3=st_d_tp3, d_fc=st_d_fc, d_pj=st_d_pj,
                 d_bk=st_d_bk, e_tp=st_e_tp, e_qk=st_e_qk, e_at=st_e_at, e_pj=st_e_pj, e_tp2=st_e_tp2, e_lg=st_e_lg)

            HB1, OB1 = NJ0 * NC * (1 + NE), NC * (1 + NE)
            pe.wait_ge(e_hl, NC)
            pe.wait_ge(e_hh, NC)
            pe.wait_ge(e_h1, NC)
            for k in range(2):
                hidden(HB1 + NJ1 * k, 2 + NE if k == 0 else None, 1, k, NJ1, NJ1 * k, 2 * NJ1, first=True)
            pe.wait_ge(e_cs, 1)
            mm(7, UT[:, :], CSO[:, :, :].rearrange("p e t -> p (e t)"), stop=False, cols=slice(0, NE * NT))
            mm(7, ON[:, :], CS[:, :, :].rearrange("p e t -> p (e t)"), start=False, cols=slice(0, NE * NT)).then_inc(e_cn, 1)
            weights_rows(e_g, None, e_gt)
            output(HB1, OB1, 1, 0, NJ1)
            for k in range(2, 2 * NC):
                slot = (1 + k // NC) % 2
                hidden(HB1 + NJ1 * k, 2 + NE + k // NC if k % NC == 0 else None, slot, k % NC, NJ1, NJ1 * (k % 2), 2 * NJ1)
                output(HB1 + NJ1 * (k - 1), OB1 + k - 1, slot if k % NC else 1 - slot, (k - 1) % 2, NJ1)
            with pe.Fori(1, NE // 2) as i:
                for n in range(2 * NC):
                    hb, ob = HB1 + 2 * NC * NJ1 * i + NJ1 * n, OB1 + 2 * NC * i + n
                    slot = (1 + n // NC) % 2
                    hidden(hb, 2 + NE + 2 * i + n // NC if n % NC == 0 else None, slot, n % NC, NJ1, NJ1 * (n % 2), 2 * NJ1)
                    output(hb - NJ1, ob - 1, slot if n % NC else 1 - slot, (n + 1) % 2, NJ1)
            output(HB1 + NJ1 * (NC * NE - 1), OB1 + NC * NE - 1, 0, 1, NJ1)
            for c in range(NC):
                pe.wait_ge(m_acc, OB1 + NC * (NE - 1) + c + 1)
                pe.wait_ge(e_gtc, NC)
                if c >= 2:
                    pe.wait_ge(e_o, c - 1)
                turn_tiles(6 + c % 2, lambda n: ACC[:, c * CH + n * P:c * CH + (n + 1) * P]).then_inc(e_bk, 1)

        @block.vector
        def _(dve):
            linked = [0]

            def link(ins):
                linked[0] += 1
                ins.then_inc(dch, 1)
                dve.wait_ge(dch, linked[0])

            V = nc.vector
            LN2H, LN2L = two_part(np.log(2.0))
            PI2A, rest = two_part(2.0 * np.pi)
            PI2B, PI2C = two_part(rest)
            ROUND = 1.5 * 2.0 ** 23

            def exp3(dst, src, scale):
                link(V.tensor_scalar(EX[:, :], src, scale, 88.0, ALU.mult, ALU.min))
                link(V.tensor_scalar(EX[:, :], EX[:, :], -87.0, None, ALU.max))
                link(V.tensor_scalar(EK[:, :], EX[:, :], float(np.log2(np.e)), ROUND, ALU.mult, ALU.add))
                link(V.tensor_scalar(EK[:, :], EK[:, :], ROUND, None, ALU.subtract))
                link(V.scalar_tensor_tensor(EF[:, :], EK[:, :], -LN2H, EX[:, :], ALU.mult, ALU.add))
                link(V.scalar_tensor_tensor(EF[:, :], EK[:, :], -LN2L, EF[:, :], ALU.mult, ALU.add))
                link(V.tensor_scalar(EI[:, :], EK[:, :], 127.0, 2.0 ** 23, ALU.add, ALU.mult))
                link(V.tensor_scalar(EQ[:, :], EF[:, :], 1 / 5040.0, None, ALU.mult))
                for f in (720, 120, 24, 6, 2, 1):
                    link(V.scalar_tensor_tensor(EQ[:, :], EQ[:, :], 1.0 / f, EF[:, :], ALU.add, ALU.mult))
                link(V.scalar_tensor_tensor(dst, EQ[:, :], 1.0, EI[:, :].bitcast(F32), ALU.add, ALU.mult))

            V.memset(SG[:, 0:2], 1.0)
            link(V.memset(SM[:, 22:23], 0.5))
            V.memset(SG[96:128, 0:1], -1.0)
            V.memset(SG[32:64, 1:2], -1.0)
            link(V.memset(SG[96:128, 1:2], -1.0))
            link(V.memset(GT[32:33, :], 1.0))

            dve.wait_ge(col_in, 16 * 9)
            exp3(SM[:, 0:3], COL[:, 0:3], 1.0)
            link(V.tensor_scalar(SM[:, 12:13], SM[:, 1:2], 1.0 / (2 * np.pi), ROUND, ALU.mult, ALU.add))
            link(V.tensor_scalar(SM[:, 12:13], SM[:, 12:13], ROUND, None, ALU.subtract))
            link(V.scalar_tensor_tensor(SM[:, 8:9], SM[:, 12:13], -PI2A, SM[:, 1:2], ALU.mult, ALU.add))
            link(V.scalar_tensor_tensor(SM[:, 8:9], SM[:, 12:13], -PI2B, SM[:, 8:9], ALU.mult, ALU.add))
            link(V.scalar_tensor_tensor(SM[:, 8:9], SM[:, 12:13], -PI2C, SM[:, 8:9], ALU.mult, ALU.add))
            link(V.tensor_scalar(SM[:, 8:9], SM[:, 8:9], 3.1415925, -3.1415925, ALU.min, ALU.max))
            link(V.scalar_tensor_tensor(SM[:, 9:10], SM[:, 8:9], -1.0, SM[:, 8:9], ALU.mult, ALU.min))
            V.tensor_scalar(SM[:, 9:10], SM[:, 9:10], np.pi / 2, None, ALU.add).then_inc(trig_in, 1)
            exp3(DEC[:, :], SM[:, 0:3], -1.0)
            link(V.tensor_tensor(SM[:, 18:19], DEC[:, 0:1], DEC[:, 0:1], ALU.mult))
            link(V.tensor_scalar(SM[:, 18:19], SM[:, 18:19], -1.0, 1.0, ALU.mult, ALU.add))
            V.tensor_scalar(SM[:, 18:19], SM[:, 18:19], 0.0, None, ALU.max).then_inc(gam_in, 1)

            dve.wait_ge(sc_done, 1)
            for b in range(B):
                last = V.tensor_copy(SCB[:, b, :], SC[:, 1, b:b + 1].to_broadcast([P, P]))
            last.then_inc(scb_done, 1)

            def clamp_gates(g, tmp):
                link(V.tensor_scalar(tmp, g, 0.0, 2.0, ALU.is_ge, ALU.mult))
                link(V.scalar_tensor_tensor(g, g, -1.0, g, ALU.mult, ALU.max))
                link(V.tensor_scalar(g, g, 0.25, None, ALU.max))
                return V.scalar_tensor_tensor(g, tmp, 1.0, g, ALU.subtract, ALU.mult)

            dve.wait_ge(modps, 1)
            link(V.tensor_copy(MF[:, :, :, :].rearrange("p n j b -> p (n j b)"), PS[:, 7, 0:2 * 6 * B]))
            for j in (CA, CB):
                link(V.tensor_scalar(MF[:, :, j, :], MF[:, :, j, :], 1.0, None, ALU.add))
            link(clamp_gates(MF[:, :, GAT, :], GTMP[:, 0, :, :]))
            clamp_gates(MF[:, :, GB, :], GTMP[:, 1, :, :]).then_inc(mod_done, 1)

            dve.wait_ge(trig, 1)
            V.memset(TC[:, 0:1], 1.0)
            V.memset(TS[:, 0:1], 0.0)
            V.tensor_copy(TC[:, 1:2], SM[:, 11:12])
            link(V.tensor_copy(TS[:, 1:2], SM[:, 10:11]))
            k = 1
            while k < L:
                n = min(k, L - k)
                o, i = slice(k + 1, k + n + 1), slice(1, n + 1)
                c1, s1 = TC[:, k:k + 1], TS[:, k:k + 1]
                V.tensor_scalar(DTMP[:, 0:n], TS[:, i], s1, None, ALU.mult)
                link(V.tensor_scalar(Q[:, 0:n], TC[:, i], s1, None, ALU.mult))
                V.scalar_tensor_tensor(TC[:, o], TC[:, i], c1, DTMP[:, 0:n], ALU.mult, ALU.subtract)
                link(V.scalar_tensor_tensor(TS[:, o], TS[:, i], c1, Q[:, 0:n], ALU.mult, ALU.add))
                k *= 2

            dve.wait_ge(turned, 1)
            V.tensor_copy(TW[:, T_BW, :], PS[:, 4, 0:P])
            V.tensor_scalar(TW[:, T_M1, :], PS[:, 4, P:2 * P], SG[:, 1:2], None, ALU.mult)
            V.tensor_scalar(TW[:, T_M2, :], PS[:, 4, 2 * P:3 * P], -1.0, None, ALU.mult)
            V.tensor_copy(TW[:, T_D, :], PS[:, 4, 3 * P:4 * P]).then_inc(tw_done, 1)
            dve.wait_ge(turned, 2)
            V.tensor_copy(TW[:, T_F0:T_F0 + 4, :].rearrange("p a b -> p (a b)"), PS[:, 5, :]).then_inc(tw_done, 1)
            dve.wait_ge(turned, 3)
            V.tensor_copy(TW[:, T_Q0:T_Q0 + 2, :].rearrange("p a b -> p (a b)")[:, 0:QKV], PS[:, 6, 0:QKV])
            V.tensor_copy(TW[:, T_PJ, :], PS[:, 6, QKV:QKV + P]).then_inc(tw_done, 1)

            dve.wait_ge(gam, 1)
            link(V.tensor_tensor(SG[:, 2:3], SG[:, 0:1], SM[:, 19:20], ALU.mult))
            V.tensor_scalar(TIN[0:64, :], TC[0:64, 0:L], SG[0:64, 2:3], None, ALU.mult)
            link(V.tensor_scalar(TIN[64:128, :], TS[64:128, 0:L], SG[64:128, 2:3], None, ALU.mult))

            dve.wait_ge(modps, 2)
            for b in range(B):
                for n in range(2):
                    last = V.tensor_copy(MODR[:, b, 3 * n:3 * n + 3, :].rearrange("p a b -> p (a b)"), PS[:, 2 * b + n, 0:3 * D])
            link(last)
            for j in (CA, CB):
                link(V.tensor_scalar(MODR[:, :, j, :], MODR[:, :, j, :], 1.0, None, ALU.add))
            clamp_gates(MODR[:, :, GB, :], U[0][:, 0:B * D].rearrange("p (b d) -> p b d", b=B)).then_inc(modr_done, 1)

            def stats(c, tile, ve, eps, rms=False):
                t = tiles(c)
                for n in range(TPC):
                    last = V.bn_stats(ST[:, t[n], :], tile(n))
                link(last)
                for n in range(TPC):
                    last = V.bn_aggr(MV[:, t[n], :], ST[:, t[n], :])
                link(last)
                v = VE[:, t[0]:t[-1] + 1]
                mean, var = MV[:, t[0]:t[-1] + 1, 0], MV[:, t[0]:t[-1] + 1, 1]
                if rms:
                    link(V.tensor_tensor(v, mean, mean, ALU.mult))
                    V.scalar_tensor_tensor(v, v, eps, var, ALU.add, ALU.add).then_inc(ve, 1)
                else:
                    V.tensor_scalar(v, var, eps, None, ALU.add).then_inc(ve, 1)

            def normalise(c, dst, src, rs, done, rms=False):
                dve.wait_ge(rs, c + 1)
                for n, t in enumerate(tiles(c)):
                    if rms:
                        last = V.tensor_scalar(dst(n), src(n), RS[:, t:t + 1], None, ALU.mult)
                    else:
                        last = V.tensor_scalar(dst(n), src(n), MV[:, t, 0:1], RS[:, t:t + 1], ALU.subtract, ALU.mult)
                last.then_inc(done, 1)

            def rows(buf, c):
                return lambda n: buf[:, TPC * c + n, :]

            def add_x(c, bank, bk, done):
                dve.wait_ge(bk, c + 1)
                x = X[:, TPC * c:TPC * (c + 1), :].rearrange("p t d -> p (t d)")
                V.tensor_tensor(x, x, PS[:, bank, :], ALU.add).then_inc(done, 1)

            def st_a_ve(c):
                dve.wait_ge(x_in, 16 * NC)
                stats(c, rows(X, c), a_ve, 1e-5)

            def st_a_u(c):
                dve.wait_ge(a_bu, c + 1)
                if c == 0:
                    dve.wait_ge(modr_done, 1)
                half = slice((c % CPB) * CH, (c % CPB + 1) * CH)
                link(V.tensor_tensor(Q, PS[:, BK["a_bu"], :], TIN[:, half], ALU.mult))
                if c >= 2:
                    dve.wait_ge(a_ws, c - 1)
                    dve.wait_ge(a_wc, c - 1)
                start = 0.0 if c % CPB == 0 else U[(c - 1) % 2][:, CH - 1:CH]
                V.tensor_tensor_scan(U[c % 2], DEC[:, 0:1].to_broadcast([P, CH]), Q, start, ALU.mult, ALU.add).then_inc(a_u, 1)
                dve.wait_ge(a_u, c + 1)
                if c >= 1:
                    dve.wait_ge(a_y, c)
                V.tensor_tensor(WC, TC[:, half], U[c % 2], ALU.mult).then_inc(a_wc, 1)

            def st_a_t(c):
                dve.wait_ge(a_z, c + 1)
                if c == 0:
                    dve.wait_ge(trig, 2)
                link(V.scalar_tensor_tensor(T1, PS[:, BK["a_z"], :], SM[:, SIG:SIG + 1], H[:, tk(c)], ALU.mult, ALU.add))
                if c >= 2:
                    dve.wait_ge(a_bk, c - 1)
                V.tensor_scalar(T2[c % 2], T1, MF[:, 0, GAT, c // CPB:c // CPB + 1], None, ALU.mult).then_inc(a_t, 1)

            def st_b_ve(c):
                dve.wait_ge(a_x, c + 1)
                stats(c, rows(X, c), b_ve, 1e-5)

            def st_b_hl(c):
                dve.wait_ge(b_hh, c + 1)
                V.tensor_tensor(Hl[:, tk(c)], H[:, tk(c)], Hh[:, tk(c)].bitcast(F32), ALU.subtract).then_inc(b_hl, 1)

            wave(A_ORDER, a_ve=st_a_ve, a_xn=lambda c: normalise(c, rows(XN, c), rows(X, c), a_rs, a_xn), a_u=st_a_u, a_t=st_a_t,
                 a_x=lambda c: add_x(c, BK["a_bk"], a_bk, a_x), b_ve=st_b_ve,
                 b_xn=lambda c: normalise(c, rows(XN, c), rows(X, c), b_rs, b_xn), b_hl=st_b_hl)

            def each(col):
                return col.rearrange("p (t a) -> p t a", a=1).to_broadcast([P, NT, NE])

            def top_two(bank, lg, d, e):
                dve.wait_ge(lg, NC)
                logits = PS[:, bank, 0:NT * NE].rearrange("p (t e) -> p t e", e=NE)
                link(V.tensor_reduce(RV[:, 0, :], logits, AX.X, ALU.max))
                V.tensor_tensor(GA[:, :, :], logits, each(RV[:, 0, :]), ALU.subtract).then_inc(d, 1)
                dve.wait_ge(e, 1)
                link(V.tensor_reduce(RV[:, 1, :], PG[:, :, :], AX.X, ALU.add))
                link(V.reciprocal(RV[:, 2, :], RV[:, 1, :]))
                link(V.tensor_tensor(PG[:, :, :], PG[:, :, :], each(RV[:, 2, :]), ALU.mult))
                for t in range(NT):
                    last = V.max(M8[:, t, :], PG[:, t, :])
                link(last)
                for t in range(NT):
                    last = V.max_index(I8[:, t, :], M8[:, t, :], PG[:, t, :])
                link(last)
                link(V.tensor_copy(IF[:, :, :], I8[:, :, 0:2]))
                V.tensor_tensor(EQ1[:, :, :], IO[:, :, :], IF[:, :, 0:1].to_broadcast([P, NT, NE]), ALU.is_equal)
                link(V.tensor_tensor(EQ2[:, :, :], IO[:, :, :], IF[:, :, 1:2].to_broadcast([P, NT, NE]), ALU.is_equal))

            def weigh(w1, w2):
                link(V.tensor_tensor(EQ1[:, :, :], EQ1[:, :, :], each(w1), ALU.mult))
                link(V.tensor_tensor(EQ2[:, :, :], EQ2[:, :, :], each(w2), ALU.mult))
                return V.tensor_tensor(GA[:, :, :], EQ1[:, :, :], EQ2[:, :, :], ALU.add)

            dve.wait_ge(a_x, NC)
            dve.wait_ge(b_hl, NC)
            dve.wait_ge(const, 4)
            top_two(BK["b_lg"], b_lg, b_d, b_e)
            V.tensor_tensor(RV[:, 3, :], M8[:, :, 1], M8[:, :, 0], ALU.subtract).then_inc(b_d, 1)
            dve.wait_ge(b_e, 2)
            link(V.tensor_scalar(RV[:, 5, :], RV[:, 4, :], 1.0, None, ALU.add))
            link(V.reciprocal(RV[:, 0, :], RV[:, 5, :]))
            link(V.tensor_tensor(RV[:, 1, :], RV[:, 4, :], RV[:, 0, :], ALU.mult))
            weigh(RV[:, 0, :], RV[:, 1, :]).then_inc(b_g, 1)

            def rests(hb, hib, ob, nj, par, first=False):
                def rest(j):
                    dve.wait_ge(m_hi_act if j % 2 else m_hi, hib + j // 2 + 1)
                    V.tensor_tensor(AL[par][:, j, :], A32[:, j, :], AH[par][:, j, :].bitcast(F32), ALU.subtract).then_inc(m_lo, 1)

                for j in range(0, nj, 2):
                    dve.wait_ge(m_act, hb + j + 1)
                    if not first:
                        dve.wait_ge(m_out, ob - 1)
                    V.tensor_copy(AH[par][:, j, :], A32[:, j, :]).then_inc(m_hi, 1)
                    rest(j)
                    rest(j + 1)

            def gate(ob, par, first=False):
                dve.wait_ge(m_out, ob + 1)
                dve.wait_ge(m_wb, ob + 1)
                if not first:
                    dve.wait_ge(m_acc, ob - 1)
                V.tensor_tensor(MG[par], PS[:, 4 + par, :], WB[par], ALU.mult).then_inc(m_gated, 1)

            rests(0, 0, 0, NJ0, 0, first=True)
            for k in range(1, NC):
                rests(NJ0 * k, NJ0 // 2 * k, k, NJ0, k % 2, first=k < 2)
                gate(k - 1, (k - 1) % 2, first=k < 3)
            with dve.Fori(0, NE // 2) as i:
                for n in range(2 * NC):
                    hb, ob = NJ0 * NC + 2 * NC * NJ0 * i + NJ0 * n, NC + 2 * NC * i + n
                    rests(hb, NJ0 // 2 * NC + NC * NJ0 * i + NJ0 // 2 * n, ob, NJ0, n % 2)
                    gate(ob - 1, (n + 1) % 2)
            gate(NC * (1 + NE) - 1, 1)

            def st_c_t(c):
                dve.wait_ge(c_be, c + 1)
                dve.wait_ge(m_acc, NC * NE + c + 1)
                if c >= 2:
                    dve.wait_ge(c_bk, c - 1)
                link(V.scalar_tensor_tensor(TE[c % 2], PS[:, BK["c_be"], :], COL[:, BS2:BS2 + 1], ACC[:, tk(c)], ALU.add, ALU.add))
                V.tensor_scalar(TE[c % 2], TE[c % 2], MF[:, 0, GB, c // CPB:c // CPB + 1], None, ALU.mult).then_inc(c_t, 1)

            def st_d_ve(c):
                dve.wait_ge(c_x, c + 1)
                stats(c, rows(X, c), d_ve, 1e-5)

            def st_d_ve2(c):
                dve.wait_ge(d_ht, c + 1)
                stats(c, rows(HT, c), d_ve2, 1e-6, rms=True)

            def st_d_nt(c):
                if c == 0:
                    dve.wait_ge(m_lo, NJ0 * NC * (1 + NE))
                    dve.wait_ge(m_hi_act, NJ0 // 2 * NC * (1 + NE))
                    dve.wait_ge(m_acc, NC * (1 + NE))
                normalise(c, rows(NTK, c), rows(HT, c), d_rs2, d_nt, rms=True)

            def st_d_x1(c):
                dve.wait_ge(d_nf, c + 1)
                if c >= 2:
                    dve.wait_ge(d_x1, c - 1)
                start = 0.0 if c % CPB == 0 else HS[(c - 1) % 2][:, CH - 1:CH]
                V.tensor_tensor_scan(HS[c % 2], DEC[:, 2:3].to_broadcast([P, CH]), NFM, start, ALU.mult, ALU.add).then_inc(d_hs, 1)
                if c >= 1:
                    dve.wait_ge(d_x1, c)
                link(V.scalar_tensor_tensor(SK, NFM, COL[:, DS:DS + 1], PS[:, BK["d_tp"], :], ALU.mult, ALU.add))
                dve.wait_ge(d_hs, c + 1)
                V.scalar_tensor_tensor(X1[:, tk(c)], HS[c % 2], COL[:, CO:CO + 1], SK, ALU.mult, ALU.add).then_inc(d_x1, 1)

            def st_d_ve3(c):
                dve.wait_ge(d_x1t, c + 1)
                stats(c, rows(XN, c), d_ve3, 1e-6, rms=True)

            def st_d_u(c):
                dve.wait_ge(d_pj, c + 1)
                link(V.tensor_tensor(U1, PS[:, BK["d_pj"], :], X1[:, tk(c)], ALU.add))
                if c >= 1:
                    dve.wait_ge(d_bk, c)
                V.tensor_scalar(U2, U1, MF[:, 1, GAT, c // CPB:c // CPB + 1], None, ALU.mult).then_inc(d_u, 1)

            def st_e_ve(c):
                dve.wait_ge(d_x, c + 1)
                stats(c, rows(X, c), e_ve, 1e-5)

            def st_e_ve2(c):
                dve.wait_ge(e_mod, c + 1)
                stats(c, rows(HT, c), e_ve2, 1e-5)

            def qkv_of(t):
                g = QV[:, t, :].rearrange("p (g w) -> p g w", w=GW)
                q = g[:, :, 0:QPK * HD].rearrange("p g (q d) -> p g q d", d=HD)
                k = g[:, :, QPK * HD:(QPK + 1) * HD].rearrange("p g (a d) -> p g a d", a=1).to_broadcast([P, NKV, QPK, HD])
                v = g[:, :, (QPK + 1) * HD:].rearrange("p g (a d) -> p g a d", a=1).to_broadcast([P, NKV, QPK, HD])
                return q, k, v

            def heads(buf, n):
                return buf[:, n * D:(n + 1) * D].rearrange("p (g q d) -> p g q d", g=NKV, q=QPK)

            def probs(c):
                return SP2[:, 6 * (c % 2):6 * (c % 2) + 6, :]

            def st_e_dd(c):
                if c < CPB:
                    return
                dve.wait_ge(e_qv, (TPC // 2) * (c + 1))
                for n, t in enumerate(tiles(c)):
                    q, k1, _ = qkv_of(t)
                    _, k0, _ = qkv_of(t - NT // B)
                    V.tensor_tensor(heads(PR, n), q, k0, ALU.mult)
                    last = V.tensor_tensor(heads(PR, TPC + n), q, k1, ALU.mult)
                link(last)
                s = probs(c)
                link(V.tensor_reduce(s[:, 0:2, :].rearrange("p a m -> p (a m)"), PR.rearrange("p (m d) -> p m d", d=HD), AX.X, ALU.add))
                link(V.tensor_tensor(s[:, 4, :], s[:, 0, :], s[:, 1, :], ALU.max))
                V.tensor_tensor(s[:, 0, :], s[:, 0, :], s[:, 4, :], ALU.subtract)
                V.tensor_tensor(s[:, 1, :], s[:, 1, :], s[:, 4, :], ALU.subtract).then_inc(e_dd, 1)

            def st_e_ao(c):
                ao = AO[:, TPC * c:TPC * (c + 1), :].rearrange("p t d -> p (t d)")
                if c < CPB:
                    dve.wait_ge(e_qv, (TPC // 2) * (c + 1))
                    for n, t in enumerate(tiles(c)):
                        last = V.tensor_copy(heads(ao, n), qkv_of(t)[2])
                    last.then_inc(e_ao, 1)
                    return
                dve.wait_ge(e_e, c - CPB + 1)
                s = probs(c)
                link(V.tensor_tensor(s[:, 4, :], s[:, 2, :], s[:, 3, :], ALU.add))
                link(V.reciprocal(s[:, 5, :], s[:, 4, :]))
                V.tensor_tensor(s[:, 2, :], s[:, 2, :], s[:, 5, :], ALU.mult)
                link(V.tensor_tensor(s[:, 3, :], s[:, 3, :], s[:, 5, :], ALU.mult))

                def prob(a, n):
                    return s[:, a, n * NH:(n + 1) * NH].rearrange("p (g q a) -> p g q a", g=NKV, a=1).to_broadcast([P, NKV, QPK, HD])

                for n, t in enumerate(tiles(c)):
                    V.tensor_tensor(heads(PR, n), qkv_of(t - NT // B)[2], prob(2, n), ALU.mult)
                    last = V.tensor_tensor(heads(PR2, n), qkv_of(t)[2], prob(3, n), ALU.mult)
                link(last)
                V.tensor_tensor(ao, PR[:, 0:CH], PR2[:, 0:CH], ALU.add).then_inc(e_ao, 1)

            def st_e_h1(c):
                dve.wait_ge(e_pj, c + 1)
                h = HT[:, TPC * c:TPC * (c + 1), :].rearrange("p t d -> p (t d)")
                V.tensor_tensor(h, h, PS[:, BK["e_pj"], :], ALU.add).then_inc(e_h1, 1)
                dve.wait_ge(e_h1, c + 1)
                stats(c, rows(HT, c), e_ve3, 1e-5)

            def st_e_hl(c):
                dve.wait_ge(e_hh, c + 1)
                V.tensor_tensor(Hl[:, tk(c)], H[:, tk(c)], Hh[:, tk(c)].bitcast(F32), ALU.subtract).then_inc(e_hl, 1)

            wave(B_ORDER, c_t=st_c_t, c_x=lambda c: add_x(c, BK["c_bk"], c_bk, c_x), d_ve=st_d_ve,
                 d_xn=lambda c: normalise(c, rows(XN, c), rows(X, c), d_rs, d_xn), d_ve2=st_d_ve2, d_nt=st_d_nt, d_x1=st_d_x1,
                 d_ve3=st_d_ve3, d_n2t=lambda c: normalise(c, rows(XN, c), rows(XN, c), d_rs3, d_n2t, rms=True),
                 d_u=st_d_u, d_x=lambda c: add_x(c, BK["d_bk"], d_bk, d_x), e_ve=st_e_ve,
                 e_xn=lambda c: normalise(c, rows(XN, c), rows(X, c), e_rs, e_xn), e_ve2=st_e_ve2,
                 e_n1=lambda c: normalise(c, rows(XN, c), rows(HT, c), e_rs2, e_n1), e_dd=st_e_dd, e_ao=st_e_ao, e_h1=st_e_h1,
                 e_n2=lambda c: normalise(c, rows(XN, c), rows(HT, c), e_rs3, e_n2), e_hl=st_e_hl)

            top_two(BK["e_lg"], e_lg, e_d, e_ee)
            def by_expert(a):
                return a.rearrange("p t e -> p e t")

            link(V.tensor_tensor(CSO[:, :, :], by_expert(EQ1[:, :, :]), by_expert(EQ2[:, :, :]), ALU.add))
            flat = "p e t -> p (e t)"
            link(V.tensor_tensor_scan(CS[:, :, :].rearrange(flat), D0[:, :, :].rearrange(flat), CSO[:, :, :].rearrange(flat), 0.0,
                                      ALU.mult, ALU.add))
            V.tensor_tensor(CS[:, :, :], CS[:, :, :], CSO[:, :, :], ALU.subtract).then_inc(e_cs, 1)
            link(V.tensor_tensor(RV[:, 0, :], M8[:, :, 0], M8[:, :, 1], ALU.add))
            link(V.reciprocal(RV[:, 1, :], RV[:, 0, :]))
            link(V.tensor_tensor(RV[:, 2, :], M8[:, :, 0], RV[:, 1, :], ALU.mult))
            link(V.tensor_tensor(RV[:, 3, :], M8[:, :, 1], RV[:, 1, :], ALU.mult))
            link(weigh(RV[:, 2, :], RV[:, 3, :]))
            dve.wait_ge(e_cn, 1)
            link(V.tensor_scalar(CS[:, :, :], PS[:, 7, 0:NE * NT].rearrange("p (e t) -> p e t", t=NT), CAP, None, ALU.is_lt))
            V.tensor_tensor(GA[:, :, :], GA[:, :, :], CS[:, :, :].rearrange("p e t -> p t e"), ALU.mult).then_inc(e_g, 1)

            HB1, HI1, OB1 = NJ0 * NC * (1 + NE), NJ0 // 2 * NC * (1 + NE), NC * (1 + NE)
            dve.wait_ge(e_h1, NC)
            dve.wait_ge(e_ao, NC)
            dve.wait_ge(e_hl, NC)
            rests(HB1, HI1, OB1, NJ1, 0)
            for k in range(1, 2 * NC):
                rests(HB1 + NJ1 * k, HI1 + NJ1 // 2 * k, OB1 + k, NJ1, k % 2)
                gate(OB1 + k - 1, (k - 1) % 2)
            with dve.Fori(1, NE // 2) as i:
                for n in range(2 * NC):
                    hb, ob = HB1 + 2 * NC * NJ1 * i + NJ1 * n, OB1 + 2 * NC * i + n
                    rests(hb, HI1 + NC * NJ1 * i + NJ1 // 2 * n, ob, NJ1, n % 2)
                    gate(ob - 1, (n + 1) % 2)
            gate(OB1 + NC * NE - 1, 1)

            for c in range(NC):
                dve.wait_ge(e_bk, c + 1)
                t = slice(TPC * c, TPC * (c + 1))
                h = HT[:, t, :].rearrange("p t d -> p (t d)")
                link(V.tensor_tensor(h, h, PS[:, 6 + c % 2, :], ALU.add))
                link(V.tensor_tensor(HT[:, t, :], HT[:, t, :], MODR[:, c // CPB, GB:GB + 1, :].to_broadcast([P, TPC, D]), ALU.mult))
                V.tensor_tensor(X[:, t, :], X[:, t, :], HT[:, t, :], ALU.add).then_inc(e_o, 1)


_OUTS = [((2, 1024, 128), "float32")]


def kernel(**inputs):
    import numpy as _np
    import concourse.bacc as _bacc
    from concourse import mybir as _mybir
    from concourse.bass_utils import run_bass_kernel_spmd as _run

    nc = _bacc.Bacc("TRN2", target_bir_lowering=False, num_devices=1)
    arrays, aps = {}, {}
    for name in inputs:
        a = _np.ascontiguousarray(inputs[name])
        if name == "L0_attn_res_logit":
            a = a.reshape(1, 1)
        arrays[f"in_{name}_dram"] = a
        aps[name] = nc.dram_tensor(f"in_{name}_dram", a.shape, _mybir.dt.from_np(a.dtype), kind="ExternalInput").ap()
    shape, dtype = _OUTS[0]
    out = nc.dram_tensor("out_0_dram", shape, _mybir.dt.from_np(_np.dtype(dtype)), kind="ExternalOutput").ap()
    adaln_two_layers(nc, aps, out)
    r = _run(nc, [arrays], core_ids=[0])
    return r.results[0]["out_0_dram"]
```

```python
from contextlib import ExitStack

import numpy as np

import concourse.bass as bass
from concourse import mybir

F32 = mybir.dt.float32
F32R = mybir.dt.float32r
I32 = mybir.dt.int32
U32 = mybir.dt.uint32
ALU = mybir.AluOpType
ACT = mybir.ActivationFunctionType
AX = mybir.AxisListType

P = 128
CH = 512
TPC = CH // P
RING = 6
LAG = 4


def two_part(value, bits=12):
    high = np.float32(value)
    high = (high.view(np.uint32) & np.uint32(0xFFFFFFFF << (24 - bits) & 0xFFFFFFFF)).view(np.float32)
    return float(high), float(value - float(high))


def adaln_two_layers(nc, A, out):
    B, L, D = A["L0_attn_x3d"].shape
    NS = A["L0_attn_B_re"].shape[0]
    HID = A["L0_attn_W1"].shape[1]
    NJ0 = HID // P
    NE = A["L0_ffn_We1"].shape[0]
    NR = A["L0_ffn_Wr1"].shape[1]
    NJ1 = A["L1_ffn_moe_w1"].shape[2] // P
    NF = A["L1_attn_ff_fc_w"].shape[0] // P
    QKV = A["L1_ffn_qkv_weight"].shape[0]
    T = B * L
    NT = T // P
    NC = T // CH
    CPB = NC // B
    NKV, NH = 4, 16
    HD = D // NH
    QPK = NH // NKV
    GW = (QPK + 2) * HD
    CAP = float(-(-T * 2 * 5 // (NE * 4)))
    assert D == P and 4 * NS == P and NE == 8 and CPB == 2 and B == 2 and NJ0 == 4 and NJ1 == 2 and NF == 2

    x_rows = A["L0_attn_x3d"].rearrange("b (t p) d -> p (b t) d", p=P)
    out_rows = out.rearrange("b (t p) d -> p (b t) d", p=P)

    def column(name):
        return A[name].rearrange("(p a) -> p a", a=1)

    with ExitStack() as ctx:
        def sb(name, shape, dt=F32):
            return ctx.enter_context(nc.sbuf_tensor(name, shape, dt))

        def sems(names):
            return [ctx.enter_context(nc.semaphore(n)) for n in names.split()]

        X = sb("X", [P, NT, D])
        HT = sb("HT", [P, NT, D])
        Hh = sb("Hh", [P, T], F32R)
        Hl = sb("Hl", [P, T], F32R)
        ACC = sb("ACC", [P, T])
        GT = sb("GT", [P, T])
        MODR = sb("MODR", [P, B, 6, D])
        XN = sb("XN", [P, 2 * TPC, D])
        H = sb("H", [P, 2, CH])

        WRAW = [[sb(f"wraw{n}_{s}", [P, HID]) for s in range(2)] for n in (1, 2)]
        W1h, W1l, W2h, W2l = ([sb(f"{n}_{s}", [P, NJ0, P], F32R) for s in range(2)] for n in ("w1h", "w1l", "w2h", "w2l"))
        AH = sb("AH", [P, RING, CH], F32R)
        AL = sb("AL", [P, RING, CH], F32R)

        def cut(region, at, n):
            return region[:, at:at + n]

        RM = sb("RM", [P, 6144])
        A32 = cut(RM, 0, NJ0 * CH).rearrange("p (j n) -> p j n", j=NJ0)
        WB = [cut(RM, 2048 + CH * n, CH) for n in range(2)]
        MG = [cut(RM, 3072 + CH * n, CH) for n in range(2)]
        GR = cut(RM, 4096, 4 * CH).rearrange("p (g n) -> p g n", g=2)
        WMOD = [cut(RM, 6 * D * n, 6 * D) for n in range(2)]
        TR = cut(RM, 2048, 11 * P).rearrange("p (a b) -> p a b", b=P)

        RB = sb("RB", [P, 10752])
        TIN, TC, TS, Q = (cut(RB, L * n, L if n < 3 else CH) for n in range(4))
        Y = [cut(RB, 3584 + CH * p, CH) for p in range(2)]
        U = [cut(RB, 4608 + CH * p, CH) for p in range(2)]
        G0 = [cut(RB, 5632 + NJ0 * CH * p, NJ0 * CH).rearrange("p (j n) -> p j n", j=NJ0) for p in range(2)]
        WC, WS = ([G0[p][:, n, :] for p in range(2)] for n in range(2))
        T2 = Y
        QV = cut(RB, 0, NT * QKV).rearrange("p (t n) -> p t n", n=QKV)
        NFM, HS, X1, N2 = ([cut(RB, 3072 + 2 * CH * k + CH * p, CH) for p in range(2)] for k in range(4))
        G1 = [cut(RB, 7168 + NF * CH * p, NF * CH).rearrange("p (j n) -> p j n", j=NF) for p in range(2)]
        PR = cut(RB, 9216, 2 * CH)
        SK = cut(RB, 10240, CH)
        U2, AOT = N2, NFM
        TE = [G1[p][:, 0, :] for p in range(2)]
        AO = [G1[p][:, 0, :] for p in range(2)]

        LW1 = sb("LW1", [P, HID])
        LW2 = sb("LW2", [P, NJ0, D])
        TW = sb("TW", [P, 11, P])
        CT = sb("CT", [P, 2, B])
        SC = sb("SC", [P, 2, B])
        SCB = sb("SCB", [P, B, P])
        MF = sb("MF", [P, 2, 6, B])
        ID = sb("ID", [P, P])
        UT = sb("UT", [P, P])
        ON = sb("ON", [P, P])
        WR1 = sb("WR1", [P, NR])
        WR2 = sb("WR2", [NR + 1, NE])
        RT = sb("RT", [P, NE])
        BR1 = sb("BR1", [NR, 1])
        B1 = sb("B1", [P, 1 + NE, NJ0])
        BE2 = sb("BE2", [NE, D])
        COL = sb("COL", [P, 12])
        EX = sb("EX", [P, 3])
        SM = sb("SM", [P, 24])
        ST = sb("ST", [P, NT, 6])
        MV = sb("MV", [P, NT, 2])
        VE = sb("VE", [P, NT])
        RS = sb("RS", [P, NT])
        MH = sb("MH", [P, NT])
        EQ1 = sb("EQ1", [P, NT, NE])
        EQ2 = sb("EQ2", [P, NT, NE])
        GA = sb("GA", [P, NT, NE])
        PG = sb("PG", [P, NT, NE])
        M8 = sb("M8", [P, NT, NE])
        I8 = sb("I8", [P, NT, NE], U32)
        IF = sb("IF", [P, NT, 2])
        IO = sb("IO", [P, NT, NE])
        RV = sb("RV", [P, 6, NT])
        SP2 = sb("SP2", [P, 2 * 6, TPC * NH])
        CS = sb("CS", [P, NT, NE])
        CSO = sb("CSO", [P, NT, NE])
        KEEP = sb("KEEP", [P, NT, NE])
        DEC = sb("DEC", [P, 3])
        EK = sb("EK", [P, 3])
        EF = sb("EF", [P, 3])
        EQ = sb("EQ", [P, 3])
        EI = sb("EI", [P, 3], I32)
        SG = sb("SG", [P, 3])
        GTMP = sb("GTMP", [P, 2, 2, B])
        CTMP = sb("CTMP", [P, B, D])

        PS = ctx.enter_context(nc.psum_tensor("PS", [P, 8, CH], F32))

        SIG = 21
        NU, TH, AL_, CO, DS, FNW, INW, L1W, L1B, L2W, L2B, BS2 = range(12)
        T_BW, T_M1, T_M2, T_D, T_F0, T_F1, T_P0, T_P1, T_Q0, T_Q1, T_PJ = range(11)
        SA, CA, GAT, SBT, CB, GB = range(6)

        (x_in0, x_in1, col_in, tr_in, tr2_in, mod_in, lru_in, small_in, raw_in0, raw_in1, out_in) = sems(
            "x_in0 x_in1 col_in tr_in tr2_in mod_in lru_in small_in raw_in0 raw_in1 out_in")
        raw_in = [raw_in0, raw_in1]
        gr_in = sems("gr_in0 gr_in1 gr_in2 gr_in3")
        (const, dch, pch, sc_done, modps, mod_done, modr_done, scb_done, gam_in, gam, trig_in, trig, turned, tw_done, tw2_done, modr_cp) = sems(
            "const dch pch sc_done modps mod_done modr_done scb_done gam_in gam trig_in trig turned tw_done tw2_done modr_cp")
        (a_ve, a_rs, a_xn, a_tp, a_h, a_bu, a_u, a_wc, a_ws, a_y, a_yc, a_hid0, a_hid1, a_gel0, a_gel1, a_z, a_t, a_bk, a_x) = sems(
            "a_ve a_rs a_xn a_tp a_h a_bu a_u a_wc a_ws a_y a_yc a_hid0 a_hid1 a_gel0 a_gel1 a_z a_t a_bk a_x")
        (b_ve, b_rs, b_xn, b_tp, b_h, b_hh, b_hl, b_r1, b_rl, b_lg, b_d, b_e, b_t2, b_e2, b_g, b_gt, b_gtc) = sems(
            "b_ve b_rs b_xn b_tp b_h b_hh b_hl b_r1 b_rl b_lg b_d b_e b_t2 b_e2 b_g b_gt b_gtc")
        (w_hi, w_split, m_hid, m_act, m_hi, m_lo, m_out, m_gated, m_wb, m_acc, m_accv) = sems(
            "w_hi w_split m_hid m_act m_hi m_lo m_out m_gated m_wb m_acc m_accv")
        (c_be, c_t, c_bk, c_x) = sems("c_be c_t c_bk c_x")
        (d_ve, d_rs, d_xn, d_ht, d_ve2, d_rs2, d_nt, d_tp, d_nf, d_hs, d_x1, d_tp2, d_x1t, d_ve3, d_rs3, d_n2t, d_tp3, d_n2, d_fc,
         d_g, d_pj, d_u, d_bk, d_x) = sems(
            "d_ve d_rs d_xn d_ht d_ve2 d_rs2 d_nt d_tp d_nf d_hs d_x1 d_tp2 d_x1t d_ve3 d_rs3 d_n2t d_tp3 d_n2 d_fc d_g d_pj "
            "d_u d_bk d_x")
        (e_ve, e_rs, e_xn, e_mod, e_ve2, e_rs2, e_n1, e_tp, e_l1, e_qk, e_qv, e_dd, e_e, e_ao, e_at, e_aot, e_pj, e_h1, e_ve3,
         e_rs3, e_n2, e_tp2, e_l2, e_hh, e_hl, e_lg, e_d, e_ee, e_cs, e_cn, e_g, e_gt, e_gtc, f_bk, f_o) = sems(
            "e_ve e_rs e_xn e_mod e_ve2 e_rs2 e_n1 e_tp e_l1 e_qk e_qv e_dd e_e e_ao e_at e_aot e_pj e_h1 e_ve3 "
            "e_rs3 e_n2 e_tp2 e_l2 e_hh e_hl e_lg e_d e_ee e_cs e_cn e_g e_gt e_gtc f_bk f_o")

        def tiles(c):
            return range(TPC * c, TPC * (c + 1))

        def tsl(c):
            return slice(TPC * c, TPC * (c + 1))

        def tk(c):
            return slice(CH * c, CH * (c + 1))

        def bx(c):
            return 4 + 2 * (c % 2)

        def by(c):
            return 5 + 2 * (c % 2)

        def hc(c):
            return H[:, c % 2, :]

        def xn(c, n):
            return XN[:, TPC * (c % 2) + n, :]

        class Step:
            pass

        steps, blocks, experts = [], [], []
        for layer in range(2):
            for g in range(NC // 2):
                for e in range(-1 if layer == 0 else 0, NE):
                    ex = Step()
                    ex.layer, ex.e, ex.nj, ex.q, ex.start = layer, e, (NJ0, NJ1)[layer], len(experts), len(blocks)
                    ex.slot = ex.q % 2
                    ex.at = 0 if layer == 0 else NJ1 * (ex.q // 2 % 2)
                    n0 = 2 * (1 + NE)
                    ex.before = ex.q - 2 if ex.q < n0 + 2 else ex.q - 4
                    experts.append(ex)
                    for c in (2 * g, 2 * g + 1):
                        st = Step()
                        st.ex, st.c, st.k, st.g = ex, c, len(steps), 2 * layer + g
                        st.first_of_sum = e == (-1 if layer == 0 else 0)
                        st.own_vector = layer == 1 and c % 2 == 1 and not st.first_of_sum
                        steps.append(st)
                        for j in range(ex.nj):
                            blocks.append((st, j))
                        st.last = len(blocks) - 1
                    ex.last = len(blocks) - 1
        NU_ = len(blocks)

        def at_most(k, test):
            return sum(1 for s in steps[:k + 1] if test(s))

        def spreads(k):
            return at_most(k, lambda s: s.ex.e >= 0)

        def pool_sums(k):
            return at_most(k, lambda s: not s.first_of_sum and not s.own_vector)

        def vector_sums(k):
            return at_most(k, lambda s: s.own_vector)

        def wait_sum(eng, k):
            if steps[k].first_of_sum:
                eng.wait_ge(m_gated, k + 1)
            elif steps[k].own_vector:
                eng.wait_ge(m_accv, vector_sums(k))
            else:
                eng.wait_ge(m_acc, pool_sums(k))

        last_step = [[max(s.k for s in steps if s.ex.layer == n and s.c == c) for c in range(NC)] for n in range(2)]
        gates = {s.last + LAG: s for s in steps}
        spreading = {s.last + LAG - 1: s for s in steps if s.ex.e >= 0}
        sums = {s.last + LAG + 1: s for s in steps if not s.first_of_sum}
        splitting, u = {}, -1
        for ex in experts[2:]:
            u = max(ex.start - 5, experts[ex.before].last + LAG + 1, u + 1)
            assert u <= ex.start
            splitting[u] = ex

        COST = dict(a_ve=1.4, a_u=1.5, a_ws=1.3, a_y=2.6, a_yc=0.6, a_hid0=1.7, a_hid1=1.7, a_gel0=1.1, a_gel1=1.1, a_z=3.4, a_t=1.2,
                    a_x=0.6, b_ve=1.4, b_h=1.3, b_hl=0.6, b_r1=0.6, b_rl=0.6, b_lg=0.5, b_d=0.5, b_e=1.7, b_t2=2.5, b_e2=0.4, b_g=0.7,
                    b_gt=0.4, b_gtc=0.6, c_t=1.2, c_x=0.6, d_ve=1.4, d_ht=2.5, d_ve2=1.5, d_tp=2.0, d_nf=0.6, d_x1=2.0, d_x1t=0.6,
                    d_ve3=1.5, d_n2=0.6, d_fc=1.7, d_g=1.1, d_pj=1.7, d_u=1.2, d_x=0.6, e_ve=1.4, e_mod=2.5, e_ve2=1.4, e_l1=0.7,
                    e_qk=1.5, e_qv=0.8, e_dd=5.0, e_e=0.5, e_ao=4.0, e_aot=0.6, e_pj=1.4, e_h1=2.0, e_l2=1.3, e_hl=0.6, e_lg=0.5,
                    e_d=0.5, e_ee=1.7, e_cs=4.5, e_cn=0.4, e_g=0.4, e_gt=0.4, e_gtc=0.6)
        ROUTE0 = "b_d b_e b_t2 b_e2 b_g b_gt b_gtc".split()
        A_ORDER = ("a_ve a_rs a_xn a_tp a_h a_bu a_u a_ws a_y a_yc a_hid0 a_gel0 a_hid1 a_gel1 a_z a_t a_bk a_x "
                   "b_ve b_rs b_xn b_tp b_h b_hl b_r1 b_rl b_lg").split()
        B_ORDER = ("c_be c_t c_bk c_x "
                   "d_ve d_rs d_xn d_ht d_ve2 d_rs2 d_nt d_tp d_nf d_x1 d_tp2 d_x1t d_ve3 d_rs3 d_n2t d_tp3 d_n2 d_fc d_g d_pj d_u d_bk d_x "
                   "e_ve e_rs e_xn e_mod e_ve2 e_rs2 e_n1 e_tp e_l1 e_qk e_qv e_dd e_e e_ao e_at e_aot e_pj e_h1 e_rs3 e_n2 e_tp2 "
                   "e_l2 e_hl e_lg e_d e_ee e_cs e_cn e_g e_gt e_gtc").split()
        when, unit_at = {}, []

        def lay(order, c, start, slack):
            for name in order:
                when[name, c] = start
                start += COST.get(name, 1.0) + slack
            return start

        def place(lo, hi, start, pace):
            for u in range(lo, hi):
                st, j = blocks[u]
                if st.first_of_sum and j == 0:
                    start = max(start, when["b_hl" if st.ex.layer == 0 else "e_hl", st.c] + 0.8)
                unit_at.append(start)
                start += pace
            return start

        S1, S2, S3, S4 = (min(s.ex.start for s in steps if s.g == n) for n in range(4))
        PACE = 1.4
        ends = [lay(A_ORDER, c, 1.5 * c, 0.2) for c in range(2)]
        for n, name in enumerate(("mod_turn", "mod_tw", "mod_mm", "mod_cp", "mod_rows", "split01")):
            when[name, 0] = when["a_hid0", 0] + 2.0 * n
        for c in range(2):
            ends[c] = lay(ROUTE0, c, ends[c], 0.3)
        end = [lay(A_ORDER + ROUTE0, c, ends[0] - 4.0 + 1.5 * (c - 2), 0.3) for c in (2, 3)]
        t = place(S1, S2, when["b_hl", 0] + 0.8, max(PACE, (when["b_hl", 2] - when["b_hl", 0]) / (S2 - S1)))
        for lo, hi, c0 in ((S2, S3, 0), (S3, S4, 2)):
            t = place(lo, lo + LAG + 2, t, PACE)
            for c in (c0, c0 + 1):
                lay(B_ORDER, c, unit_at[steps[last_step[0][c]].last + LAG + 1] + 3.0, 0.3)
            until = when["e_hl", 0] if c0 == 0 else when["e_g", 3]
            t = place(lo + LAG + 2, hi, t, max(PACE, (until - t) / (hi - lo - LAG - 2)))
        place(S4, NU_, t, PACE)
        unit_at += [unit_at[-1] + PACE * (n + 1) for n in range(LAG + 3)]
        for c in range(NC):
            lay(["f_bk", "f_o"], c, unit_at[steps[last_step[1][c]].last + LAG + 1] + 3.5, 0.5)

        def run(skew, unit, **mine):
            order = [(unit_at[u] + skew, "unit", u) for u in range(len(unit_at))]
            order += [(t, name, c) for (name, c), t in when.items() if name in mine]
            for _, name, n in sorted(order, key=lambda item: item[0]):
                if name == "unit":
                    unit(n)
                else:
                    mine[name](n)

        block = ctx.enter_context(nc.Block())

        @block.sync
        def _(sp):
            def load(dst, src, sem):
                sp.dma_start(dst, src).then_inc(sem, 16)

            with nc.allow_non_contiguous_dma(reason="small parameters"):
                for c in range(2):
                    load(X[:, tsl(c), :], x_rows[:, tsl(c), :], x_in0)
                for g in range(4):
                    load(COL[NS * g:NS * (g + 1), NU:NU + 1], column("L0_attn_nu_log"), col_in)
                    load(COL[NS * g:NS * (g + 1), TH:TH + 1], column("L0_attn_theta_log"), col_in)
                load(COL[:, AL_:AL_ + 1], column("L1_attn_a_log"), col_in)
                for n in range(2):
                    load(CT[:, n, :], A[f"L{n}_c"].rearrange("b d -> d b"), mod_in)
                    load(WMOD[n], A[f"L{n}_wmod"], mod_in)
                for g, n in enumerate(["L0_attn_B_re", "L0_attn_B_im", "L0_attn_B_im", "L0_attn_B_re"]):
                    load(TR[NS * g:NS * (g + 1), 0, :], A[n], tr_in)
                for g, (n, m) in enumerate([("L0_attn_C_re", "L0_attn_C_im"), ("L0_attn_C_im", "L0_attn_C_re")] * 2):
                    load(TR[:, 1, NS * g:NS * (g + 1)], A[n], tr_in)
                    load(TR[:, 2, NS * g:NS * (g + 1)], A[m], tr_in)
                load(TR[:, 3, :], A["L0_attn_D_mat"], tr_in)
                load(LW1[:, :], A["L0_attn_W1"], lru_in)
                load(LW2[:, :, :], A["L0_attn_W2"].rearrange("(j p) n -> p j n", p=P), lru_in)
                load(SM[:, 20:21], A["L0_attn_res_logit"].to_broadcast([P, 1]), small_in)
                for k, n in ((CO, "L1_attn_c_out"), (DS, "L1_attn_d_skip"), (FNW, "L1_attn_ff_norm_w"),
                             (INW, "L1_attn_input_norm_w"), (L1W, "L1_ffn_ln1_weight"), (L1B, "L1_ffn_ln1_bias"),
                             (L2W, "L1_ffn_ln2_weight"), (L2B, "L1_ffn_ln2_bias"), (BS2, "L0_ffn_bs2")):
                    load(COL[:, k:k + 1], column(n), small_in)
                load(WR1[:, :], A["L0_ffn_Wr1"], small_in)
                load(WR2[0:NR, :], A["L0_ffn_Wr2"], small_in)
                load(WR2[NR:NR + 1, :], A["L0_ffn_br2"].rearrange("(a n) -> a n", a=1), small_in)
                load(BR1[:, :], column("L0_ffn_br1"), small_in)
                load(B1[:, 0, :], A["L0_ffn_bs1"].rearrange("(p j) -> p j", j=NJ0), small_in)
                load(B1[:, 1:1 + NE, :], A["L0_ffn_be1"].rearrange("e (p j) -> p e j", j=NJ0), small_in)
                load(BE2[:, :], A["L0_ffn_be2"], small_in)
                load(RT[:, :], A["L1_ffn_router_weight"], small_in)
                for c in range(2, NC):
                    load(X[:, tsl(c), :], x_rows[:, tsl(c), :], x_in1)
                load(TR[:, 4:6, :], A["L1_attn_ff_fc_w"].rearrange("(j p) n -> p j n", p=P), tr2_in)
                load(TR[:, 6:8, :], A["L1_attn_ff_proj_w"].rearrange("o (j n) -> o j n", j=NF), tr2_in)
                load(TR[:, 8, :], A["L1_ffn_qkv_weight"][0:P, :], tr2_in)
                load(TR[0:QKV - P, 9, :], A["L1_ffn_qkv_weight"][P:QKV, :], tr2_in)
                load(TR[:, 10, :], A["L1_ffn_proj_weight"], tr2_in)

            def raw(ex):
                s = ex.q % 2
                if ex.q >= 2:
                    sp.wait_ge(w_split, ex.q - 1)
                if ex.e < 0:
                    w1, w2 = A["L0_ffn_Ws1"], A["L0_ffn_Ws2"]
                elif ex.layer == 0:
                    w1, w2 = A["L0_ffn_We1"][ex.e], A["L0_ffn_We2"][ex.e]
                else:
                    w1, w2 = A["L1_ffn_moe_w1"][ex.e], A["L1_ffn_moe_w2"][ex.e]
                load(WRAW[0][s][:, 0:ex.nj * P], w1, raw_in[s])
                load(WRAW[1][s][:, 0:ex.nj * P], w2.rearrange("(p j) n -> p (j n)", j=ex.nj), raw_in[s])

            def rows(g):
                for c in (2 * (g % 2), 2 * (g % 2) + 1):
                    sp.wait_ge(b_gtc if g < 2 else e_gtc, c + 1)
                    if g >= 1 and c % 2 == 0:
                        sp.wait_ge(m_wb, spreads(max(s.k for s in steps if s.g == g - 1)))
                    for h in range(NE // 4):
                        load(GR[0:P:32, h, tk(c % 2)], GT[4 * h:4 * h + 4, tk(c)], gr_in[g])

            rows_after = {min(ex.q for ex in experts if ex.start == s) + (3 if n == 0 else 2): n for n, s in enumerate((S1, S2, S3, S4))}
            for ex in experts:
                raw(ex)
                if ex.q in rows_after:
                    rows(rows_after[ex.q])
            for c in range(NC):
                sp.wait_ge(f_o, c + 1)
                sp.dma_start(out_rows[:, tsl(c), :], X[:, tsl(c), :]).then_inc(out_in, 16)
            sp.wait_ge(out_in, 16 * NC)

        @block.gpsimd
        def _(pool):
            linked = [0]
            newest = [None]

            def note(ins, sem, count):
                ins.then_inc(sem, 1)
                newest[0] = (sem, count)

            def link(ins):
                linked[0] += 1
                note(ins, pch, linked[0])
                pool.wait_ge(pch, linked[0])

            nc.gpsimd.memset(MH[:, :], -0.5)
            nc.gpsimd.memset(ID[:, :], 0.0)
            link(nc.gpsimd.memset(ON[:, :], 1.0))
            nc.gpsimd.affine_select(out=ID[:, :], in_=ID[:, :], compare_op=ALU.not_equal, fill=1.0, base=0,
                                    pattern=[[-1, P]], channel_multiplier=1).then_inc(const, 1)

            def root(ve, rs, c):
                pool.wait_ge(ve, c + 1)
                note(nc.gpsimd.tensor_tensor(RS[:, tsl(c)], VE[:, tsl(c)], MH[:, tsl(c)], ALU.pow), rs, c + 1)

            for c in range(2):
                root(a_ve, a_rs, c)
            nc.gpsimd.affine_select(out=UT[:, :], in_=ON[:, :], compare_op=ALU.is_gt, fill=0.0, base=0,
                                    pattern=[[1, P]], channel_multiplier=-1).then_inc(const, 1)
            nc.gpsimd.iota(IO[:, :, :], [[0, NT], [1, NE]], base=0, channel_multiplier=0,
                           allow_small_or_imprecise_dtypes=True).then_inc(const, 1)
            pool.wait_ge(gam_in, 1)
            nc.gpsimd.tensor_tensor(SM[:, 19:20], SM[:, 18:19], SM[:, 22:23], ALU.pow).then_inc(gam, 1)

            def a_out_sin(c):
                pool.wait_ge(a_u, c + 1)
                if c >= 2:
                    pool.wait_ge(a_z, c - 1)
                note(nc.gpsimd.tensor_tensor(WS[c % 2], TS[:, tk(c % CPB)], U[c % 2], ALU.mult), a_ws, c + 1)

            def rests_of(ex):
                s, at = ex.slot, slice(ex.at, ex.at + ex.nj)
                r1 = WRAW[0][ex.q % 2][:, 0:ex.nj * P].rearrange("p (m j) -> p j m", j=ex.nj)
                r2 = WRAW[1][ex.q % 2][:, 0:ex.nj * P].rearrange("p (j m) -> p j m", j=ex.nj)
                pool.wait_ge(w_hi, 2 * ex.q + 1)
                nc.gpsimd.tensor_tensor(W1l[s][:, at, :], r1, W1h[s][:, at, :].bitcast(F32), ALU.subtract)
                pool.wait_ge(w_hi, 2 * ex.q + 2)
                note(nc.gpsimd.tensor_tensor(W2l[s][:, at, :], r2, W2h[s][:, at, :].bitcast(F32), ALU.subtract),
                     w_split, ex.q + 1)

            def spread(st):
                if st.k >= 2:
                    pool.wait_ge(m_gated, st.k - 1)
                pool.wait_ge(gr_in[st.g], 2 * 16 * (NE // 4))
                pool.wait_ge(*newest[0])
                e = st.ex.e
                note(nc.gpsimd.partition_broadcast(WB[st.k % 2], GR[32 * (e % 4):32 * (e % 4) + 1, e // 4, tk(st.c % 2)]),
                     m_wb, spreads(st.k))
                pool.wait_ge(m_wb, spreads(st.k))

            def unit(u):
                if u in splitting:
                    rests_of(splitting[u])
                if u in sums and not sums[u].own_vector:
                    st = sums[u]
                    pool.wait_ge(m_gated, st.k + 1)
                    wait_sum(pool, st.k - 2)
                    note(nc.gpsimd.tensor_tensor(ACC[:, tk(st.c)], ACC[:, tk(st.c)], MG[st.k % 2], ALU.add), m_acc, pool_sums(st.k))
                if u in spreading:
                    spread(spreading[u])

            def modulate(xn_sem, mod, c, shift, scale):
                pool.wait_ge(xn_sem, c + 1)
                if c == 0:
                    pool.wait_ge(modr_done, 1)
                b = c // CPB
                link(nc.gpsimd.tensor_tensor(HT[:, tsl(c), :], XN[:, tsl(c % 2), :],
                                             MODR[:, b, scale:scale + 1, :].to_broadcast([P, TPC, D]), ALU.mult))
                note(nc.gpsimd.tensor_tensor(HT[:, tsl(c), :], HT[:, tsl(c), :],
                                             MODR[:, b, shift:shift + 1, :].to_broadcast([P, TPC, D]), ALU.add), mod, c + 1)

            run(3.4, unit, a_rs=lambda c: root(a_ve, a_rs, c) if c >= 2 else None, a_ws=a_out_sin,
                b_rs=lambda c: root(b_ve, b_rs, c),
                split01=lambda _: [rests_of(experts[q]) for q in range(2)],
                d_rs=lambda c: root(d_ve, d_rs, c), d_ht=lambda c: modulate(d_xn, d_ht, c, SA, CA),
                d_rs2=lambda c: root(d_ve2, d_rs2, c), d_rs3=lambda c: root(d_ve3, d_rs3, c),
                e_rs=lambda c: root(e_ve, e_rs, c), e_mod=lambda c: modulate(e_xn, e_mod, c, SBT, CB),
                e_rs2=lambda c: root(e_ve2, e_rs2, c), e_rs3=lambda c: root(e_ve3, e_rs3, c))

        @block.scalar
        def _(act):
            act.wait_ge(mod_in, 64)
            nc.scalar.activation(SC[:, :, :], CT[:, :, :], ACT.Silu).then_inc(sc_done, 1)
            act.wait_ge(trig_in, 1)
            nc.scalar.activation(SM[:, 10:12], SM[:, 8:10], ACT.Sin).then_inc(trig, 1)
            act.wait_ge(small_in, 16 * 18)
            nc.scalar.activation(SM[:, SIG:SIG + 1], SM[:, 20:21], ACT.Tanh, scale=0.5).then_inc(trig, 1)

            def evacuate(tp, out_sem, c, dst, bank, scale, bias=0.0):
                act.wait_ge(tp, c + 1)
                nc.scalar.activation(dst, PS[:, bank, :], ACT.Identity, scale=scale, bias=bias).then_inc(out_sem, 1)

            def st_a_h(c):
                if c == 0:
                    act.wait_ge(mod_done, 1)
                b = c // CPB
                evacuate(a_tp, a_h, c, hc(c), bx(c), MF[:, 0, CA, b:b + 1], MF[:, 0, SA, b:b + 1])

            def st_a_yc(c):
                act.wait_ge(a_y, c + 1)
                nc.scalar.activation(Y[c % 2], PS[:, bx(c), :], ACT.Copy).then_inc(a_yc, 1)

            def st_a_gel(c, half):
                for j in (2 * half, 2 * half + 1):
                    act.wait_ge(a_hid1 if half else a_hid0, 2 * c + j % 2 + 1)
                    nc.scalar.activation(G0[c % 2][:, j, :], PS[:, bx(c) + j % 2, :], ACT.Gelu_apprx_tanh)\
                        .then_inc(a_gel1 if half else a_gel0, 1)

            def st_b_h(c):
                b = c // CPB
                evacuate(b_tp, b_h, c, hc(c), bx(c), MF[:, 0, CB, b:b + 1], MF[:, 0, SBT, b:b + 1])
                nc.scalar.activation(Hh[:, tk(c)], PS[:, bx(c), :], ACT.Identity, scale=MF[:, 0, CB, b:b + 1],
                                     bias=MF[:, 0, SBT, b:b + 1]).then_inc(b_hh, 1)

            def st_b_rl(c):
                act.wait_ge(b_r1, c + 1)
                nc.scalar.activation(GT[0:NR, tk(c)], PS[0:NR, by(c), :], ACT.Relu, bias=BR1[:, :]).then_inc(b_rl, 1)

            def st_exp(d, e, c):
                act.wait_ge(d, c + 1)
                nc.scalar.activation(PG[:, tsl(c), :], GA[:, tsl(c), :], ACT.Exp).then_inc(e, 1)

            def st_b_e2(c):
                act.wait_ge(b_t2, c + 1)
                nc.scalar.activation(RV[:, 4, tsl(c)], RV[:, 3, tsl(c)], ACT.Tanh, scale=0.25).then_inc(b_e2, 1)

            def st_gtc(gt, gtc, c):
                act.wait_ge(gt, c + 1)
                nc.scalar.activation(GT[0:NE, tk(c)], PS[0:NE, gt_bank(gt, c), 0:CH], ACT.Copy).then_inc(gtc, 1)

            def gt_bank(gt, c):
                return by(c) if gt is b_gt else bx(c)

            def highs_of(ex):
                s, at = ex.slot, slice(ex.at, ex.at + ex.nj)
                r1 = WRAW[0][ex.q % 2][:, 0:ex.nj * P].rearrange("p (m j) -> p j m", j=ex.nj)
                r2 = WRAW[1][ex.q % 2][:, 0:ex.nj * P].rearrange("p (j m) -> p j m", j=ex.nj)
                act.wait_ge(raw_in[ex.q % 2], 32 * (ex.q // 2 + 1))
                if ex.before >= 0:
                    act.wait_ge(m_out, experts[ex.before].last + 1)
                nc.scalar.activation(W1h[s][:, at, :], r1, ACT.Copy).then_inc(w_hi, 1)
                nc.scalar.activation(W2h[s][:, at, :], r2, ACT.Copy).then_inc(w_hi, 1)

            def unit(u):
                if u in splitting:
                    highs_of(splitting[u])
                if u < NU_:
                    st, j = blocks[u]
                    act.wait_ge(m_hid, u + 1)
                    if u >= NJ0:
                        act.wait_ge(m_lo, u - NJ0 + 1)
                    if u == 0:
                        act.wait_ge(modps, 2)
                    if st.ex.layer == 0:
                        nc.scalar.activation(A32[:, u % NJ0, :], PS[:, u % 2, :], ACT.Silu,
                                             bias=B1[:, 1 + st.ex.e, j:j + 1]).then_inc(m_act, 1)
                    else:
                        nc.scalar.activation(A32[:, u % NJ0, :], PS[:, u % 2, :], ACT.Gelu_apprx_tanh).then_inc(m_act, 1)
                if 1 <= u <= NU_:
                    act.wait_ge(m_act, u)
                    if u - 1 >= RING:
                        act.wait_ge(m_out, u - RING)
                    nc.scalar.activation(AH[:, (u - 1) % RING, :], A32[:, (u - 1) % NJ0, :], ACT.Copy).then_inc(m_hi, 1)

            def st_mod_tw(_):
                act.wait_ge(turned, 2)
                nc.scalar.activation(TW[:, T_F0:T_F0 + 4, :].rearrange("p a b -> p (a b)"), PS[:, 1, :], ACT.Copy)
                act.wait_ge(turned, 3)
                nc.scalar.activation(TW[:, T_Q0:T_Q0 + 2, :].rearrange("p a b -> p (a b)")[:, 0:QKV], PS[:, 2, 0:QKV], ACT.Copy)
                nc.scalar.activation(TW[:, T_PJ, :], PS[:, 2, QKV:QKV + P], ACT.Copy).then_inc(tw2_done, 1)

            def st_mod_cp(_):
                act.wait_ge(modps, 2)
                for b in range(B):
                    for n in range(2):
                        last = nc.scalar.activation(MODR[:, b, 3 * n:3 * n + 3, :].rearrange("p a b -> p (a b)"),
                                                    PS[:, 2 * b + n, 0:3 * D], ACT.Copy)
                last.then_inc(modr_cp, 1)

            def st_d_g(c):
                for j in range(NF):
                    act.wait_ge(d_fc, NF * c + j + 1)
                    nc.scalar.activation(G1[c % 2][:, j, :], PS[:, bx(c) + j, :], ACT.Silu).then_inc(d_g, 1)

            def st_e_l1(c):
                evacuate(e_tp, e_l1, c, hc(c), bx(c), COL[:, L1W:L1W + 1], COL[:, L1B:L1B + 1])

            def st_e_qv(c):
                for n in range(TPC // 2):
                    act.wait_ge(e_qk, (TPC // 2) * c + n + 1)
                    t = TPC * c + 2 * n
                    nc.scalar.activation(QV[:, t:t + 2, :], PS[:, by(c) - n, 0:2 * QKV].rearrange("p (t n) -> p t n", t=2),
                                         ACT.Copy).then_inc(e_qv, 1)

            def st_e_e(c):
                if c >= CPB:
                    n = 6 * (c % 2)
                    act.wait_ge(e_dd, c - CPB + 1)
                    nc.scalar.activation(SP2[:, n + 5, :], SP2[:, n + 4, :], ACT.Tanh,
                                         scale=float(0.5 / np.sqrt(np.float32(HD)))).then_inc(e_e, 1)

            def st_e_l2(c):
                evacuate(e_tp2, e_l2, c, hc(c), by(c), COL[:, L2W:L2W + 1], COL[:, L2B:L2B + 1])
                nc.scalar.activation(Hh[:, tk(c)], PS[:, by(c), :], ACT.Identity, scale=COL[:, L2W:L2W + 1],
                                     bias=COL[:, L2B:L2B + 1]).then_inc(e_hh, 1)

            run(1.3, unit, a_h=st_a_h, a_yc=st_a_yc, a_gel0=lambda c: st_a_gel(c, 0), a_gel1=lambda c: st_a_gel(c, 1), b_h=st_b_h,
                b_rl=st_b_rl, b_e=lambda c: st_exp(b_d, b_e, c), b_e2=st_b_e2, b_gtc=lambda c: st_gtc(b_gt, b_gtc, c),
                split01=lambda _: [highs_of(experts[q]) for q in range(2)], mod_tw=st_mod_tw, mod_cp=st_mod_cp,
                d_nf=lambda c: evacuate(d_tp, d_nf, c, NFM[c % 2], by(c), COL[:, INW:INW + 1]),
                d_x1t=lambda c: evacuate(d_tp2, d_x1t, c, XN[:, tsl(c % 2), :].rearrange("p t d -> p (t d)"), bx(c), 1.0),
                d_n2=lambda c: evacuate(d_tp3, d_n2, c, N2[c % 2], by(c), COL[:, FNW:FNW + 1]),
                d_g=st_d_g, e_l1=st_e_l1, e_qv=st_e_qv, e_e=st_e_e,
                e_aot=lambda c: evacuate(e_at, e_aot, c, AOT[c % 2], by(c), 1.0),
                e_l2=st_e_l2, e_ee=lambda c: st_exp(e_d, e_ee, c), e_gtc=lambda c: st_gtc(e_gt, e_gtc, c))

        @block.tensor
        def _(pe):
            def mm(bank, lhsT, rhs, start=True, stop=True, rows=P, cols=slice(0, CH)):
                return nc.tensor.matmul(PS[0:rows, bank, cols], lhsT, rhs, start=start, stop=stop)

            def turn_tiles(bank, src, rows=P):
                for n in range(TPC):
                    last = nc.tensor.transpose(PS[0:rows, bank, n * P:(n + 1) * P], src(n), ID[:, :])
                return last

            pe.wait_ge(const, 1)
            pe.wait_ge(sc_done, 1)
            for n in range(2):
                for j in range(6):
                    at = (6 * n + j) * B
                    last = mm(3, WMOD[n][:, j * D:(j + 1) * D], SC[:, n, :], cols=slice(at, at + B))
            last.then_inc(modps, 1)
            pe.wait_ge(tr_in, 16 * 13)
            for n in range(4):
                last = nc.tensor.transpose(PS[:, 0, n * P:(n + 1) * P], TR[:, n, :], ID[:, :])
            last.then_inc(turned, 1)

            def st_mod_turn(_):
                pe.wait_ge(tr2_in, 16 * 5)
                for n in range(4, 8):
                    last = nc.tensor.transpose(PS[:, 1, (n - 4) * P:(n - 3) * P], TR[:, n, :], ID[:, :])
                last.then_inc(turned, 1)
                nc.tensor.transpose(PS[:, 2, 0:P], TR[:, 8, :], ID[:, :])
                nc.tensor.transpose(PS[:, 2, P:QKV], TR[0:QKV - P, 9, :], ID[0:QKV - P, 0:QKV - P])
                nc.tensor.transpose(PS[:, 2, QKV:QKV + P], TR[:, 10, :], ID[:, :]).then_inc(turned, 1)

            def st_mod_mm(_):
                pe.wait_ge(scb_done, 1)
                pe.wait_ge(mod_done, 1)
                pe.wait_ge(tw_done, 1)
                pe.wait_ge(tw2_done, 1)
                for b in range(B):
                    for n in range(2):
                        last = mm(2 * b + n, SCB[:, b, :], WMOD[1][:, n * 3 * D:(n + 1) * 3 * D], cols=slice(0, 3 * D))
                last.then_inc(modps, 1)

            def st_a_tp(c):
                pe.wait_ge(a_xn, c + 1)
                if c >= 2:
                    pe.wait_ge(b_gtc, c - 1)
                turn_tiles(bx(c), lambda n: xn(c, n)).then_inc(a_tp, 1)

            def st_a_bu(c):
                if c == 0:
                    pe.wait_ge(tw_done, 1)
                pe.wait_ge(a_h, c + 1)
                mm(by(c), TW[:, T_BW, :], hc(c)).then_inc(a_bu, 1)

            def st_a_y(c):
                pe.wait_ge(a_wc, c + 1)
                mm(bx(c), TW[:, T_D, :], hc(c), stop=False)
                mm(bx(c), TW[:, T_M1, :], WC[c % 2], start=False, stop=False)
                pe.wait_ge(a_ws, c + 1)
                mm(bx(c), TW[:, T_M2, :], WS[c % 2], start=False).then_inc(a_y, 1)

            def st_a_hid(c, half):
                if c == 0 and half == 0:
                    pe.wait_ge(lru_in, 32)
                pe.wait_ge(a_yc, c + 1)
                for j in (2 * half, 2 * half + 1):
                    if half == 1:
                        pe.wait_ge(a_gel0, 2 * c + j % 2 + 1)
                    mm(bx(c) + j % 2, LW1[:, j * P:(j + 1) * P], Y[c % 2]).then_inc(a_hid1 if half else a_hid0, 1)

            def st_a_z(c):
                pe.wait_ge(a_gel1, 2 * c + 2)
                for j in range(NJ0):
                    last = mm(bx(c), LW2[:, j, :], G0[c % 2][:, j, :], start=(j == 0), stop=(j == NJ0 - 1))
                last.then_inc(a_z, 1)

            def st_a_bk(c):
                pe.wait_ge(a_t, c + 1)
                turn_tiles(by(c), lambda n: T2[c % 2][:, n * P:(n + 1) * P]).then_inc(a_bk, 1)

            def st_b_tp(c):
                pe.wait_ge(b_xn, c + 1)
                turn_tiles(bx(c), lambda n: xn(c, n)).then_inc(b_tp, 1)

            def st_b_r1(c):
                if c == 0:
                    pe.wait_ge(small_in, 16 * 18)
                pe.wait_ge(b_h, c + 1)
                mm(by(c), WR1[:, :], hc(c), rows=NR).then_inc(b_r1, 1)

            def st_b_lg(c):
                pe.wait_ge(b_rl, c + 1)
                for n, t in enumerate(tiles(c)):
                    last = mm(bx(c), GT[0:NR + 1, t * P:(t + 1) * P], WR2[:, :], cols=slice(n * NE, (n + 1) * NE))
                last.then_inc(b_lg, 1)

            def st_gt(g, gt, bank, c):
                pe.wait_ge(g, c + 1)
                turn_tiles(bank, lambda n: GA[:, TPC * c + n, :], rows=NE).then_inc(gt, 1)

            def hidden(u):
                st, j = blocks[u]
                ex, c = st.ex, st.c
                w = slice(ex.at, ex.at + ex.nj)
                if u == ex.start:
                    pe.wait_ge(w_split, ex.q + 1)
                if st.first_of_sum and j == 0:
                    pe.wait_ge(b_hl if ex.layer == 0 else e_hl, c + 1)
                if u == 0:
                    pe.wait_ge(modr_cp, 1)
                if u >= 2:
                    pe.wait_ge(m_act, u - 1)
                mm(u % 2, W1h[ex.slot][:, w, :][:, j, :], Hh[:, tk(c)], stop=False)
                mm(u % 2, W1h[ex.slot][:, w, :][:, j, :], Hl[:, tk(c)], start=False, stop=False)
                mm(u % 2, W1l[ex.slot][:, w, :][:, j, :], Hh[:, tk(c)], start=False).then_inc(m_hid, 1)

            def output(u):
                st, j = blocks[u]
                ex, bank = st.ex, 2 + st.k % 2
                a = ex.at + j
                if j == 0 and st.k >= 2:
                    pe.wait_ge(m_gated, st.k - 1)
                pe.wait_ge(m_lo, u + 1)
                mm(bank, W2h[ex.slot][:, a, :], AH[:, u % RING, :], start=(j == 0), stop=False)
                mm(bank, W2l[ex.slot][:, a, :], AH[:, u % RING, :], start=False, stop=False)
                mm(bank, W2h[ex.slot][:, a, :], AL[:, u % RING, :], start=False, stop=(j == ex.nj - 1)).then_inc(m_out, 1)

            def unit(u):
                if u < NU_:
                    hidden(u)
                if LAG <= u < NU_ + LAG:
                    output(u - LAG)

            def st_c_be(c):
                pe.wait_ge(b_gtc, NC)
                if c >= 2:
                    pe.wait_ge(e_gtc, c - 1)
                mm(bx(c), BE2[:, :], GT[0:NE, tk(c)]).then_inc(c_be, 1)

            def st_c_bk(c):
                pe.wait_ge(c_t, c + 1)
                turn_tiles(by(c), lambda n: TE[c % 2][:, n * P:(n + 1) * P]).then_inc(c_bk, 1)

            def st_d_tp(c):
                pe.wait_ge(d_nt, c + 1)
                turn_tiles(bx(c), lambda n: HT[:, TPC * c + n, :])
                turn_tiles(by(c), lambda n: xn(c, n)).then_inc(d_tp, 1)

            def st_d_tp2(c):
                pe.wait_ge(d_x1, c + 1)
                turn_tiles(bx(c), lambda n: X1[c % 2][:, n * P:(n + 1) * P]).then_inc(d_tp2, 1)

            def st_d_tp3(c):
                pe.wait_ge(d_n2t, c + 1)
                turn_tiles(by(c), lambda n: xn(c, n)).then_inc(d_tp3, 1)

            def st_d_fc(c):
                pe.wait_ge(d_n2, c + 1)
                for j in range(NF):
                    mm(bx(c) + j, TW[:, T_F0 + j, :], N2[c % 2]).then_inc(d_fc, 1)

            def st_d_pj(c):
                for j in range(NF):
                    pe.wait_ge(d_g, NF * c + j + 1)
                    last = mm(bx(c), TW[:, T_P0 + j, :], G1[c % 2][:, j, :], start=(j == 0), stop=(j == NF - 1))
                last.then_inc(d_pj, 1)

            def st_d_bk(c):
                pe.wait_ge(d_u, c + 1)
                turn_tiles(by(c), lambda n: U2[c % 2][:, n * P:(n + 1) * P]).then_inc(d_bk, 1)

            def st_e_tp(c):
                pe.wait_ge(e_n1, c + 1)
                turn_tiles(bx(c), lambda n: xn(c, n)).then_inc(e_tp, 1)

            def st_e_qk(c):
                pe.wait_ge(e_l1, c + 1)
                for n in range(TPC // 2):
                    for m in range(2):
                        i = 2 * n + m
                        last = mm(by(c) - n, hc(c)[:, i * P:(i + 1) * P], TW[:, T_Q0:T_Q0 + 2, :].rearrange("p a b -> p (a b)")[:, 0:QKV],
                                  cols=slice(m * QKV, (m + 1) * QKV))
                    last.then_inc(e_qk, 1)

            def st_e_at(c):
                pe.wait_ge(e_ao, c + 1)
                turn_tiles(by(c), lambda n: AO[c % 2][:, n * P:(n + 1) * P]).then_inc(e_at, 1)

            def st_e_pj(c):
                pe.wait_ge(e_aot, c + 1)
                for n in range(TPC):
                    last = mm(bx(c), AOT[c % 2][:, n * P:(n + 1) * P], TW[:, T_PJ, :], cols=slice(n * P, (n + 1) * P))
                last.then_inc(e_pj, 1)

            def st_e_tp2(c):
                pe.wait_ge(e_n2, c + 1)
                turn_tiles(by(c), lambda n: xn(c, n)).then_inc(e_tp2, 1)

            def st_e_lg(c):
                pe.wait_ge(e_hh, c + 1)
                for n in range(TPC):
                    last = mm(bx(c), hc(c)[:, n * P:(n + 1) * P], RT[:, :], cols=slice(n * NE, (n + 1) * NE))
                last.then_inc(e_lg, 1)

            def st_e_cn(c):
                if c == 0:
                    pe.wait_ge(const, 3)
                pe.wait_ge(e_cs, c + 1)
                flat = "p t e -> p (t e)"
                mm(by(c), UT[:, :], CSO[:, tsl(c), :].rearrange(flat), stop=False, cols=slice(0, NE * TPC))
                mm(by(c), ON[:, :], CS[:, tsl(c), :].rearrange(flat), start=False, cols=slice(0, NE * TPC)).then_inc(e_cn, 1)

            def st_f_bk(c):
                pe.wait_ge(e_gtc, NC)
                wait_sum(pe, last_step[1][c])
                if c >= 2:
                    pe.wait_ge(f_o, c - 1)
                turn_tiles(by(c), lambda n: ACC[:, c * CH + n * P:c * CH + (n + 1) * P]).then_inc(f_bk, 1)

            run(0.0, unit, mod_turn=st_mod_turn, mod_mm=st_mod_mm, a_tp=st_a_tp, a_bu=st_a_bu, a_y=st_a_y, a_hid0=lambda c: st_a_hid(c, 0),
                a_hid1=lambda c: st_a_hid(c, 1), a_z=st_a_z, a_bk=st_a_bk, b_tp=st_b_tp, b_r1=st_b_r1, b_lg=st_b_lg,
                b_gt=lambda c: st_gt(b_g, b_gt, by(c), c), c_be=st_c_be, c_bk=st_c_bk, d_tp=st_d_tp, d_tp2=st_d_tp2, d_tp3=st_d_tp3,
                d_fc=st_d_fc, d_pj=st_d_pj, d_bk=st_d_bk, e_tp=st_e_tp, e_qk=st_e_qk, e_at=st_e_at, e_pj=st_e_pj, e_tp2=st_e_tp2,
                e_lg=st_e_lg, e_cn=st_e_cn, e_gt=lambda c: st_gt(e_g, e_gt, bx(c), c), f_bk=st_f_bk)

        @block.vector
        def _(dve):
            linked = [0]

            def link(ins):
                linked[0] += 1
                ins.then_inc(dch, 1)
                dve.wait_ge(dch, linked[0])

            V = nc.vector
            LN2H, LN2L = two_part(np.log(2.0))
            PI2A, rest = two_part(2.0 * np.pi)
            PI2B, PI2C = two_part(rest)
            ROUND = 1.5 * 2.0 ** 23

            def exp3(dst, src, scale):
                link(V.tensor_scalar(EX[:, :], src, scale, 88.0, ALU.mult, ALU.min))
                link(V.tensor_scalar(EX[:, :], EX[:, :], -87.0, None, ALU.max))
                link(V.tensor_scalar(EK[:, :], EX[:, :], float(np.log2(np.e)), ROUND, ALU.mult, ALU.add))
                link(V.tensor_scalar(EK[:, :], EK[:, :], ROUND, None, ALU.subtract))
                link(V.scalar_tensor_tensor(EF[:, :], EK[:, :], -LN2H, EX[:, :], ALU.mult, ALU.add))
                link(V.scalar_tensor_tensor(EF[:, :], EK[:, :], -LN2L, EF[:, :], ALU.mult, ALU.add))
                link(V.tensor_scalar(EI[:, :], EK[:, :], 127.0, 2.0 ** 23, ALU.add, ALU.mult))
                link(V.tensor_scalar(EQ[:, :], EF[:, :], 1 / 5040.0, None, ALU.mult))
                for f in (720, 120, 24, 6, 2, 1):
                    link(V.scalar_tensor_tensor(EQ[:, :], EQ[:, :], 1.0 / f, EF[:, :], ALU.add, ALU.mult))
                link(V.scalar_tensor_tensor(dst, EQ[:, :], 1.0, EI[:, :].bitcast(F32), ALU.add, ALU.mult))

            def stats(c, tile, ve, eps, rms=False):
                t = tiles(c)
                for n in range(TPC):
                    last = V.bn_stats(ST[:, t[n], :], tile(n))
                link(last)
                for n in range(TPC):
                    last = V.bn_aggr(MV[:, t[n], :], ST[:, t[n], :])
                link(last)
                v = VE[:, tsl(c)]
                mean, var = MV[:, tsl(c), 0], MV[:, tsl(c), 1]
                if rms:
                    link(V.tensor_tensor(v, mean, mean, ALU.mult))
                    V.scalar_tensor_tensor(v, v, eps, var, ALU.add, ALU.add).then_inc(ve, 1)
                else:
                    V.tensor_scalar(v, var, eps, None, ALU.add).then_inc(ve, 1)

            def normalise(c, dst, src, rs, done, rms=False):
                dve.wait_ge(rs, c + 1)
                for n, t in enumerate(tiles(c)):
                    if rms:
                        last = V.tensor_scalar(dst(n), src(n), RS[:, t:t + 1], None, ALU.mult)
                    else:
                        last = V.tensor_scalar(dst(n), src(n), MV[:, t, 0:1], RS[:, t:t + 1], ALU.subtract, ALU.mult)
                last.then_inc(done, 1)

            def rows(buf, c):
                return lambda n: buf[:, TPC * c + n, :]

            def xns(c):
                return lambda n: xn(c, n)

            def add_x(c, bk, done):
                dve.wait_ge(bk, c + 1)
                x = X[:, tsl(c), :].rearrange("p t d -> p (t d)")
                V.tensor_tensor(x, x, PS[:, by(c), :], ALU.add).then_inc(done, 1)

            def st_a_ve(c):
                dve.wait_ge(x_in0 if c < 2 else x_in1, 32)
                stats(c, rows(X, c), a_ve, 1e-5)

            def st_a_xn(c):
                if c >= 2:
                    dve.wait_ge(b_tp, c - 1)
                normalise(c, xns(c), rows(X, c), a_rs, a_xn)

            for c in range(2):
                st_a_ve(c)

            V.memset(SG[:, 0:2], 1.0)
            link(V.memset(SM[:, 22:23], 0.5))
            V.memset(SG[96:128, 0:1], -1.0)
            V.memset(SG[32:64, 1:2], -1.0)
            link(V.memset(SG[96:128, 1:2], -1.0))

            dve.wait_ge(col_in, 16 * 9)
            exp3(SM[:, 0:3], COL[:, 0:3], 1.0)
            link(V.tensor_scalar(SM[:, 12:13], SM[:, 1:2], 1.0 / (2 * np.pi), ROUND, ALU.mult, ALU.add))
            link(V.tensor_scalar(SM[:, 12:13], SM[:, 12:13], ROUND, None, ALU.subtract))
            link(V.scalar_tensor_tensor(SM[:, 8:9], SM[:, 12:13], -PI2A, SM[:, 1:2], ALU.mult, ALU.add))
            link(V.scalar_tensor_tensor(SM[:, 8:9], SM[:, 12:13], -PI2B, SM[:, 8:9], ALU.mult, ALU.add))
            link(V.scalar_tensor_tensor(SM[:, 8:9], SM[:, 12:13], -PI2C, SM[:, 8:9], ALU.mult, ALU.add))
            link(V.tensor_scalar(SM[:, 8:9], SM[:, 8:9], 3.1415925, -3.1415925, ALU.min, ALU.max))
            link(V.scalar_tensor_tensor(SM[:, 9:10], SM[:, 8:9], -1.0, SM[:, 8:9], ALU.mult, ALU.min))
            V.tensor_scalar(SM[:, 9:10], SM[:, 9:10], np.pi / 2, None, ALU.add).then_inc(trig_in, 1)
            for c in range(2):
                st_a_xn(c)
            exp3(DEC[:, :], SM[:, 0:3], -1.0)
            link(V.tensor_tensor(SM[:, 18:19], DEC[:, 0:1], DEC[:, 0:1], ALU.mult))
            link(V.tensor_scalar(SM[:, 18:19], SM[:, 18:19], -1.0, 1.0, ALU.mult, ALU.add))
            V.tensor_scalar(SM[:, 18:19], SM[:, 18:19], 0.0, None, ALU.max).then_inc(gam_in, 1)

            def clamp_gates(g, tmp):
                link(V.tensor_scalar(tmp, g, 0.0, 2.0, ALU.is_ge, ALU.mult))
                link(V.scalar_tensor_tensor(g, g, -1.0, g, ALU.mult, ALU.max))
                link(V.tensor_scalar(g, g, 0.25, None, ALU.max))
                return V.scalar_tensor_tensor(g, tmp, 1.0, g, ALU.subtract, ALU.mult)

            dve.wait_ge(modps, 1)
            link(V.tensor_copy(MF[:, :, :, :].rearrange("p n j b -> p (n j b)"), PS[:, 3, 0:2 * 6 * B]))
            for j in (CA, CB):
                link(V.tensor_scalar(MF[:, :, j, :], MF[:, :, j, :], 1.0, None, ALU.add))
            link(clamp_gates(MF[:, :, GAT, :], GTMP[:, 0, :, :]))
            clamp_gates(MF[:, :, GB, :], GTMP[:, 1, :, :]).then_inc(mod_done, 1)

            dve.wait_ge(turned, 1)
            V.tensor_copy(TW[:, T_BW, :], PS[:, 0, 0:P])
            V.tensor_scalar(TW[:, T_M1, :], PS[:, 0, P:2 * P], SG[:, 1:2], None, ALU.mult)
            V.tensor_scalar(TW[:, T_M2, :], PS[:, 0, 2 * P:3 * P], -1.0, None, ALU.mult)
            V.tensor_copy(TW[:, T_D, :], PS[:, 0, 3 * P:4 * P]).then_inc(tw_done, 1)

            dve.wait_ge(trig, 1)
            V.memset(TC[:, 0:1], 1.0)
            V.memset(TS[:, 0:1], 0.0)
            V.tensor_copy(TC[:, 1:2], SM[:, 11:12])
            link(V.tensor_copy(TS[:, 1:2], SM[:, 10:11]))
            k = 1
            while k + 1 < L:
                n = min(k, L - 1 - k)
                o, i = slice(k + 1, k + n + 1), slice(1, n + 1)
                c1, s1 = TC[:, k:k + 1], TS[:, k:k + 1]
                V.tensor_scalar(Y[0][:, 0:n], TS[:, i], s1, None, ALU.mult)
                link(V.tensor_scalar(Q[:, 0:n], TC[:, i], s1, None, ALU.mult))
                V.scalar_tensor_tensor(TC[:, o], TC[:, i], c1, Y[0][:, 0:n], ALU.mult, ALU.subtract)
                link(V.scalar_tensor_tensor(TS[:, o], TS[:, i], c1, Q[:, 0:n], ALU.mult, ALU.add))
                k *= 2

            dve.wait_ge(gam, 1)
            link(V.tensor_tensor(SG[:, 2:3], SG[:, 0:1], SM[:, 19:20], ALU.mult))
            V.tensor_scalar(TIN[0:64, :], TC[0:64, 0:L], SG[0:64, 2:3], None, ALU.mult)
            link(V.tensor_scalar(TIN[64:128, :], TS[64:128, 0:L], SG[64:128, 2:3], None, ALU.mult))

            dve.wait_ge(trig, 2)
            link(V.tensor_scalar(SM[:, SIG:SIG + 1], SM[:, SIG:SIG + 1], 0.5, 0.5, ALU.mult, ALU.add))
            V.memset(GT[32:33, :], 1.0)
            dve.wait_ge(sc_done, 1)
            for b in range(B):
                last = V.tensor_copy(SCB[:, b, :], SC[:, 1, b:b + 1].to_broadcast([P, P]))
            last.then_inc(scb_done, 1)

            def st_mod_rows(_):
                dve.wait_ge(modr_cp, 1)
                for j in (CA, CB):
                    link(V.tensor_scalar(MODR[:, :, j, :], MODR[:, :, j, :], 1.0, None, ALU.add))
                clamp_gates(MODR[:, :, GB, :], CTMP[:, :, :]).then_inc(modr_done, 1)

            def st_a_u(c):
                dve.wait_ge(a_bu, c + 1)
                half = tk(c % CPB)
                link(V.tensor_tensor(Q, PS[:, by(c), :], TIN[:, half], ALU.mult))
                if c >= 2:
                    dve.wait_ge(a_z, c - 1)
                start = 0.0 if c % CPB == 0 else U[(c - 1) % 2][:, CH - 1:CH]
                V.tensor_tensor_scan(U[c % 2], DEC[:, 0:1].to_broadcast([P, CH]), Q, start, ALU.mult, ALU.add).then_inc(a_u, 1)
                dve.wait_ge(a_u, c + 1)
                V.tensor_tensor(WC[c % 2], TC[:, half], U[c % 2], ALU.mult).then_inc(a_wc, 1)

            def st_a_t(c):
                dve.wait_ge(a_z, c + 1)
                link(V.scalar_tensor_tensor(T2[c % 2], PS[:, bx(c), :], SM[:, SIG:SIG + 1], hc(c), ALU.mult, ALU.add))
                V.tensor_scalar(T2[c % 2], T2[c % 2], MF[:, 0, GAT, c // CPB:c // CPB + 1], None, ALU.mult).then_inc(a_t, 1)

            def st_b_ve(c):
                dve.wait_ge(a_x, c + 1)
                stats(c, rows(X, c), b_ve, 1e-5)

            def st_hl(hh, hl, c):
                dve.wait_ge(hh, c + 1)
                V.tensor_tensor(Hl[:, tk(c)], hc(c), Hh[:, tk(c)].bitcast(F32), ALU.subtract).then_inc(hl, 1)

            def each(col):
                return col.rearrange("p (t a) -> p t a", a=1).to_broadcast([P, TPC, NE])

            def st_logits(lg, d, c):
                dve.wait_ge(lg, c + 1)
                logits = PS[:, bx(c), 0:TPC * NE].rearrange("p (t e) -> p t e", e=NE)
                link(V.tensor_reduce(RV[:, 0, tsl(c)], logits, AX.X, ALU.max))
                V.tensor_tensor(GA[:, tsl(c), :], logits, each(RV[:, 0, tsl(c)]), ALU.subtract).then_inc(d, 1)

            def top_two(e, c):
                dve.wait_ge(e, c + 1)
                t4 = tsl(c)
                link(V.tensor_reduce(RV[:, 1, t4], PG[:, t4, :], AX.X, ALU.add))
                link(V.reciprocal(RV[:, 2, t4], RV[:, 1, t4]))
                link(V.tensor_tensor(PG[:, t4, :], PG[:, t4, :], each(RV[:, 2, t4]), ALU.mult))
                for t in tiles(c):
                    last = V.max(M8[:, t, :], PG[:, t, :])
                link(last)
                for t in tiles(c):
                    last = V.max_index(I8[:, t, :], M8[:, t, :], PG[:, t, :])
                link(last)
                link(V.tensor_copy(IF[:, t4, :], I8[:, t4, 0:2]))
                if c == 0:
                    dve.wait_ge(const, 3)
                V.tensor_tensor(EQ1[:, t4, :], IO[:, t4, :], IF[:, t4, 0:1].to_broadcast([P, TPC, NE]), ALU.is_equal)
                return V.tensor_tensor(EQ2[:, t4, :], IO[:, t4, :], IF[:, t4, 1:2].to_broadcast([P, TPC, NE]), ALU.is_equal)

            def weigh(w1, w2, c):
                t4 = tsl(c)
                V.tensor_tensor(EQ1[:, t4, :], EQ1[:, t4, :], each(w1), ALU.mult)
                link(V.tensor_tensor(EQ2[:, t4, :], EQ2[:, t4, :], each(w2), ALU.mult))
                return V.tensor_tensor(GA[:, t4, :], EQ1[:, t4, :], EQ2[:, t4, :], ALU.add)

            def st_b_t2(c):
                link(top_two(b_e, c))
                V.tensor_tensor(RV[:, 3, tsl(c)], M8[:, tsl(c), 1], M8[:, tsl(c), 0], ALU.subtract).then_inc(b_t2, 1)

            def st_b_g(c):
                dve.wait_ge(b_e2, c + 1)
                V.tensor_scalar(RV[:, 0, tsl(c)], RV[:, 4, tsl(c)], -0.5, 0.5, ALU.mult, ALU.add)
                link(V.tensor_scalar(RV[:, 1, tsl(c)], RV[:, 4, tsl(c)], 0.5, 0.5, ALU.mult, ALU.add))
                weigh(RV[:, 0, tsl(c)], RV[:, 1, tsl(c)], c).then_inc(b_g, 1)

            def unit(u):
                if u >= 1 and u <= NU_:
                    dve.wait_ge(m_hi, u)
                    r = (u - 1) % RING
                    V.tensor_tensor(AL[:, r, :], A32[:, (u - 1) % NJ0, :], AH[:, r, :].bitcast(F32), ALU.subtract).then_inc(m_lo, 1)
                if u in sums and sums[u].own_vector:
                    st = sums[u]
                    dve.wait_ge(m_gated, st.k + 1)
                    wait_sum(dve, st.k - 2)
                    V.tensor_tensor(ACC[:, tk(st.c)], ACC[:, tk(st.c)], MG[st.k % 2], ALU.add).then_inc(m_accv, 1)
                if u in gates:
                    st = gates[u]
                    dve.wait_ge(m_out, st.last + 1)
                    out_ps = PS[:, 2 + st.k % 2, :]
                    if st.ex.e < 0:
                        V.tensor_copy(ACC[:, tk(st.c)], out_ps).then_inc(m_gated, 1)
                        return
                    dve.wait_ge(m_wb, spreads(st.k))
                    if st.first_of_sum:
                        V.tensor_tensor(ACC[:, tk(st.c)], out_ps, WB[st.k % 2], ALU.mult).then_inc(m_gated, 1)
                        return
                    wait_sum(dve, st.k - 2)
                    V.tensor_tensor(MG[st.k % 2], out_ps, WB[st.k % 2], ALU.mult).then_inc(m_gated, 1)

            def st_c_t(c):
                dve.wait_ge(c_be, c + 1)
                wait_sum(dve, last_step[0][c])
                link(V.scalar_tensor_tensor(TE[c % 2], PS[:, bx(c), :], COL[:, BS2:BS2 + 1], ACC[:, tk(c)], ALU.add, ALU.add))
                V.tensor_scalar(TE[c % 2], TE[c % 2], MF[:, 0, GB, c // CPB:c // CPB + 1], None, ALU.mult).then_inc(c_t, 1)

            def st_d_ve(c):
                dve.wait_ge(c_x, c + 1)
                stats(c, rows(X, c), d_ve, 1e-5)

            def st_d_ve2(c):
                dve.wait_ge(d_ht, c + 1)
                stats(c, rows(HT, c), d_ve2, 1e-6, rms=True)

            def st_d_x1(c):
                dve.wait_ge(d_nf, c + 1)
                start = 0.0 if c % CPB == 0 else HS[(c - 1) % 2][:, CH - 1:CH]
                p = c % 2
                V.tensor_tensor_scan(HS[p], DEC[:, 2:3].to_broadcast([P, CH]), NFM[p], start, ALU.mult, ALU.add).then_inc(d_hs, 1)
                if c >= 1:
                    dve.wait_ge(d_x1, c)
                link(V.scalar_tensor_tensor(SK, NFM[p], COL[:, DS:DS + 1], PS[:, bx(c), :], ALU.mult, ALU.add))
                dve.wait_ge(d_hs, c + 1)
                V.scalar_tensor_tensor(X1[p], HS[p], COL[:, CO:CO + 1], SK, ALU.mult, ALU.add).then_inc(d_x1, 1)

            def st_d_ve3(c):
                dve.wait_ge(d_x1t, c + 1)
                stats(c, xns(c), d_ve3, 1e-6, rms=True)

            def st_d_u(c):
                dve.wait_ge(d_pj, c + 1)
                link(V.tensor_tensor(U2[c % 2], PS[:, bx(c), :], X1[c % 2], ALU.add))
                V.tensor_scalar(U2[c % 2], U2[c % 2], MF[:, 1, GAT, c // CPB:c // CPB + 1], None, ALU.mult).then_inc(d_u, 1)

            def st_e_ve(c):
                dve.wait_ge(d_x, c + 1)
                stats(c, rows(X, c), e_ve, 1e-5)

            def st_e_ve2(c):
                dve.wait_ge(e_mod, c + 1)
                stats(c, rows(HT, c), e_ve2, 1e-5)

            def qkv_of(t):
                g = QV[:, t, :].rearrange("p (g w) -> p g w", w=GW)
                q = g[:, :, 0:QPK * HD].rearrange("p g (q d) -> p g q d", d=HD)
                k = g[:, :, QPK * HD:(QPK + 1) * HD].rearrange("p g (a d) -> p g a d", a=1).to_broadcast([P, NKV, QPK, HD])
                v = g[:, :, (QPK + 1) * HD:].rearrange("p g (a d) -> p g a d", a=1).to_broadcast([P, NKV, QPK, HD])
                return q, k, v

            def heads(buf, n):
                return buf[:, n * D:(n + 1) * D].rearrange("p (g q d) -> p g q d", g=NKV, q=QPK)

            def probs(c):
                return SP2[:, 6 * (c % 2):6 * (c % 2) + 6, :]

            def st_e_dd(c):
                if c < CPB:
                    return
                dve.wait_ge(e_qv, (TPC // 2) * (c + 1))
                for n, t in enumerate(tiles(c)):
                    q, k1, _ = qkv_of(t)
                    _, k0, _ = qkv_of(t - NT // B)
                    V.tensor_tensor(heads(PR, n), q, k0, ALU.mult)
                    last = V.tensor_tensor(heads(PR, TPC + n), q, k1, ALU.mult)
                link(last)
                s = probs(c)
                link(V.tensor_reduce(s[:, 0:2, :].rearrange("p a m -> p (a m)"), PR.rearrange("p (m d) -> p m d", d=HD), AX.X, ALU.add))
                V.tensor_tensor(s[:, 4, :], s[:, 0, :], s[:, 1, :], ALU.subtract).then_inc(e_dd, 1)

            def st_e_ao(c):
                ao = AO[c % 2]
                if c < CPB:
                    dve.wait_ge(e_qv, (TPC // 2) * (c + 1))
                    for n, t in enumerate(tiles(c)):
                        last = V.tensor_copy(heads(ao, n), qkv_of(t)[2])
                    last.then_inc(e_ao, 1)
                    return
                dve.wait_ge(e_e, c - CPB + 1)
                s = probs(c)
                V.tensor_scalar(s[:, 2, :], s[:, 5, :], 0.5, 0.5, ALU.mult, ALU.add)
                link(V.tensor_scalar(s[:, 3, :], s[:, 5, :], -0.5, 0.5, ALU.mult, ALU.add))

                def prob(a, n):
                    return s[:, a, n * NH:(n + 1) * NH].rearrange("p (g q a) -> p g q a", g=NKV, a=1).to_broadcast([P, NKV, QPK, HD])

                if c > CPB:
                    dve.wait_ge(e_ao, c)
                for n, t in enumerate(tiles(c)):
                    V.tensor_tensor(heads(PR, n), qkv_of(t - NT // B)[2], prob(2, n), ALU.mult)
                    last = V.tensor_tensor(heads(PR, TPC + n), qkv_of(t)[2], prob(3, n), ALU.mult)
                link(last)
                V.tensor_tensor(ao, PR[:, 0:CH], PR[:, CH:2 * CH], ALU.add).then_inc(e_ao, 1)

            def st_e_h1(c):
                dve.wait_ge(e_pj, c + 1)
                h = HT[:, tsl(c), :].rearrange("p t d -> p (t d)")
                V.tensor_tensor(h, h, PS[:, bx(c), :], ALU.add).then_inc(e_h1, 1)
                dve.wait_ge(e_h1, c + 1)
                stats(c, rows(HT, c), e_ve3, 1e-5)

            def st_e_cs(c):
                link(top_two(e_ee, c))
                link(V.tensor_tensor(CSO[:, tsl(c), :], EQ1[:, tsl(c), :], EQ2[:, tsl(c), :], ALU.add))
                for t in tiles(c):
                    if t == 0:
                        last = V.memset(CS[:, 0, :], 0.0)
                    else:
                        last = V.tensor_tensor(CS[:, t, :], CS[:, t - 1, :], CSO[:, t - 1, :], ALU.add)
                    if t != tiles(c)[-1]:
                        link(last)
                last.then_inc(e_cs, 1)
                link(V.tensor_tensor(RV[:, 0, tsl(c)], M8[:, tsl(c), 0], M8[:, tsl(c), 1], ALU.add))
                link(V.reciprocal(RV[:, 1, tsl(c)], RV[:, 0, tsl(c)]))
                V.tensor_tensor(RV[:, 2, tsl(c)], M8[:, tsl(c), 0], RV[:, 1, tsl(c)], ALU.mult)
                link(V.tensor_tensor(RV[:, 3, tsl(c)], M8[:, tsl(c), 1], RV[:, 1, tsl(c)], ALU.mult))
                link(weigh(RV[:, 2, tsl(c)], RV[:, 3, tsl(c)], c))

            def st_e_g(c):
                dve.wait_ge(e_cn, c + 1)
                before = PS[:, by(c), 0:NE * TPC].rearrange("p (t e) -> p t e", e=NE)
                link(V.tensor_scalar(KEEP[:, tsl(c), :], before, CAP, None, ALU.is_lt))
                V.tensor_tensor(GA[:, tsl(c), :], GA[:, tsl(c), :], KEEP[:, tsl(c), :], ALU.mult).then_inc(e_g, 1)

            def st_f_o(c):
                dve.wait_ge(f_bk, c + 1)
                h = HT[:, tsl(c), :].rearrange("p t d -> p (t d)")
                link(V.tensor_tensor(h, h, PS[:, by(c), :], ALU.add))
                link(V.tensor_tensor(HT[:, tsl(c), :], HT[:, tsl(c), :], MODR[:, c // CPB, GB:GB + 1, :].to_broadcast([P, TPC, D]), ALU.mult))
                V.tensor_tensor(X[:, tsl(c), :], X[:, tsl(c), :], HT[:, tsl(c), :], ALU.add).then_inc(f_o, 1)

            run(2.6, unit, mod_rows=st_mod_rows, a_ve=lambda c: st_a_ve(c) if c >= 2 else None,
                a_xn=lambda c: st_a_xn(c) if c >= 2 else None, a_u=st_a_u, a_t=st_a_t,
                a_x=lambda c: add_x(c, a_bk, a_x), b_ve=st_b_ve, b_xn=lambda c: normalise(c, xns(c), rows(X, c), b_rs, b_xn),
                b_hl=lambda c: st_hl(b_hh, b_hl, c), b_d=lambda c: st_logits(b_lg, b_d, c), b_t2=st_b_t2, b_g=st_b_g,
                c_t=st_c_t, c_x=lambda c: add_x(c, c_bk, c_x), d_ve=st_d_ve,
                d_xn=lambda c: normalise(c, xns(c), rows(X, c), d_rs, d_xn), d_ve2=st_d_ve2,
                d_nt=lambda c: normalise(c, xns(c), rows(HT, c), d_rs2, d_nt, rms=True), d_x1=st_d_x1, d_ve3=st_d_ve3,
                d_n2t=lambda c: normalise(c, xns(c), xns(c), d_rs3, d_n2t, rms=True), d_u=st_d_u,
                d_x=lambda c: add_x(c, d_bk, d_x), e_ve=st_e_ve, e_xn=lambda c: normalise(c, xns(c), rows(X, c), e_rs, e_xn),
                e_ve2=st_e_ve2, e_n1=lambda c: normalise(c, xns(c), rows(HT, c), e_rs2, e_n1), e_dd=st_e_dd, e_ao=st_e_ao,
                e_h1=st_e_h1, e_n2=lambda c: normalise(c, xns(c), rows(HT, c), e_rs3, e_n2), e_hl=lambda c: st_hl(e_hh, e_hl, c),
                e_d=lambda c: st_logits(e_lg, e_d, c), e_cs=st_e_cs, e_g=st_e_g, f_o=st_f_o)


_OUTS = [((2, 1024, 128), "float32")]


def kernel(**inputs):
    import numpy as _np
    import concourse.bacc as _bacc
    from concourse import mybir as _mybir
    from concourse.bass_utils import run_bass_kernel_spmd as _run

    nc = _bacc.Bacc("TRN2", target_bir_lowering=False, num_devices=1)
    arrays, aps = {}, {}
    for name in inputs:
        a = _np.ascontiguousarray(inputs[name])
        if name == "L0_attn_res_logit":
            a = a.reshape(1, 1)
        arrays[f"in_{name}_dram"] = a
        aps[name] = nc.dram_tensor(f"in_{name}_dram", a.shape, _mybir.dt.from_np(a.dtype), kind="ExternalInput").ap()
    shape, dtype = _OUTS[0]
    out = nc.dram_tensor("out_0_dram", shape, _mybir.dt.from_np(_np.dtype(dtype)), kind="ExternalOutput").ap()
    adaln_two_layers(nc, aps, out)
    r = _run(nc, [arrays], core_ids=[0])
    return r.results[0]["out_0_dram"]
```

```python
from contextlib import ExitStack

import numpy as np

import concourse.bass as bass
from concourse import mybir

F32 = mybir.dt.float32
F32R = mybir.dt.float32r
I32 = mybir.dt.int32
U32 = mybir.dt.uint32
ALU = mybir.AluOpType
ACT = mybir.ActivationFunctionType
AX = mybir.AxisListType

P = 128
CH = 512
TPC = CH // P
RING = 6


def two_part(value, bits=12):
    high = np.float32(value)
    high = (high.view(np.uint32) & np.uint32(0xFFFFFFFF << (24 - bits) & 0xFFFFFFFF)).view(np.float32)
    return float(high), float(value - float(high))


def adaln_two_layers(nc, A, out):
    B, L, D = A["L0_attn_x3d"].shape
    NS = A["L0_attn_B_re"].shape[0]
    HID = A["L0_attn_W1"].shape[1]
    NJ0 = HID // P
    NE = A["L0_ffn_We1"].shape[0]
    NR = A["L0_ffn_Wr1"].shape[1]
    NJ1 = A["L1_ffn_moe_w1"].shape[2] // P
    NF = A["L1_attn_ff_fc_w"].shape[0] // P
    QKV = A["L1_ffn_qkv_weight"].shape[0]
    T = B * L
    NT = T // P
    NC = T // CH
    CPB = NC // B
    NKV, NH = 4, 16
    HD = D // NH
    QPK = NH // NKV
    GW = (QPK + 2) * HD
    CAP = float(-(-T * 2 * 5 // (NE * 4)))
    assert D == P and 4 * NS == P and NE == 8 and CPB == 2 and B == 2 and NJ0 == 4 and NJ1 == 2 and NF == 2

    x_rows = A["L0_attn_x3d"].rearrange("b (t p) d -> p (b t) d", p=P)
    out_rows = out.rearrange("b (t p) d -> p (b t) d", p=P)

    def column(name):
        return A[name].rearrange("(p a) -> p a", a=1)

    with ExitStack() as ctx:
        def sb(name, shape, dt=F32):
            return ctx.enter_context(nc.sbuf_tensor(name, shape, dt))

        def sems(names):
            return [ctx.enter_context(nc.semaphore(n)) for n in names.split()]

        X = sb("X", [P, NT, D])
        HT = sb("HT", [P, NT, D])
        Hh = sb("Hh", [P, T], F32R)
        Hl = sb("Hl", [P, T], F32R)
        ACC = sb("ACC", [P, T])
        GT = sb("GT", [P, T])
        MODR = sb("MODR", [P, B, 6, D])
        XN = sb("XN", [P, 2 * TPC, D])
        H = sb("H", [P, 2, CH])

        WRAW = [[sb(f"wraw{n}_{s}", [P, HID]) for s in range(2)] for n in (1, 2)]
        W1h, W1l, W2h, W2l = ([sb(f"{n}_{s}", [P, NJ0, P], F32R) for s in range(2)] for n in ("w1h", "w1l", "w2h", "w2l"))
        AH = sb("AH", [P, RING, CH], F32R)
        AL = sb("AL", [P, RING, CH], F32R)

        def cut(region, at, n):
            return region[:, at:at + n]

        RM = sb("RM", [P, 6144])
        A32 = cut(RM, 0, NJ0 * CH).rearrange("p (j n) -> p j n", j=NJ0)
        WB = [cut(RM, 2048 + CH * n, CH) for n in range(2)]
        MG = [cut(RM, 3072 + CH * n, CH) for n in range(2)]
        GR = cut(RM, 4096, 4 * CH).rearrange("p (g n) -> p g n", g=2)
        WMOD = [cut(RM, 6 * D * n, 6 * D) for n in range(2)]
        TR = cut(RM, 2048, 11 * P).rearrange("p (a b) -> p a b", b=P)

        RB = sb("RB", [P, 10752])
        TIN, TC, TS, Q = (cut(RB, L * n, L if n < 3 else CH) for n in range(4))
        Y = [cut(RB, 3584 + CH * p, CH) for p in range(2)]
        U = [cut(RB, 4608 + CH * p, CH) for p in range(2)]
        G0 = [cut(RB, 5632 + NJ0 * CH * p, NJ0 * CH).rearrange("p (j n) -> p j n", j=NJ0) for p in range(2)]
        WC, WS = ([G0[p][:, n, :] for p in range(2)] for n in range(2))
        T2 = Y
        QV = cut(RB, 0, NT * QKV).rearrange("p (t n) -> p t n", n=QKV)
        NFM, HS, X1, N2 = ([cut(RB, 3072 + 2 * CH * k + CH * p, CH) for p in range(2)] for k in range(4))
        G1 = [cut(RB, 7168 + NF * CH * p, NF * CH).rearrange("p (j n) -> p j n", j=NF) for p in range(2)]
        PR = cut(RB, 9216, CH)
        DKV = cut(RB, 9728, 2 * TPC * NKV * 2 * HD).rearrange("p (a m d) -> p a m d", a=2, d=2 * HD)
        SK = cut(RB, 10240, CH)
        U2, AOT = N2, NFM
        TE = [G1[p][:, 0, :] for p in range(2)]
        AO = [G1[p][:, 0, :] for p in range(2)]

        LW1 = sb("LW1", [P, HID])
        LW2 = sb("LW2", [P, NJ0, D])
        TW = sb("TW", [P, 11, P])
        CT = sb("CT", [P, 2, B])
        SC = sb("SC", [P, 2, B])
        SCB = sb("SCB", [P, B, P])
        MF = sb("MF", [P, 2, 6, B])
        ID = sb("ID", [P, P])
        UT = sb("UT", [P, P])
        ON = sb("ON", [P, P])
        WR1 = sb("WR1", [P, NR])
        WR2 = sb("WR2", [NR + 1, NE])
        RT = sb("RT", [P, NE])
        BR1 = sb("BR1", [NR, 1])
        B1 = sb("B1", [P, 1 + NE, NJ0])
        BE2 = sb("BE2", [NE, D])
        COL = sb("COL", [P, 12])
        EX = sb("EX", [P, 3])
        SM = sb("SM", [P, 24])
        ST = sb("ST", [P, NT, 6])
        MV = sb("MV", [P, NT, 2])
        VE = sb("VE", [P, NT])
        RS = sb("RS", [P, NT])
        MH = sb("MH", [P, NT])
        EQ1 = sb("EQ1", [P, NT, NE])
        EQ2 = sb("EQ2", [P, NT, NE])
        GA = sb("GA", [P, NT, NE])
        PG = sb("PG", [P, NT, NE])
        M8 = sb("M8", [P, NT, NE])
        I8 = sb("I8", [P, NT, NE], U32)
        IF = sb("IF", [P, NT, 2])
        IO = sb("IO", [P, NT, NE])
        RV = sb("RV", [P, 6, NT])
        SD, ST_, SP0 = (sb(n, [P, 2, TPC * NH]) for n in ("SD", "ST_", "SP0"))
        CS = sb("CS", [P, NT, NE])
        CSO = sb("CSO", [P, NT, NE])
        KEEP = sb("KEEP", [P, NT, NE])
        DEC = sb("DEC", [P, 3])
        IE = sb("IE", [P, 3])
        EK = sb("EK", [P, 3])
        EF = sb("EF", [P, 3])
        EQ = sb("EQ", [P, 3])
        EI = sb("EI", [P, 3], I32)
        SG = sb("SG", [P, 3])
        GTMP = sb("GTMP", [P, 2, 2, B])
        CTMP = sb("CTMP", [P, B, D])

        PS = ctx.enter_context(nc.psum_tensor("PS", [P, 8, CH], F32))

        SIG = 21
        NU, TH, AL_, CO, DS, FNW, INW, L1W, L1B, L2W, L2B, BS2 = range(12)
        T_BW, T_M1, T_M2, T_D, T_F0, T_F1, T_P0, T_P1, T_Q0, T_Q1, T_PJ = range(11)
        SA, CA, GAT, SBT, CB, GB = range(6)

        (x_in0, x_in1, x_in2, col_in, tr_in, tr2_in, mod_in, lru_in, small_in, raw_in0, raw_in1, out_in) = sems(
            "x_in0 x_in1 x_in2 col_in tr_in tr2_in mod_in lru_in small_in raw_in0 raw_in1 out_in")
        raw_in = [raw_in0, raw_in1]
        gr_in = sems("gr_in0 gr_in1 gr_in2 gr_in3")
        (const, dch, pch, sc_done, modps, mod_done, modr_done, scb_done, rates_in, dec_done, gam_in, gam, trig_in, trig, turned, tw_done, tw2_done, modr_cp) = sems(
            "const dch pch sc_done modps mod_done modr_done scb_done rates_in dec_done gam_in gam trig_in trig turned tw_done tw2_done modr_cp")
        (a_ve, a_rs, a_xn, a_tp, a_h, a_bu, a_u, a_wc, a_ws, a_y, a_yc, a_hid0, a_hid1, a_gel0, a_gel1, a_z, a_t, a_bk, a_x) = sems(
            "a_ve a_rs a_xn a_tp a_h a_bu a_u a_wc a_ws a_y a_yc a_hid0 a_hid1 a_gel0 a_gel1 a_z a_t a_bk a_x")
        (b_ve, b_rs, b_xn, b_tp, b_h, b_hh, b_hl, b_r1, b_rl, b_lg, b_d, b_e, b_t2, b_e2, b_g, b_gt, b_gtc) = sems(
            "b_ve b_rs b_xn b_tp b_h b_hh b_hl b_r1 b_rl b_lg b_d b_e b_t2 b_e2 b_g b_gt b_gtc")
        (w_hi, w_split, m_hid, m_act, m_hi, m_hiv, m_lo, m_out, m_gated, m_wb, m_acc, m_accv) = sems(
            "w_hi w_split m_hid m_act m_hi m_hiv m_lo m_out m_gated m_wb m_acc m_accv")
        (c_be, c_t, c_bk, c_x) = sems("c_be c_t c_bk c_x")
        (d_ve, d_rs, d_xn, d_ht, d_ve2, d_rs2, d_nt, d_tp, d_nf, d_hs, d_x1, d_tp2, d_x1t, d_ve3, d_rs3, d_n2t, d_tp3, d_n2, d_fc,
         d_g, d_pj, d_u, d_bk, d_x) = sems(
            "d_ve d_rs d_xn d_ht d_ve2 d_rs2 d_nt d_tp d_nf d_hs d_x1 d_tp2 d_x1t d_ve3 d_rs3 d_n2t d_tp3 d_n2 d_fc d_g d_pj "
            "d_u d_bk d_x")
        (e_ve, e_rs, e_xn, e_mod, e_ve2, e_rs2, e_n1, e_tp, e_l1, e_qk, e_qv, e_dd, e_e, e_ao, e_at, e_aot, e_pj, e_h1, e_ve3,
         e_rs3, e_n2, e_tp2, e_l2, e_hh, e_hl, e_lg, e_d, e_ee, e_cs, e_cn, e_g, e_gt, e_gtc, f_x, f_bk, f_o) = sems(
            "e_ve e_rs e_xn e_mod e_ve2 e_rs2 e_n1 e_tp e_l1 e_qk e_qv e_dd e_e e_ao e_at e_aot e_pj e_h1 e_ve3 "
            "e_rs3 e_n2 e_tp2 e_l2 e_hh e_hl e_lg e_d e_ee e_cs e_cn e_g e_gt e_gtc f_x f_bk f_o")

        def tiles(c):
            return range(TPC * c, TPC * (c + 1))

        def tsl(c):
            return slice(TPC * c, TPC * (c + 1))

        def tk(c):
            return slice(CH * c, CH * (c + 1))

        def bx(c):
            return 4 + 2 * (c % 2)

        def by(c):
            return 5 + 2 * (c % 2)

        def hc(c):
            return H[:, c % 2, :]

        def xn(c, n):
            return XN[:, TPC * (c % 2) + n, :]

        class Step:
            pass

        steps, blocks, experts = [], [], []
        for layer in range(2):
            for g in range(NC // 2):
                for e in range(-1 if layer == 0 else 0, NE):
                    ex = Step()
                    ex.layer, ex.e, ex.nj, ex.q, ex.start = layer, e, (NJ0, NJ1)[layer], len(experts), len(blocks)
                    ex.slot = ex.q % 2
                    ex.at = 0 if layer == 0 else NJ1 * (ex.q // 2 % 2)
                    n0 = 2 * (1 + NE)
                    ex.before = ex.q - 2 if ex.q < n0 + 2 else ex.q - 4
                    experts.append(ex)
                    for c in (2 * g, 2 * g + 1):
                        st = Step()
                        st.ex, st.c, st.k, st.g = ex, c, len(steps), 2 * layer + g
                        st.first_of_sum = e == (-1 if layer == 0 else 0)
                        st.own_vector = st.g == 3 and c % 2 == 1 and not st.first_of_sum
                        steps.append(st)
                        for j in range(ex.nj):
                            blocks.append((st, j))
                        st.last = len(blocks) - 1
                    ex.last = len(blocks) - 1

        def at_most(k, test):
            return sum(1 for s in steps[:k + 1] if test(s))

        def spreads(k):
            return at_most(k, lambda s: s.ex.e >= 0)

        def pool_sums(k):
            return at_most(k, lambda s: not s.first_of_sum and not s.own_vector)

        def vector_sums(k):
            return at_most(k, lambda s: s.own_vector)

        def wait_sum(eng, k):
            if steps[k].first_of_sum:
                eng.wait_ge(m_gated, k + 1)
            elif steps[k].own_vector:
                eng.wait_ge(m_accv, vector_sums(k))
            else:
                eng.wait_ge(m_acc, pool_sums(k))

        def by_vector(u):
            return blocks[u][0].g == 0 and u % 3 == 2

        def highs(u):
            return sum(1 for n in range(u + 1) if not by_vector(n))

        def mg_before(k):
            return max((n for n in range(k % 2, k, 2) if not steps[n].first_of_sum), default=None)

        last_step = [[max(s.k for s in steps if s.ex.layer == n and s.c == c) for c in range(NC)] for n in range(2)]

        def stages(text):
            return {n: float(t) for n, t in (pair.split(":") for pair in text.split())}

        TIMES = {
            "PE": stages("a_tp:0.9 a_bu:1.9 a_y:1.9 a_hid0:1.9 a_hid1:1.9 a_z:3.6 a_bk:0.9 b_tp:0.9 b_r1:1.0 b_lg:0.5 b_gt:0.5 c_be:1.0 "
                         "c_bk:0.9 d_tp:1.8 d_tp2:0.9 d_tp3:0.9 d_fc:1.9 d_pj:1.9 d_bk:0.9 e_tp:0.9 e_qk:1.5 e_at:0.9 e_pj:1.3 e_tp2:0.9 "
                         "e_lg:0.5 e_cn:0.5 e_gt:0.5 f_bk:0.9 mod_turn:1.0 mod_mm:2.6 hidden:0.65 output:0.65"),
            "ACT": stages("res_gate:0.3 a_h:0.8 a_yc:0.7 a_gel0:1.1 a_gel1:1.1 b_h:1.5 b_rl:0.7 b_e:0.3 b_e2:0.3 b_gtc:0.7 "
                          "d_nf:0.7 d_nt:1.1 d_n2t:1.1 d_x1t:0.7 d_n2:0.7 "
                          "d_g:1.1 e_l1:0.8 e_qv:0.9 e_e:0.4 e_aot:0.7 e_l2:1.5 e_ee:0.3 e_gtc:0.7 mod_tw:1.1 mod_cp:1.8 "
                          "activate:0.57 high:0.54 w_high:1.1"),
            "DVE": stages("a_ve:1.6 a_xn:1.1 a_u:2.0 a_t:1.2 a_x:0.7 b_ve:1.6 b_xn:1.1 b_hl:0.7 b_d:0.4 b_t2:2.0 b_g:0.6 c_t:1.3 c_x:0.7 "
                          "d_ve:1.6 d_xn:1.1 d_ve2:1.8 d_x1:2.1 d_ve3:1.8 d_u:1.2 d_x:0.7 e_ve:1.6 e_xn:1.1 e_ve2:1.6 "
                          "e_n1:1.1 e_dd:2.2 e_ao:2.2 e_h1:2.3 e_n2:1.1 e_hl:0.7 e_d:0.4 e_cs:3.5 e_g:0.3 f_o:0.7 "
                          "upper:3.0 small:1.5 mod_rows:2.0 rest:0.62 gate:0.65 sum_v:0.62"),
            "POOL": stages("a_rs:1.1 a_ws:1.4 b_rs:1.1 d_rs:1.1 d_ht:2.6 d_rs2:1.1 d_rs3:1.1 e_rs:1.1 e_mod:2.6 e_rs2:1.1 e_rs3:1.1 f_x:2.6 "
                           "w_rest:2.3 spread:0.8 sum_p:1.25"),
            "SP": stages("raw:1.1 rows:1.1"),
        }
        ROUTE0 = "b_d b_e b_t2 b_e2 b_g b_gt b_gtc".split()
        A_ORDER = ("a_ve a_rs a_xn a_tp a_h a_bu a_u a_ws a_y a_yc a_hid0 a_gel0 a_hid1 a_gel1 a_z a_t a_bk a_x "
                   "b_ve b_rs b_xn b_tp b_h b_hl b_r1 b_rl b_lg").split() + ROUTE0
        B_ORDER = ("c_be c_t c_bk c_x "
                   "d_ve d_rs d_xn d_ht d_ve2 d_rs2 d_nt d_tp d_nf d_x1 d_tp2 d_x1t d_ve3 d_rs3 d_n2t d_tp3 d_n2 d_fc d_g d_pj d_u d_bk d_x "
                   "e_ve e_rs e_xn e_mod e_ve2 e_rs2 e_n1 e_tp e_l1 e_qk e_qv e_dd e_e e_ao e_at e_aot e_pj e_h1 e_rs3 e_n2 e_tp2 "
                   "e_l2 e_hl e_lg e_d e_ee e_cs e_cn e_g e_gt e_gtc").split()
        engine_of = {name: eng for eng, names in TIMES.items() for name in names}
        TABLE = dict(a_gel0="gelu", a_gel1="gelu", b_e="exp", e_ee="exp", d_g="silu")

        needs = {}

        def task(name, n, *before):
            needs[name, n] = [b for b in before if b is not None] + ([(name, n - 1)] if (name, n - 1) in needs else [])

        def sum_task(k):
            return ("gate" if steps[k].first_of_sum else "sum_v" if steps[k].own_vector else "sum_p", k)

        for c in range(NC):
            chain = A_ORDER[3:] if c == 0 else A_ORDER
            for m, name in enumerate(chain):
                task(name, c, (chain[m - 1], c) if m else None)
            if c >= 2:
                needs["a_tp", c].append(("b_gtc", c - 2))
                needs["a_xn", c].append(("b_tp", c - 2))
                needs["a_u", c].append(("a_z", c - 2))
        task("upper", 0, ("a_u", 0))
        needs["a_u", 1].append(("upper", 0))
        task("res_gate", 0, ("a_h", 0))
        task("small", 0, ("upper", 0), ("res_gate", 0))
        needs["a_t", 0].append(("small", 0))
        for m, name in enumerate(("mod_turn", "mod_tw", "mod_mm", "mod_cp", "mod_rows")):
            task(name, 0, (("mod_turn", "mod_tw", "mod_mm", "mod_cp")[m - 1], 0) if m else ("a_hid1", 0))
        needs["mod_mm", 0].append(("small", 0))
        for c in range(NC):
            for m, name in enumerate(B_ORDER):
                task(name, c, (B_ORDER[m - 1], c) if m else ("b_gtc", NC - 1))
            needs["c_t", c].append(sum_task(last_step[0][c]))
            if c >= 2:
                needs["c_be", c].append(("e_gtc", c - 2))
            task("f_x", c, ("e_n2", c))
            task("f_bk", c, ("e_gtc", NC - 1), sum_task(last_step[1][c]), ("f_o", c - 2) if c >= 2 else None)
            task("f_o", c, ("f_bk", c), ("f_x", c))
        needs["d_ht", 0].append(("mod_rows", 0))
        for u, (st, j) in enumerate(blocks):
            k = st.k
            task("hidden", u, ("activate", u - 2) if u >= 2 else ("mod_cp", 0), ("w_rest", st.ex.q),
                 ("b_hl" if st.ex.layer == 0 else "e_hl", st.c))
            task("activate", u, ("hidden", u), ("rest", u - NJ0) if u >= NJ0 else None)
            if not by_vector(u):
                task("high", highs(u) - 1, ("activate", u), ("output", u - RING) if u >= RING else None)
            task("rest", u, ("high", highs(u) - 1) if not by_vector(u) else ("activate", u),
                 ("output", u - RING) if u >= RING else None)
            task("output", u, ("rest", u), ("gate", k - 2) if j == 0 and k >= 2 else None)
        for st in steps:
            k, prior = st.k, sum_task(st.k - 2) if st.k >= 2 else None
            if st.ex.e >= 0:
                task("spread", k, ("gate", k - 2) if k >= 2 else None, ("rows", 2 * st.g + 1))
            task("gate", k, ("output", st.last), ("spread", k) if st.ex.e >= 0 else None,
                 sum_task(mg_before(k)) if not st.first_of_sum and mg_before(k) is not None else None,
                 ("gate", k - 1) if k >= 1 else None)
            if not st.first_of_sum:
                task("sum_v" if st.own_vector else "sum_p", k, ("gate", k), prior)
        for g in range(NC):
            for c in range(2):
                task("rows", 2 * g + c, ("b_gtc" if g < 2 else "e_gtc", 2 * (g % 2) + c),
                     ("spread", max(s.k for s in steps if s.g == g - 1)) if g >= 1 else None)
        for ex in experts:
            task("raw", ex.q, ("w_rest", ex.q - 2) if ex.q >= 2 else None)
            task("w_high", ex.q, ("output", experts[ex.before].last) if ex.before >= 0 else None,
                 ("raw", ex.q), ("a_ws", ex.q) if ex.q < 2 else None)
            task("w_rest", ex.q, ("w_high", ex.q))
        for name in ("spread", "sum_v", "sum_p"):
            ks = sorted(n for m, n in needs if m == name)
            for a, b in zip(ks, ks[1:]):
                needs[name, b].append((name, a))

        def took(name, n):
            t = TIMES[engine_of[name]][name]
            if name in ("w_high", "w_rest") and experts[n].layer == 1:
                t = t / 2
            if name == "rest" and by_vector(n):
                t = t + 0.4
            return t

        def after(name, n, b):
            if engine_of[b[0]] == "SP" and engine_of[name] != "SP":
                return 2.2
            return 0.2 if engine_of[b[0]] != engine_of[name] else 0.03

        TABLE_LOAD, RELUCTANCE = 1.28, 5.0

        def listed():
            users = {t: [] for t in needs}
            for t, before in needs.items():
                for b in set(before):
                    users[b].append(t)
            tail, left = {}, [t for t in needs if not users[t]]
            waits = {t: len(users[t]) for t in needs}
            while left:
                t = left.pop()
                tail[t] = took(*t) + max((after(*v, t) + tail[v] for v in users[t]), default=0.0)
                for b in set(needs[t]):
                    waits[b] -= 1
                    if waits[b] == 0:
                        left.append(b)
            free = dict(PE=16.0, ACT=18.0, DVE=25.0, POOL=14.0, SP=20.0)
            order = {eng: [] for eng in TIMES}
            open_ = {t: len(set(before)) for t, before in needs.items()}
            ready = {eng: [] for eng in TIMES}
            for t, n in open_.items():
                if n == 0:
                    ready[engine_of[t[0]]].append((0.0, t))
            table, done = None, {}
            while any(ready.values()):
                best = None
                for eng, waiting in ready.items():
                    if not waiting:
                        continue
                    now = max(free[eng], min(r for r, _ in waiting))

                    def key(item):
                        name, n = item[1]
                        change = 0 if eng != "ACT" or table_of(name, n) in (None, table) else RELUCTANCE
                        return change - tail[item[1]], n

                    pick = min((item for item in waiting if item[0] <= now), key=key)
                    at = max(now, pick[0])
                    if best is None or at < best[0]:
                        best = (at, eng, pick)
                at, eng, pick = best
                ready[eng].remove(pick)
                name, n = t = pick[1]
                end = at + took(name, n)
                if eng == "ACT" and table_of(name, n) not in (None, table):
                    table, end = table_of(name, n), end + TABLE_LOAD
                free[eng] = done[t] = end
                order[eng].append(t)
                for v in users[t]:
                    open_[v] -= 1
                    if open_[v] == 0:
                        ready[engine_of[v[0]]].append((max(done[b] + after(*v, b) for b in set(needs[v])), v))
            assert len(done) == len(needs)
            return order

        def table_of(name, n):
            if name == "activate":
                return "silu" if blocks[n][0].ex.layer == 0 else "gelu"
            return TABLE.get(name)

        ORDER = listed()

        def run(eng, **mine):
            for name, n in ORDER[eng]:
                mine[name](n)

        block = ctx.enter_context(nc.Block())

        @block.sync
        def _(sp):
            def load(dst, src, sem):
                sp.dma_start(dst, src).then_inc(sem, 16)

            with nc.allow_non_contiguous_dma(reason="small parameters"):
                load(X[:, tsl(0), :], x_rows[:, tsl(0), :], x_in0)
                for k, n in ((NU, "L0_attn_nu_log"), (TH, "L0_attn_theta_log")):
                    load(COL[:, k:k + 1], A[n].rearrange("(g p a) -> g p a", g=1, a=1).to_broadcast([4, NS, 1]), col_in)
                load(COL[:, AL_:AL_ + 1], column("L1_attn_a_log"), col_in)
                for n in range(2):
                    load(CT[:, n, :], A[f"L{n}_c"].rearrange("b d -> d b"), mod_in)
                    load(WMOD[n], A[f"L{n}_wmod"], mod_in)
                load(X[:, tsl(1), :], x_rows[:, tsl(1), :], x_in1)
                for g, n in enumerate(["L0_attn_B_re", "L0_attn_B_im", "L0_attn_B_im", "L0_attn_B_re"]):
                    load(TR[NS * g:NS * (g + 1), 0, :], A[n], tr_in)
                for g, (n, m) in enumerate([("L0_attn_C_re", "L0_attn_C_im"), ("L0_attn_C_im", "L0_attn_C_re")] * 2):
                    load(TR[:, 1, NS * g:NS * (g + 1)], A[n], tr_in)
                    load(TR[:, 2, NS * g:NS * (g + 1)], A[m], tr_in)
                load(TR[:, 3, :], A["L0_attn_D_mat"], tr_in)
                load(LW1[:, :], A["L0_attn_W1"], lru_in)
                load(LW2[:, :, :], A["L0_attn_W2"].rearrange("(j p) n -> p j n", p=P), lru_in)
                load(SM[:, 20:21], A["L0_attn_res_logit"].to_broadcast([P, 1]), small_in)
                for k, n in ((CO, "L1_attn_c_out"), (DS, "L1_attn_d_skip"), (FNW, "L1_attn_ff_norm_w"),
                             (INW, "L1_attn_input_norm_w"), (L1W, "L1_ffn_ln1_weight"), (L1B, "L1_ffn_ln1_bias"),
                             (L2W, "L1_ffn_ln2_weight"), (L2B, "L1_ffn_ln2_bias"), (BS2, "L0_ffn_bs2")):
                    load(COL[:, k:k + 1], column(n), small_in)
                load(WR1[:, :], A["L0_ffn_Wr1"], small_in)
                load(WR2[0:NR, :], A["L0_ffn_Wr2"], small_in)
                load(WR2[NR:NR + 1, :], A["L0_ffn_br2"].rearrange("(a n) -> a n", a=1), small_in)
                load(BR1[:, :], column("L0_ffn_br1"), small_in)
                load(B1[:, 0, :], A["L0_ffn_bs1"].rearrange("(p j) -> p j", j=NJ0), small_in)
                load(B1[:, 1:1 + NE, :], A["L0_ffn_be1"].rearrange("e (p j) -> p e j", j=NJ0), small_in)
                load(BE2[:, :], A["L0_ffn_be2"], small_in)
                load(RT[:, :], A["L1_ffn_router_weight"], small_in)
                for c in range(2, NC):
                    load(X[:, tsl(c), :], x_rows[:, tsl(c), :], x_in2)
                load(TR[:, 4:6, :], A["L1_attn_ff_fc_w"].rearrange("(j p) n -> p j n", p=P), tr2_in)
                load(TR[:, 6:8, :], A["L1_attn_ff_proj_w"].rearrange("o (j n) -> o j n", j=NF), tr2_in)
                load(TR[:, 8, :], A["L1_ffn_qkv_weight"][0:P, :], tr2_in)
                load(TR[0:QKV - P, 9, :], A["L1_ffn_qkv_weight"][P:QKV, :], tr2_in)
                load(TR[:, 10, :], A["L1_ffn_proj_weight"], tr2_in)

            def raw(ex):
                s = ex.q % 2
                if ex.q >= 2:
                    sp.wait_ge(w_split, ex.q - 1)
                if ex.e < 0:
                    w1, w2 = A["L0_ffn_Ws1"], A["L0_ffn_Ws2"]
                elif ex.layer == 0:
                    w1, w2 = A["L0_ffn_We1"][ex.e], A["L0_ffn_We2"][ex.e]
                else:
                    w1, w2 = A["L1_ffn_moe_w1"][ex.e], A["L1_ffn_moe_w2"][ex.e]
                load(WRAW[0][s][:, 0:ex.nj * P], w1, raw_in[s])
                load(WRAW[1][s][:, 0:ex.nj * P], w2.rearrange("(p j) n -> p (j n)", j=ex.nj), raw_in[s])

            def rows(n):
                g, c = n // 2, n % 4
                sp.wait_ge(b_gtc if g < 2 else e_gtc, c + 1)
                if g >= 1:
                    sp.wait_ge(m_wb, spreads(max(s.k for s in steps if s.g == g - 1)))
                for h in range(NE // 4):
                    load(GR[0:P:32, h, tk(c % 2)], GT[4 * h:4 * h + 4, tk(c)], gr_in[g])

            run("SP", raw=lambda q: raw(experts[q]), rows=rows)
            for c in range(NC):
                sp.wait_ge(f_o, c + 1)
                sp.dma_start(out_rows[:, tsl(c), :], X[:, tsl(c), :]).then_inc(out_in, 16)
            sp.wait_ge(out_in, 16 * NC)

        @block.gpsimd
        def _(pool):
            linked = [0]
            newest = [None]

            def note(ins, sem, count):
                ins.then_inc(sem, 1)
                newest[0] = (sem, count)

            def link(ins):
                linked[0] += 1
                note(ins, pch, linked[0])
                pool.wait_ge(pch, linked[0])

            nc.gpsimd.memset(MH[:, :], -0.5)
            nc.gpsimd.memset(IE[:, :], float(np.exp(-1.0)))
            nc.gpsimd.memset(ID[:, :], 0.0)
            link(nc.gpsimd.memset(ON[:, :], 1.0))
            nc.gpsimd.affine_select(out=ID[:, :], in_=ID[:, :], compare_op=ALU.not_equal, fill=1.0, base=0,
                                    pattern=[[-1, P]], channel_multiplier=1).then_inc(const, 1)

            def root(ve, rs, c):
                pool.wait_ge(ve, c + 1)
                note(nc.gpsimd.tensor_tensor(RS[:, tsl(c)], VE[:, tsl(c)], MH[:, tsl(c)], ALU.pow), rs, c + 1)

            root(a_ve, a_rs, 0)
            nc.gpsimd.affine_select(out=UT[:, :], in_=ON[:, :], compare_op=ALU.is_gt, fill=0.0, base=0,
                                    pattern=[[1, P]], channel_multiplier=-1).then_inc(const, 1)
            nc.gpsimd.iota(IO[:, :, :], [[0, NT], [1, NE]], base=0, channel_multiplier=0,
                           allow_small_or_imprecise_dtypes=True).then_inc(const, 1)
            pool.wait_ge(rates_in, 1)
            nc.gpsimd.tensor_tensor(DEC[:, :], IE[:, :], SM[:, 0:3], ALU.pow).then_inc(dec_done, 1)
            pool.wait_ge(gam_in, 1)
            nc.gpsimd.tensor_tensor(SM[:, 19:20], SM[:, 18:19], SM[:, 22:23], ALU.pow).then_inc(gam, 1)

            def a_out_sin(c):
                pool.wait_ge(a_u, c + 1)
                if c >= 2:
                    pool.wait_ge(a_z, c - 1)
                note(nc.gpsimd.tensor_tensor(WS[c % 2], TS[:, tk(c % CPB)], U[c % 2], ALU.mult), a_ws, c + 1)

            def rests_of(ex):
                s, at = ex.slot, slice(ex.at, ex.at + ex.nj)
                r1 = WRAW[0][ex.q % 2][:, 0:ex.nj * P].rearrange("p (m j) -> p j m", j=ex.nj)
                r2 = WRAW[1][ex.q % 2][:, 0:ex.nj * P].rearrange("p (j m) -> p j m", j=ex.nj)
                pool.wait_ge(w_hi, 2 * ex.q + 1)
                nc.gpsimd.tensor_tensor(W1l[s][:, at, :], r1, W1h[s][:, at, :].bitcast(F32), ALU.subtract)
                pool.wait_ge(w_hi, 2 * ex.q + 2)
                note(nc.gpsimd.tensor_tensor(W2l[s][:, at, :], r2, W2h[s][:, at, :].bitcast(F32), ALU.subtract),
                     w_split, ex.q + 1)

            def spread(st):
                if st.k >= 2:
                    pool.wait_ge(m_gated, st.k - 1)
                pool.wait_ge(gr_in[st.g], 2 * 16 * (NE // 4))
                pool.wait_ge(*newest[0])
                e = st.ex.e
                note(nc.gpsimd.partition_broadcast(WB[st.k % 2], GR[32 * (e % 4):32 * (e % 4) + 1, e // 4, tk(st.c % 2)]),
                     m_wb, spreads(st.k))
                pool.wait_ge(m_wb, spreads(st.k))

            def add_up(k):
                st = steps[k]
                pool.wait_ge(m_gated, k + 1)
                wait_sum(pool, k - 2)
                note(nc.gpsimd.tensor_tensor(ACC[:, tk(st.c)], ACC[:, tk(st.c)], MG[k % 2], ALU.add), m_acc, pool_sums(k))

            def modulate(xn_sem, mod, c, shift, scale):
                pool.wait_ge(xn_sem, c + 1)
                if c == 0:
                    pool.wait_ge(modr_done, 1)
                b = c // CPB
                link(nc.gpsimd.tensor_tensor(HT[:, tsl(c), :], XN[:, tsl(c % 2), :],
                                             MODR[:, b, scale:scale + 1, :].to_broadcast([P, TPC, D]), ALU.mult))
                note(nc.gpsimd.tensor_tensor(HT[:, tsl(c), :], HT[:, tsl(c), :],
                                             MODR[:, b, shift:shift + 1, :].to_broadcast([P, TPC, D]), ALU.add), mod, c + 1)

            def gate_input(c):
                pool.wait_ge(e_n2, c + 1)
                b = c // CPB
                link(nc.gpsimd.tensor_tensor(HT[:, tsl(c), :], HT[:, tsl(c), :],
                                             MODR[:, b, GB:GB + 1, :].to_broadcast([P, TPC, D]), ALU.mult))
                note(nc.gpsimd.tensor_tensor(X[:, tsl(c), :], X[:, tsl(c), :], HT[:, tsl(c), :], ALU.add), f_x, c + 1)

            run("POOL", w_rest=lambda q: rests_of(experts[q]), spread=lambda k: spread(steps[k]), sum_p=add_up, f_x=gate_input,
                a_rs=lambda c: root(a_ve, a_rs, c), a_ws=a_out_sin, b_rs=lambda c: root(b_ve, b_rs, c),
                d_rs=lambda c: root(d_ve, d_rs, c), d_ht=lambda c: modulate(d_xn, d_ht, c, SA, CA),
                d_rs2=lambda c: root(d_ve2, d_rs2, c), d_rs3=lambda c: root(d_ve3, d_rs3, c),
                e_rs=lambda c: root(e_ve, e_rs, c), e_mod=lambda c: modulate(e_xn, e_mod, c, SBT, CB),
                e_rs2=lambda c: root(e_ve2, e_rs2, c), e_rs3=lambda c: root(e_ve3, e_rs3, c))

        @block.scalar
        def _(act):
            act.wait_ge(mod_in, 64)
            nc.scalar.activation(SC[:, :, :], CT[:, :, :], ACT.Silu).then_inc(sc_done, 1)
            act.wait_ge(trig_in, 1)
            nc.scalar.activation(SM[:, 10:12], SM[:, 8:10], ACT.Sin).then_inc(trig, 1)

            def st_res_gate(_):
                act.wait_ge(small_in, 16 * 18)
                nc.scalar.activation(SM[:, SIG:SIG + 1], SM[:, 20:21], ACT.Tanh, scale=0.5).then_inc(trig, 1)

            def evacuate(tp, out_sem, c, dst, bank, scale, bias=0.0):
                act.wait_ge(tp, c + 1)
                nc.scalar.activation(dst, PS[:, bank, :], ACT.Identity, scale=scale, bias=bias).then_inc(out_sem, 1)

            def st_a_h(c):
                if c == 0:
                    act.wait_ge(mod_done, 1)
                b = c // CPB
                evacuate(a_tp, a_h, c, hc(c), bx(c), MF[:, 0, CA, b:b + 1], MF[:, 0, SA, b:b + 1])

            def st_a_yc(c):
                act.wait_ge(a_y, c + 1)
                nc.scalar.activation(Y[c % 2], PS[:, bx(c), :], ACT.Copy).then_inc(a_yc, 1)

            def st_a_gel(c, half):
                for j in (2 * half, 2 * half + 1):
                    act.wait_ge(a_hid1 if half else a_hid0, 2 * c + j % 2 + 1)
                    nc.scalar.activation(G0[c % 2][:, j, :], PS[:, bx(c) + j % 2, :], ACT.Gelu_apprx_tanh)\
                        .then_inc(a_gel1 if half else a_gel0, 1)

            def st_b_h(c):
                b = c // CPB
                evacuate(b_tp, b_h, c, hc(c), bx(c), MF[:, 0, CB, b:b + 1], MF[:, 0, SBT, b:b + 1])
                nc.scalar.activation(Hh[:, tk(c)], PS[:, bx(c), :], ACT.Identity, scale=MF[:, 0, CB, b:b + 1],
                                     bias=MF[:, 0, SBT, b:b + 1]).then_inc(b_hh, 1)

            def st_b_rl(c):
                act.wait_ge(b_r1, c + 1)
                nc.scalar.activation(GT[0:NR, tk(c)], PS[0:NR, by(c), :], ACT.Relu, bias=BR1[:, :]).then_inc(b_rl, 1)

            def st_exp(d, e, c):
                act.wait_ge(d, c + 1)
                nc.scalar.activation(PG[:, tsl(c), :], GA[:, tsl(c), :], ACT.Exp).then_inc(e, 1)

            def st_b_e2(c):
                act.wait_ge(b_t2, c + 1)
                nc.scalar.activation(RV[:, 4, tsl(c)], RV[:, 3, tsl(c)], ACT.Tanh, scale=0.25).then_inc(b_e2, 1)

            def st_gtc(gt, gtc, c):
                act.wait_ge(gt, c + 1)
                nc.scalar.activation(GT[0:NE, tk(c)], PS[0:NE, gt_bank(gt, c), 0:CH], ACT.Copy).then_inc(gtc, 1)

            def gt_bank(gt, c):
                return by(c) if gt is b_gt else bx(c)

            def highs_of(ex):
                s, at = ex.slot, slice(ex.at, ex.at + ex.nj)
                r1 = WRAW[0][ex.q % 2][:, 0:ex.nj * P].rearrange("p (m j) -> p j m", j=ex.nj)
                r2 = WRAW[1][ex.q % 2][:, 0:ex.nj * P].rearrange("p (j m) -> p j m", j=ex.nj)
                act.wait_ge(raw_in[ex.q % 2], 32 * (ex.q // 2 + 1))
                if ex.before >= 0:
                    act.wait_ge(m_out, experts[ex.before].last + 1)
                nc.scalar.activation(W1h[s][:, at, :], r1, ACT.Copy).then_inc(w_hi, 1)
                nc.scalar.activation(W2h[s][:, at, :], r2, ACT.Copy).then_inc(w_hi, 1)

            def activate(u):
                st, j = blocks[u]
                act.wait_ge(m_hid, u + 1)
                if u >= NJ0:
                    act.wait_ge(m_lo, u - NJ0 + 1)
                if u == 0:
                    act.wait_ge(modps, 2)
                if st.ex.layer == 0:
                    nc.scalar.activation(A32[:, u % NJ0, :], PS[:, u % 2, :], ACT.Silu,
                                         bias=B1[:, 1 + st.ex.e, j:j + 1]).then_inc(m_act, 1)
                else:
                    nc.scalar.activation(A32[:, u % NJ0, :], PS[:, u % 2, :], ACT.Gelu_apprx_tanh).then_inc(m_act, 1)

            own = [u for u in range(len(blocks)) if not by_vector(u)]

            def high(n):
                u = own[n]
                act.wait_ge(m_act, u + 1)
                if u >= RING:
                    act.wait_ge(m_out, u + 1 - RING)
                nc.scalar.activation(AH[:, u % RING, :], A32[:, u % NJ0, :], ACT.Copy).then_inc(m_hi, 1)

            def st_mod_tw(_):
                act.wait_ge(turned, 2)
                nc.scalar.activation(TW[:, T_F0:T_F0 + 4, :].rearrange("p a b -> p (a b)"), PS[:, 1, :], ACT.Copy)
                act.wait_ge(turned, 3)
                nc.scalar.activation(TW[:, T_Q0:T_Q0 + 2, :].rearrange("p a b -> p (a b)")[:, 0:QKV], PS[:, 2, 0:QKV], ACT.Copy)
                nc.scalar.activation(TW[:, T_PJ, :], PS[:, 2, QKV:QKV + P], ACT.Copy).then_inc(tw2_done, 1)

            def st_mod_cp(_):
                act.wait_ge(modps, 2)
                for b in range(B):
                    for n in range(2):
                        last = nc.scalar.activation(MODR[:, b, 3 * n:3 * n + 3, :].rearrange("p a b -> p (a b)"),
                                                    PS[:, 2 * b + n, 0:3 * D], ACT.Copy)
                last.then_inc(modr_cp, 1)

            def rms(c, dst, src, rs, done):
                act.wait_ge(rs, c + 1)
                for n, t in enumerate(tiles(c)):
                    last = nc.scalar.activation(dst(n), src(n), ACT.Copy, scale=RS[:, t:t + 1])
                last.then_inc(done, 1)

            def st_d_g(c):
                for j in range(NF):
                    act.wait_ge(d_fc, NF * c + j + 1)
                    nc.scalar.activation(G1[c % 2][:, j, :], PS[:, bx(c) + j, :], ACT.Silu).then_inc(d_g, 1)

            def st_e_l1(c):
                evacuate(e_tp, e_l1, c, hc(c), bx(c), COL[:, L1W:L1W + 1], COL[:, L1B:L1B + 1])

            def st_e_qv(c):
                for n in range(TPC // 2):
                    act.wait_ge(e_qk, (TPC // 2) * c + n + 1)
                    t = TPC * c + 2 * n
                    nc.scalar.activation(QV[:, t:t + 2, :], PS[:, by(c) - n, 0:2 * QKV].rearrange("p (t n) -> p t n", t=2),
                                         ACT.Copy).then_inc(e_qv, 1)

            def st_e_e(c):
                if c >= CPB:
                    act.wait_ge(e_dd, c - CPB + 1)
                    nc.scalar.activation(ST_[:, c % 2, :], SD[:, c % 2, :], ACT.Tanh,
                                         scale=float(0.5 / np.sqrt(np.float32(HD)))).then_inc(e_e, 1)

            def st_e_l2(c):
                evacuate(e_tp2, e_l2, c, hc(c), by(c), COL[:, L2W:L2W + 1], COL[:, L2B:L2B + 1])
                nc.scalar.activation(Hh[:, tk(c)], PS[:, by(c), :], ACT.Identity, scale=COL[:, L2W:L2W + 1],
                                     bias=COL[:, L2B:L2B + 1]).then_inc(e_hh, 1)

            run("ACT", res_gate=st_res_gate, activate=activate, high=high, w_high=lambda q: highs_of(experts[q]), a_h=st_a_h, a_yc=st_a_yc,
                a_gel0=lambda c: st_a_gel(c, 0), a_gel1=lambda c: st_a_gel(c, 1), b_h=st_b_h,
                b_rl=st_b_rl, b_e=lambda c: st_exp(b_d, b_e, c), b_e2=st_b_e2, b_gtc=lambda c: st_gtc(b_gt, b_gtc, c),
                mod_tw=st_mod_tw, mod_cp=st_mod_cp,
                d_nf=lambda c: evacuate(d_tp, d_nf, c, NFM[c % 2], by(c), COL[:, INW:INW + 1]),
                d_x1t=lambda c: evacuate(d_tp2, d_x1t, c, XN[:, tsl(c % 2), :].rearrange("p t d -> p (t d)"), bx(c), 1.0),
                d_n2=lambda c: evacuate(d_tp3, d_n2, c, N2[c % 2], by(c), COL[:, FNW:FNW + 1]),
                d_nt=lambda c: rms(c, lambda n: xn(c, n), lambda n: HT[:, TPC * c + n, :], d_rs2, d_nt),
                d_n2t=lambda c: rms(c, lambda n: xn(c, n), lambda n: xn(c, n), d_rs3, d_n2t),
                d_g=st_d_g, e_l1=st_e_l1, e_qv=st_e_qv, e_e=st_e_e,
                e_aot=lambda c: evacuate(e_at, e_aot, c, AOT[c % 2], by(c), 1.0),
                e_l2=st_e_l2, e_ee=lambda c: st_exp(e_d, e_ee, c), e_gtc=lambda c: st_gtc(e_gt, e_gtc, c))

        @block.tensor
        def _(pe):
            def mm(bank, lhsT, rhs, start=True, stop=True, rows=P, cols=slice(0, CH)):
                return nc.tensor.matmul(PS[0:rows, bank, cols], lhsT, rhs, start=start, stop=stop)

            def turn_tiles(bank, src, rows=P):
                for n in range(TPC):
                    last = nc.tensor.transpose(PS[0:rows, bank, n * P:(n + 1) * P], src(n), ID[:, :])
                return last

            pe.wait_ge(const, 1)
            pe.wait_ge(sc_done, 1)
            for n in range(2):
                for j in range(6):
                    at = (6 * n + j) * B
                    last = mm(3, WMOD[n][:, j * D:(j + 1) * D], SC[:, n, :], cols=slice(at, at + B))
            last.then_inc(modps, 1)
            pe.wait_ge(tr_in, 16 * 13)
            for n in range(4):
                last = nc.tensor.transpose(PS[:, 0, n * P:(n + 1) * P], TR[:, n, :], ID[:, :])
            last.then_inc(turned, 1)

            def st_mod_turn(_):
                pe.wait_ge(tr2_in, 16 * 5)
                for n in range(4, 8):
                    last = nc.tensor.transpose(PS[:, 1, (n - 4) * P:(n - 3) * P], TR[:, n, :], ID[:, :])
                last.then_inc(turned, 1)
                nc.tensor.transpose(PS[:, 2, 0:P], TR[:, 8, :], ID[:, :])
                nc.tensor.transpose(PS[:, 2, P:QKV], TR[0:QKV - P, 9, :], ID[0:QKV - P, 0:QKV - P])
                nc.tensor.transpose(PS[:, 2, QKV:QKV + P], TR[:, 10, :], ID[:, :]).then_inc(turned, 1)

            def st_mod_mm(_):
                pe.wait_ge(scb_done, 1)
                pe.wait_ge(mod_done, 1)
                pe.wait_ge(tw_done, 1)
                pe.wait_ge(tw2_done, 1)
                for b in range(B):
                    for n in range(2):
                        last = mm(2 * b + n, SCB[:, b, :], WMOD[1][:, n * 3 * D:(n + 1) * 3 * D], cols=slice(0, 3 * D))
                last.then_inc(modps, 1)

            def st_a_tp(c):
                pe.wait_ge(a_xn, c + 1)
                if c >= 2:
                    pe.wait_ge(b_gtc, c - 1)
                turn_tiles(bx(c), lambda n: xn(c, n)).then_inc(a_tp, 1)

            def st_a_bu(c):
                if c == 0:
                    pe.wait_ge(tw_done, 1)
                pe.wait_ge(a_h, c + 1)
                mm(by(c), TW[:, T_BW, :], hc(c)).then_inc(a_bu, 1)
                mm(bx(c), TW[:, T_D, :], hc(c), stop=False)

            def st_a_y(c):
                pe.wait_ge(a_wc, c + 1)
                mm(bx(c), TW[:, T_M1, :], WC[c % 2], start=False, stop=False)
                pe.wait_ge(a_ws, c + 1)
                mm(bx(c), TW[:, T_M2, :], WS[c % 2], start=False).then_inc(a_y, 1)

            def st_a_hid(c, half):
                if c == 0 and half == 0:
                    pe.wait_ge(lru_in, 32)
                pe.wait_ge(a_yc, c + 1)
                for j in (2 * half, 2 * half + 1):
                    if half == 1:
                        pe.wait_ge(a_gel0, 2 * c + j % 2 + 1)
                    mm(bx(c) + j % 2, LW1[:, j * P:(j + 1) * P], Y[c % 2]).then_inc(a_hid1 if half else a_hid0, 1)

            def st_a_z(c):
                pe.wait_ge(a_gel1, 2 * c + 2)
                for j in range(NJ0):
                    last = mm(bx(c), LW2[:, j, :], G0[c % 2][:, j, :], start=(j == 0), stop=(j == NJ0 - 1))
                last.then_inc(a_z, 1)

            def st_a_bk(c):
                pe.wait_ge(a_t, c + 1)
                turn_tiles(by(c), lambda n: T2[c % 2][:, n * P:(n + 1) * P]).then_inc(a_bk, 1)

            def st_b_tp(c):
                pe.wait_ge(b_xn, c + 1)
                turn_tiles(bx(c), lambda n: xn(c, n)).then_inc(b_tp, 1)

            def st_b_r1(c):
                if c == 0:
                    pe.wait_ge(small_in, 16 * 18)
                pe.wait_ge(b_h, c + 1)
                mm(by(c), WR1[:, :], hc(c), rows=NR).then_inc(b_r1, 1)

            def st_b_lg(c):
                pe.wait_ge(b_rl, c + 1)
                for n, t in enumerate(tiles(c)):
                    last = mm(bx(c), GT[0:NR + 1, t * P:(t + 1) * P], WR2[:, :], cols=slice(n * NE, (n + 1) * NE))
                last.then_inc(b_lg, 1)

            def st_gt(g, gt, bank, c):
                pe.wait_ge(g, c + 1)
                turn_tiles(bank, lambda n: GA[:, TPC * c + n, :], rows=NE).then_inc(gt, 1)

            def hidden(u):
                st, j = blocks[u]
                ex, c = st.ex, st.c
                w = slice(ex.at, ex.at + ex.nj)
                if u == ex.start:
                    pe.wait_ge(w_split, ex.q + 1)
                if st.first_of_sum and j == 0:
                    pe.wait_ge(b_hl if ex.layer == 0 else e_hl, c + 1)
                if u == 0:
                    pe.wait_ge(modr_cp, 1)
                if u >= 2:
                    pe.wait_ge(m_act, u - 1)
                mm(u % 2, W1h[ex.slot][:, w, :][:, j, :], Hh[:, tk(c)], stop=False)
                mm(u % 2, W1h[ex.slot][:, w, :][:, j, :], Hl[:, tk(c)], start=False, stop=False)
                mm(u % 2, W1l[ex.slot][:, w, :][:, j, :], Hh[:, tk(c)], start=False).then_inc(m_hid, 1)

            def output(u):
                st, j = blocks[u]
                ex, bank = st.ex, 2 + st.k % 2
                a = ex.at + j
                if j == 0 and st.k >= 2:
                    pe.wait_ge(m_gated, st.k - 1)
                pe.wait_ge(m_lo, u + 1)
                mm(bank, W2h[ex.slot][:, a, :], AH[:, u % RING, :], start=(j == 0), stop=False)
                mm(bank, W2l[ex.slot][:, a, :], AH[:, u % RING, :], start=False, stop=False)
                mm(bank, W2h[ex.slot][:, a, :], AL[:, u % RING, :], start=False, stop=(j == ex.nj - 1)).then_inc(m_out, 1)

            def st_c_be(c):
                pe.wait_ge(b_gtc, NC)
                if c >= 2:
                    pe.wait_ge(e_gtc, c - 1)
                mm(bx(c), BE2[:, :], GT[0:NE, tk(c)]).then_inc(c_be, 1)

            def st_c_bk(c):
                pe.wait_ge(c_t, c + 1)
                turn_tiles(by(c), lambda n: TE[c % 2][:, n * P:(n + 1) * P]).then_inc(c_bk, 1)

            def st_d_tp(c):
                pe.wait_ge(d_nt, c + 1)
                turn_tiles(bx(c), lambda n: HT[:, TPC * c + n, :])
                turn_tiles(by(c), lambda n: xn(c, n)).then_inc(d_tp, 1)

            def st_d_tp2(c):
                pe.wait_ge(d_x1, c + 1)
                turn_tiles(bx(c), lambda n: X1[c % 2][:, n * P:(n + 1) * P]).then_inc(d_tp2, 1)

            def st_d_tp3(c):
                pe.wait_ge(d_n2t, c + 1)
                turn_tiles(by(c), lambda n: xn(c, n)).then_inc(d_tp3, 1)

            def st_d_fc(c):
                pe.wait_ge(d_n2, c + 1)
                for j in range(NF):
                    mm(bx(c) + j, TW[:, T_F0 + j, :], N2[c % 2]).then_inc(d_fc, 1)

            def st_d_pj(c):
                for j in range(NF):
                    pe.wait_ge(d_g, NF * c + j + 1)
                    last = mm(bx(c), TW[:, T_P0 + j, :], G1[c % 2][:, j, :], start=(j == 0), stop=(j == NF - 1))
                last.then_inc(d_pj, 1)

            def st_d_bk(c):
                pe.wait_ge(d_u, c + 1)
                turn_tiles(by(c), lambda n: U2[c % 2][:, n * P:(n + 1) * P]).then_inc(d_bk, 1)

            def st_e_tp(c):
                pe.wait_ge(e_n1, c + 1)
                turn_tiles(bx(c), lambda n: xn(c, n)).then_inc(e_tp, 1)

            def st_e_qk(c):
                pe.wait_ge(e_l1, c + 1)
                for n in range(TPC // 2):
                    for m in range(2):
                        i = 2 * n + m
                        last = mm(by(c) - n, hc(c)[:, i * P:(i + 1) * P], TW[:, T_Q0:T_Q0 + 2, :].rearrange("p a b -> p (a b)")[:, 0:QKV],
                                  cols=slice(m * QKV, (m + 1) * QKV))
                    last.then_inc(e_qk, 1)

            def st_e_at(c):
                pe.wait_ge(e_ao, c + 1)
                turn_tiles(by(c), lambda n: AO[c % 2][:, n * P:(n + 1) * P]).then_inc(e_at, 1)

            def st_e_pj(c):
                pe.wait_ge(e_aot, c + 1)
                for n in range(TPC):
                    last = mm(bx(c), AOT[c % 2][:, n * P:(n + 1) * P], TW[:, T_PJ, :], cols=slice(n * P, (n + 1) * P))
                last.then_inc(e_pj, 1)

            def st_e_tp2(c):
                pe.wait_ge(e_n2, c + 1)
                turn_tiles(by(c), lambda n: xn(c, n)).then_inc(e_tp2, 1)

            def st_e_lg(c):
                pe.wait_ge(e_hh, c + 1)
                for n in range(TPC):
                    last = mm(bx(c), hc(c)[:, n * P:(n + 1) * P], RT[:, :], cols=slice(n * NE, (n + 1) * NE))
                last.then_inc(e_lg, 1)

            def st_e_cn(c):
                if c == 0:
                    pe.wait_ge(const, 3)
                pe.wait_ge(e_cs, c + 1)
                flat = "p t e -> p (t e)"
                mm(by(c), UT[:, :], CSO[:, tsl(c), :].rearrange(flat), stop=False, cols=slice(0, NE * TPC))
                mm(by(c), ON[:, :], CS[:, tsl(c), :].rearrange(flat), start=False, cols=slice(0, NE * TPC)).then_inc(e_cn, 1)

            def st_f_bk(c):
                pe.wait_ge(e_gtc, NC)
                wait_sum(pe, last_step[1][c])
                if c >= 2:
                    pe.wait_ge(f_o, c - 1)
                turn_tiles(by(c), lambda n: ACC[:, c * CH + n * P:c * CH + (n + 1) * P]).then_inc(f_bk, 1)

            run("PE", hidden=hidden, output=output, mod_turn=st_mod_turn, mod_mm=st_mod_mm, a_tp=st_a_tp,
                a_bu=st_a_bu, a_y=st_a_y, a_hid0=lambda c: st_a_hid(c, 0),
                a_hid1=lambda c: st_a_hid(c, 1), a_z=st_a_z, a_bk=st_a_bk, b_tp=st_b_tp, b_r1=st_b_r1, b_lg=st_b_lg,
                b_gt=lambda c: st_gt(b_g, b_gt, by(c), c), c_be=st_c_be, c_bk=st_c_bk, d_tp=st_d_tp, d_tp2=st_d_tp2, d_tp3=st_d_tp3,
                d_fc=st_d_fc, d_pj=st_d_pj, d_bk=st_d_bk, e_tp=st_e_tp, e_qk=st_e_qk, e_at=st_e_at, e_pj=st_e_pj, e_tp2=st_e_tp2,
                e_lg=st_e_lg, e_cn=st_e_cn, e_gt=lambda c: st_gt(e_g, e_gt, bx(c), c), f_bk=st_f_bk)

        @block.vector
        def _(dve):
            linked = [0]

            def link(ins):
                linked[0] += 1
                ins.then_inc(dch, 1)
                dve.wait_ge(dch, linked[0])

            V = nc.vector
            LN2H, LN2L = two_part(np.log(2.0))
            PI2A, rest = two_part(2.0 * np.pi)
            PI2B, PI2C = two_part(rest)
            ROUND = 1.5 * 2.0 ** 23

            def exp3(dst, src, scale):
                link(V.tensor_scalar(EX[:, :], src, scale, 88.0, ALU.mult, ALU.min))
                link(V.tensor_scalar(EX[:, :], EX[:, :], -87.0, None, ALU.max))
                link(V.tensor_scalar(EK[:, :], EX[:, :], float(np.log2(np.e)), ROUND, ALU.mult, ALU.add))
                link(V.tensor_scalar(EK[:, :], EK[:, :], ROUND, None, ALU.subtract))
                link(V.scalar_tensor_tensor(EF[:, :], EK[:, :], -LN2H, EX[:, :], ALU.mult, ALU.add))
                link(V.scalar_tensor_tensor(EF[:, :], EK[:, :], -LN2L, EF[:, :], ALU.mult, ALU.add))
                link(V.tensor_scalar(EI[:, :], EK[:, :], 127.0, 2.0 ** 23, ALU.add, ALU.mult))
                link(V.tensor_scalar(EQ[:, :], EF[:, :], 1 / 5040.0, None, ALU.mult))
                for f in (720, 120, 24, 6, 2, 1):
                    link(V.scalar_tensor_tensor(EQ[:, :], EQ[:, :], 1.0 / f, EF[:, :], ALU.add, ALU.mult))
                return V.scalar_tensor_tensor(dst, EQ[:, :], 1.0, EI[:, :].bitcast(F32), ALU.add, ALU.mult)

            def stats(c, tile, ve, eps, rms=False):
                t = tiles(c)
                for n in range(TPC):
                    last = V.bn_stats(ST[:, t[n], :], tile(n))
                link(last)
                for n in range(TPC):
                    last = V.bn_aggr(MV[:, t[n], :], ST[:, t[n], :])
                link(last)
                v = VE[:, tsl(c)]
                mean, var = MV[:, tsl(c), 0], MV[:, tsl(c), 1]
                if rms:
                    link(V.tensor_tensor(v, mean, mean, ALU.mult))
                    V.scalar_tensor_tensor(v, v, eps, var, ALU.add, ALU.add).then_inc(ve, 1)
                else:
                    V.tensor_scalar(v, var, eps, None, ALU.add).then_inc(ve, 1)

            def normalise(c, dst, src, rs, done, rms=False):
                dve.wait_ge(rs, c + 1)
                for n, t in enumerate(tiles(c)):
                    if rms:
                        last = V.tensor_scalar(dst(n), src(n), RS[:, t:t + 1], None, ALU.mult)
                    else:
                        last = V.tensor_scalar(dst(n), src(n), MV[:, t, 0:1], RS[:, t:t + 1], ALU.subtract, ALU.mult)
                last.then_inc(done, 1)

            def rows(buf, c):
                return lambda n: buf[:, TPC * c + n, :]

            def xns(c):
                return lambda n: xn(c, n)

            def add_x(c, bk, done):
                dve.wait_ge(bk, c + 1)
                x = X[:, tsl(c), :].rearrange("p t d -> p (t d)")
                V.tensor_tensor(x, x, PS[:, by(c), :], ALU.add).then_inc(done, 1)

            def st_a_ve(c):
                dve.wait_ge((x_in0, x_in1, x_in2, x_in2)[c], 16 if c < 2 else 32)
                stats(c, rows(X, c), a_ve, 1e-5)

            def st_a_xn(c):
                if c >= 2:
                    dve.wait_ge(b_tp, c - 1)
                normalise(c, xns(c), rows(X, c), a_rs, a_xn)

            st_a_ve(0)

            V.memset(SG[:, 0:2], 1.0)
            link(V.memset(SM[:, 22:23], 0.5))
            V.memset(SG[96:128, 0:1], -1.0)
            V.memset(SG[32:64, 1:2], -1.0)
            link(V.memset(SG[96:128, 1:2], -1.0))

            dve.wait_ge(col_in, 16 * 3)
            exp3(SM[:, 0:3], COL[:, 0:3], 1.0).then_inc(rates_in, 1)
            dve.wait_ge(rates_in, 1)
            link(V.tensor_scalar(SM[:, 12:13], SM[:, 1:2], 1.0 / (2 * np.pi), ROUND, ALU.mult, ALU.add))
            link(V.tensor_scalar(SM[:, 12:13], SM[:, 12:13], ROUND, None, ALU.subtract))
            link(V.scalar_tensor_tensor(SM[:, 8:9], SM[:, 12:13], -PI2A, SM[:, 1:2], ALU.mult, ALU.add))
            link(V.scalar_tensor_tensor(SM[:, 8:9], SM[:, 12:13], -PI2B, SM[:, 8:9], ALU.mult, ALU.add))
            link(V.scalar_tensor_tensor(SM[:, 8:9], SM[:, 12:13], -PI2C, SM[:, 8:9], ALU.mult, ALU.add))
            link(V.tensor_scalar(SM[:, 8:9], SM[:, 8:9], 3.1415925, -3.1415925, ALU.min, ALU.max))
            link(V.scalar_tensor_tensor(SM[:, 9:10], SM[:, 8:9], -1.0, SM[:, 8:9], ALU.mult, ALU.min))
            V.tensor_scalar(SM[:, 9:10], SM[:, 9:10], np.pi / 2, None, ALU.add).then_inc(trig_in, 1)
            st_a_xn(0)
            dve.wait_ge(dec_done, 1)
            link(V.tensor_tensor(SM[:, 18:19], DEC[:, 0:1], DEC[:, 0:1], ALU.mult))
            link(V.tensor_scalar(SM[:, 18:19], SM[:, 18:19], -1.0, 1.0, ALU.mult, ALU.add))
            V.tensor_scalar(SM[:, 18:19], SM[:, 18:19], 0.0, None, ALU.max).then_inc(gam_in, 1)

            def clamp_gates(g, tmp):
                link(V.tensor_scalar(tmp, g, 0.0, 2.0, ALU.is_ge, ALU.mult))
                link(V.scalar_tensor_tensor(g, g, -1.0, g, ALU.mult, ALU.max))
                link(V.tensor_scalar(g, g, 0.25, None, ALU.max))
                return V.scalar_tensor_tensor(g, tmp, 1.0, g, ALU.subtract, ALU.mult)

            def modulation_and_turned():
                dve.wait_ge(modps, 1)
                link(V.tensor_copy(MF[:, :, :, :].rearrange("p n j b -> p (n j b)"), PS[:, 3, 0:2 * 6 * B]))
                for j in (CA, CB):
                    link(V.tensor_scalar(MF[:, :, j, :], MF[:, :, j, :], 1.0, None, ALU.add))
                link(clamp_gates(MF[:, :, GAT, :], GTMP[:, 0, :, :]))
                clamp_gates(MF[:, :, GB, :], GTMP[:, 1, :, :]).then_inc(mod_done, 1)

                dve.wait_ge(turned, 1)
                V.tensor_copy(TW[:, T_BW, :], PS[:, 0, 0:P])
                V.tensor_scalar(TW[:, T_M1, :], PS[:, 0, P:2 * P], SG[:, 1:2], None, ALU.mult)
                V.tensor_scalar(TW[:, T_M2, :], PS[:, 0, 2 * P:3 * P], -1.0, None, ALU.mult)
                V.tensor_copy(TW[:, T_D, :], PS[:, 0, 3 * P:4 * P]).then_inc(tw_done, 1)

            dve.wait_ge(trig, 1)
            V.memset(TC[:, 0:1], 1.0)
            V.memset(TS[:, 0:1], 0.0)
            V.tensor_copy(TC[:, 1:2], SM[:, 11:12])
            link(V.tensor_copy(TS[:, 1:2], SM[:, 10:11]))

            def double(k):
                n = min(k, L - 1 - k)
                o, i = slice(k + 1, k + n + 1), slice(1, n + 1)
                c1, s1 = TC[:, k:k + 1], TS[:, k:k + 1]
                V.tensor_scalar(T2[1][:, 0:n], TS[:, i], s1, None, ALU.mult)
                link(V.tensor_scalar(Q[:, 0:n], TC[:, i], s1, None, ALU.mult))
                V.scalar_tensor_tensor(TC[:, o], TC[:, i], c1, T2[1][:, 0:n], ALU.mult, ALU.subtract)
                link(V.scalar_tensor_tensor(TS[:, o], TS[:, i], c1, Q[:, 0:n], ALU.mult, ALU.add))

            def input_table(half):
                V.tensor_scalar(TIN[0:64, half], TC[0:64, half], SG[0:64, 2:3], None, ALU.mult)
                link(V.tensor_scalar(TIN[64:128, half], TS[64:128, half], SG[64:128, 2:3], None, ALU.mult))

            k = 1
            while k < CH:
                if k == CH // 8:
                    modulation_and_turned()
                double(k)
                k *= 2
            dve.wait_ge(gam, 1)
            link(V.tensor_tensor(SG[:, 2:3], SG[:, 0:1], SM[:, 19:20], ALU.mult))
            input_table(tk(0))

            def upper_tables(_):
                double(CH)
                input_table(tk(1))

            def small_things(_):
                dve.wait_ge(trig, 2)
                link(V.tensor_scalar(SM[:, SIG:SIG + 1], SM[:, SIG:SIG + 1], 0.5, 0.5, ALU.mult, ALU.add))
                V.memset(GT[32:33, :], 1.0)
                dve.wait_ge(sc_done, 1)
                for b in range(B):
                    last = V.tensor_copy(SCB[:, b, :], SC[:, 1, b:b + 1].to_broadcast([P, P]))
                last.then_inc(scb_done, 1)

            def st_mod_rows(_):
                dve.wait_ge(modr_cp, 1)
                for j in (CA, CB):
                    link(V.tensor_scalar(MODR[:, :, j, :], MODR[:, :, j, :], 1.0, None, ALU.add))
                clamp_gates(MODR[:, :, GB, :], CTMP[:, :, :]).then_inc(modr_done, 1)

            def st_a_u(c):
                dve.wait_ge(a_bu, c + 1)
                half = tk(c % CPB)
                link(V.tensor_tensor(Q, PS[:, by(c), :], TIN[:, half], ALU.mult))
                if c >= 2:
                    dve.wait_ge(a_z, c - 1)
                start = 0.0 if c % CPB == 0 else U[(c - 1) % 2][:, CH - 1:CH]
                V.tensor_tensor_scan(U[c % 2], DEC[:, 0:1].to_broadcast([P, CH]), Q, start, ALU.mult, ALU.add).then_inc(a_u, 1)
                dve.wait_ge(a_u, c + 1)
                V.tensor_tensor(WC[c % 2], TC[:, half], U[c % 2], ALU.mult).then_inc(a_wc, 1)

            def st_a_t(c):
                dve.wait_ge(a_z, c + 1)
                link(V.scalar_tensor_tensor(T2[c % 2], PS[:, bx(c), :], SM[:, SIG:SIG + 1], hc(c), ALU.mult, ALU.add))
                V.tensor_scalar(T2[c % 2], T2[c % 2], MF[:, 0, GAT, c // CPB:c // CPB + 1], None, ALU.mult).then_inc(a_t, 1)

            def st_b_ve(c):
                dve.wait_ge(a_x, c + 1)
                stats(c, rows(X, c), b_ve, 1e-5)

            def st_hl(hh, hl, c):
                dve.wait_ge(hh, c + 1)
                V.tensor_tensor(Hl[:, tk(c)], hc(c), Hh[:, tk(c)].bitcast(F32), ALU.subtract).then_inc(hl, 1)

            def each(col):
                return col.rearrange("p (t a) -> p t a", a=1).to_broadcast([P, TPC, NE])

            def st_logits(lg, d, c):
                dve.wait_ge(lg, c + 1)
                logits = PS[:, bx(c), 0:TPC * NE].rearrange("p (t e) -> p t e", e=NE)
                link(V.tensor_reduce(RV[:, 0, tsl(c)], logits, AX.X, ALU.max))
                V.tensor_tensor(GA[:, tsl(c), :], logits, each(RV[:, 0, tsl(c)]), ALU.subtract).then_inc(d, 1)

            def top_two(e, c):
                dve.wait_ge(e, c + 1)
                t4 = tsl(c)
                link(V.tensor_reduce(RV[:, 1, t4], PG[:, t4, :], AX.X, ALU.add))
                link(V.reciprocal(RV[:, 2, t4], RV[:, 1, t4]))
                link(V.tensor_tensor(PG[:, t4, :], PG[:, t4, :], each(RV[:, 2, t4]), ALU.mult))
                for t in tiles(c):
                    last = V.max(M8[:, t, :], PG[:, t, :])
                link(last)
                for t in tiles(c):
                    last = V.max_index(I8[:, t, :], M8[:, t, :], PG[:, t, :])
                link(last)
                link(V.tensor_copy(IF[:, t4, :], I8[:, t4, 0:2]))
                if c == 0:
                    dve.wait_ge(const, 3)
                V.tensor_tensor(EQ1[:, t4, :], IO[:, t4, :], IF[:, t4, 0:1].to_broadcast([P, TPC, NE]), ALU.is_equal)
                return V.tensor_tensor(EQ2[:, t4, :], IO[:, t4, :], IF[:, t4, 1:2].to_broadcast([P, TPC, NE]), ALU.is_equal)

            def weigh(w1, w2, c):
                t4 = tsl(c)
                V.tensor_tensor(EQ1[:, t4, :], EQ1[:, t4, :], each(w1), ALU.mult)
                link(V.tensor_tensor(EQ2[:, t4, :], EQ2[:, t4, :], each(w2), ALU.mult))
                return V.tensor_tensor(GA[:, t4, :], EQ1[:, t4, :], EQ2[:, t4, :], ALU.add)

            def st_b_t2(c):
                link(top_two(b_e, c))
                V.tensor_tensor(RV[:, 3, tsl(c)], M8[:, tsl(c), 1], M8[:, tsl(c), 0], ALU.subtract).then_inc(b_t2, 1)

            def st_b_g(c):
                dve.wait_ge(b_e2, c + 1)
                V.tensor_scalar(RV[:, 0, tsl(c)], RV[:, 4, tsl(c)], -0.5, 0.5, ALU.mult, ALU.add)
                link(V.tensor_scalar(RV[:, 1, tsl(c)], RV[:, 4, tsl(c)], 0.5, 0.5, ALU.mult, ALU.add))
                weigh(RV[:, 0, tsl(c)], RV[:, 1, tsl(c)], c).then_inc(b_g, 1)

            def rest(u):
                r = u % RING
                if by_vector(u):
                    dve.wait_ge(m_act, u + 1)
                    if u >= RING:
                        dve.wait_ge(m_out, u + 1 - RING)
                    V.tensor_copy(AH[:, r, :], A32[:, u % NJ0, :]).then_inc(m_hiv, 1)
                    dve.wait_ge(m_hiv, u + 1 - highs(u))
                else:
                    dve.wait_ge(m_hi, highs(u))
                V.tensor_tensor(AL[:, r, :], A32[:, u % NJ0, :], AH[:, r, :].bitcast(F32), ALU.subtract).then_inc(m_lo, 1)

            def add_up(k):
                st = steps[k]
                dve.wait_ge(m_gated, k + 1)
                wait_sum(dve, k - 2)
                V.tensor_tensor(ACC[:, tk(st.c)], ACC[:, tk(st.c)], MG[k % 2], ALU.add).then_inc(m_accv, 1)

            def gate(k):
                st = steps[k]
                dve.wait_ge(m_out, st.last + 1)
                out_ps = PS[:, 2 + k % 2, :]
                if st.ex.e < 0:
                    V.tensor_copy(ACC[:, tk(st.c)], out_ps).then_inc(m_gated, 1)
                    return
                dve.wait_ge(m_wb, spreads(k))
                if st.first_of_sum:
                    dst = ACC[:, tk(st.c)]
                else:
                    dst = MG[k % 2]
                    if mg_before(k) is not None:
                        wait_sum(dve, mg_before(k))
                if st.ex.layer == 0:
                    V.tensor_tensor(dst, out_ps, WB[k % 2], ALU.mult).then_inc(m_gated, 1)
                else:
                    V.scalar_tensor_tensor(dst, out_ps, MF[:, 1, GB, st.c // CPB:st.c // CPB + 1], WB[k % 2],
                                           ALU.mult, ALU.mult).then_inc(m_gated, 1)

            def st_c_t(c):
                dve.wait_ge(c_be, c + 1)
                wait_sum(dve, last_step[0][c])
                link(V.scalar_tensor_tensor(TE[c % 2], PS[:, bx(c), :], COL[:, BS2:BS2 + 1], ACC[:, tk(c)], ALU.add, ALU.add))
                V.tensor_scalar(TE[c % 2], TE[c % 2], MF[:, 0, GB, c // CPB:c // CPB + 1], None, ALU.mult).then_inc(c_t, 1)

            def st_d_ve(c):
                dve.wait_ge(c_x, c + 1)
                stats(c, rows(X, c), d_ve, 1e-5)

            def st_d_ve2(c):
                dve.wait_ge(d_ht, c + 1)
                stats(c, rows(HT, c), d_ve2, 1e-6, rms=True)

            def st_d_x1(c):
                dve.wait_ge(d_nf, c + 1)
                start = 0.0 if c % CPB == 0 else HS[(c - 1) % 2][:, CH - 1:CH]
                p = c % 2
                V.tensor_tensor_scan(HS[p], DEC[:, 2:3].to_broadcast([P, CH]), NFM[p], start, ALU.mult, ALU.add).then_inc(d_hs, 1)
                if c >= 1:
                    dve.wait_ge(d_x1, c)
                link(V.scalar_tensor_tensor(SK, NFM[p], COL[:, DS:DS + 1], PS[:, bx(c), :], ALU.mult, ALU.add))
                dve.wait_ge(d_hs, c + 1)
                V.scalar_tensor_tensor(X1[p], HS[p], COL[:, CO:CO + 1], SK, ALU.mult, ALU.add).then_inc(d_x1, 1)

            def st_d_ve3(c):
                dve.wait_ge(d_x1t, c + 1)
                stats(c, xns(c), d_ve3, 1e-6, rms=True)

            def st_d_u(c):
                dve.wait_ge(d_pj, c + 1)
                link(V.tensor_tensor(U2[c % 2], PS[:, bx(c), :], X1[c % 2], ALU.add))
                V.tensor_scalar(U2[c % 2], U2[c % 2], MF[:, 1, GAT, c // CPB:c // CPB + 1], None, ALU.mult).then_inc(d_u, 1)

            def st_e_ve(c):
                dve.wait_ge(d_x, c + 1)
                stats(c, rows(X, c), e_ve, 1e-5)

            def st_e_ve2(c):
                dve.wait_ge(e_mod, c + 1)
                stats(c, rows(HT, c), e_ve2, 1e-5)

            def qkv_of(t):
                g = QV[:, t, :].rearrange("p (g w) -> p g w", w=GW)
                q = g[:, :, 0:QPK * HD].rearrange("p g (q d) -> p g q d", d=HD)
                k = g[:, :, QPK * HD:(QPK + 1) * HD].rearrange("p g (a d) -> p g a d", a=1).to_broadcast([P, NKV, QPK, HD])
                v = g[:, :, (QPK + 1) * HD:].rearrange("p g (a d) -> p g a d", a=1).to_broadcast([P, NKV, QPK, HD])
                return q, k, v

            def heads(buf, n):
                return buf[:, n * D:(n + 1) * D].rearrange("p (g q d) -> p g q d", g=NKV, q=QPK)

            def of_group(x):
                return x.rearrange("p g (a d) -> p g a d", a=1).to_broadcast([P, NKV, QPK, HD])

            def st_e_dd(c):
                if c < CPB:
                    return
                dve.wait_ge(e_qv, (TPC // 2) * (c + 1))
                kv0, kv1 = (QV[:, tsl(n), :].rearrange("p t (g w) -> p (t g) w", w=GW)[:, :, QPK * HD:] for n in (c - CPB, c))
                link(V.tensor_tensor(DKV[:, c % 2, :, :], kv0, kv1, ALU.subtract))
                for n, t in enumerate(tiles(c)):
                    last = V.tensor_tensor(heads(PR, n), qkv_of(t)[0], of_group(DKV[:, c % 2, NKV * n:NKV * (n + 1), 0:HD]), ALU.mult)
                link(last)
                V.tensor_reduce(SD[:, c % 2, :], PR[:, 0:CH].rearrange("p (m d) -> p m d", d=HD), AX.X, ALU.add).then_inc(e_dd, 1)

            def st_e_ao(c):
                ao = AO[c % 2]
                if c < CPB:
                    dve.wait_ge(e_qv, (TPC // 2) * (c + 1))
                    for n, t in enumerate(tiles(c)):
                        last = V.tensor_copy(heads(ao, n), qkv_of(t)[2])
                    last.then_inc(e_ao, 1)
                    return
                dve.wait_ge(e_e, c - CPB + 1)
                if c > CPB:
                    dve.wait_ge(e_ao, c)
                link(V.tensor_scalar(SP0[:, c % 2, :], ST_[:, c % 2, :], 0.5, 0.5, ALU.mult, ALU.add))
                for n, t in enumerate(tiles(c)):
                    prob = SP0[:, c % 2, n * NH:(n + 1) * NH].rearrange("p (g q a) -> p g q a", g=NKV, a=1).to_broadcast([P, NKV, QPK, HD])
                    last = V.tensor_tensor(heads(PR, n), of_group(DKV[:, c % 2, NKV * n:NKV * (n + 1), HD:2 * HD]), prob, ALU.mult)
                link(last)
                for n, t in enumerate(tiles(c)):
                    last = V.tensor_tensor(heads(ao, n), heads(PR, n), qkv_of(t)[2], ALU.add)
                last.then_inc(e_ao, 1)

            def st_e_h1(c):
                dve.wait_ge(e_pj, c + 1)
                h = HT[:, tsl(c), :].rearrange("p t d -> p (t d)")
                V.tensor_tensor(h, h, PS[:, bx(c), :], ALU.add).then_inc(e_h1, 1)
                dve.wait_ge(e_h1, c + 1)
                stats(c, rows(HT, c), e_ve3, 1e-5)

            def st_e_cs(c):
                link(top_two(e_ee, c))
                link(V.tensor_tensor(CSO[:, tsl(c), :], EQ1[:, tsl(c), :], EQ2[:, tsl(c), :], ALU.add))
                for t in tiles(c):
                    if t == 0:
                        last = V.memset(CS[:, 0, :], 0.0)
                    else:
                        last = V.tensor_tensor(CS[:, t, :], CS[:, t - 1, :], CSO[:, t - 1, :], ALU.add)
                    if t != tiles(c)[-1]:
                        link(last)
                last.then_inc(e_cs, 1)
                link(V.tensor_tensor(RV[:, 0, tsl(c)], M8[:, tsl(c), 0], M8[:, tsl(c), 1], ALU.add))
                link(V.reciprocal(RV[:, 1, tsl(c)], RV[:, 0, tsl(c)]))
                V.tensor_tensor(RV[:, 2, tsl(c)], M8[:, tsl(c), 0], RV[:, 1, tsl(c)], ALU.mult)
                link(V.tensor_tensor(RV[:, 3, tsl(c)], M8[:, tsl(c), 1], RV[:, 1, tsl(c)], ALU.mult))
                link(weigh(RV[:, 2, tsl(c)], RV[:, 3, tsl(c)], c))

            def st_e_g(c):
                dve.wait_ge(e_cn, c + 1)
                before = PS[:, by(c), 0:NE * TPC].rearrange("p (t e) -> p t e", e=NE)
                link(V.tensor_scalar(KEEP[:, tsl(c), :], before, CAP, None, ALU.is_lt))
                V.tensor_tensor(GA[:, tsl(c), :], GA[:, tsl(c), :], KEEP[:, tsl(c), :], ALU.mult).then_inc(e_g, 1)

            def st_f_o(c):
                dve.wait_ge(f_bk, c + 1)
                dve.wait_ge(f_x, c + 1)
                x = X[:, tsl(c), :].rearrange("p t d -> p (t d)")
                V.tensor_tensor(x, x, PS[:, by(c), :], ALU.add).then_inc(f_o, 1)

            run("DVE", rest=rest, gate=gate, sum_v=add_up, upper=upper_tables, small=small_things, mod_rows=st_mod_rows, a_ve=st_a_ve,
                a_xn=st_a_xn, a_u=st_a_u, a_t=st_a_t,
                a_x=lambda c: add_x(c, a_bk, a_x), b_ve=st_b_ve, b_xn=lambda c: normalise(c, xns(c), rows(X, c), b_rs, b_xn),
                b_hl=lambda c: st_hl(b_hh, b_hl, c), b_d=lambda c: st_logits(b_lg, b_d, c), b_t2=st_b_t2, b_g=st_b_g,
                c_t=st_c_t, c_x=lambda c: add_x(c, c_bk, c_x), d_ve=st_d_ve,
                d_xn=lambda c: normalise(c, xns(c), rows(X, c), d_rs, d_xn), d_ve2=st_d_ve2,
                d_x1=st_d_x1, d_ve3=st_d_ve3,
                d_u=st_d_u,
                d_x=lambda c: add_x(c, d_bk, d_x), e_ve=st_e_ve, e_xn=lambda c: normalise(c, xns(c), rows(X, c), e_rs, e_xn),
                e_ve2=st_e_ve2, e_n1=lambda c: normalise(c, xns(c), rows(HT, c), e_rs2, e_n1), e_dd=st_e_dd, e_ao=st_e_ao,
                e_h1=st_e_h1, e_n2=lambda c: normalise(c, xns(c), rows(HT, c), e_rs3, e_n2), e_hl=lambda c: st_hl(e_hh, e_hl, c),
                e_d=lambda c: st_logits(e_lg, e_d, c), e_cs=st_e_cs, e_g=st_e_g, f_o=st_f_o)


_OUTS = [((2, 1024, 128), "float32")]


def kernel(**inputs):
    import numpy as _np
    import concourse.bacc as _bacc
    from concourse import mybir as _mybir
    from concourse.bass_utils import run_bass_kernel_spmd as _run

    nc = _bacc.Bacc("TRN2", target_bir_lowering=False, num_devices=1)
    arrays, aps = {}, {}
    for name in inputs:
        a = _np.ascontiguousarray(inputs[name])
        if name == "L0_attn_res_logit":
            a = a.reshape(1, 1)
        arrays[f"in_{name}_dram"] = a
        aps[name] = nc.dram_tensor(f"in_{name}_dram", a.shape, _mybir.dt.from_np(a.dtype), kind="ExternalInput").ap()
    shape, dtype = _OUTS[0]
    out = nc.dram_tensor("out_0_dram", shape, _mybir.dt.from_np(_np.dtype(dtype)), kind="ExternalOutput").ap()
    adaln_two_layers(nc, aps, out)
    r = _run(nc, [arrays], core_ids=[0])
    return r.results[0]["out_0_dram"]
```
